# Optimizing a Trainium2 kernel written in Bass

```python
import numpy as np
import jax
import jax.numpy as jnp

def _softmax(x, axis=-1):
    return jax.nn.softmax(x, axis=axis)

def _gelu(x):
    return jax.nn.gelu(x, approximate=True)

def _silu(x):
    return jax.nn.silu(x)

def _sigmoid(x):
    return jax.nn.sigmoid(x)

def _layernorm(x, axis=-1, eps=1e-05):
    m = jnp.mean(x, axis=axis, keepdims=True)
    v = jnp.var(x, axis=axis, keepdims=True)
    return (x - m) / jnp.sqrt(v + eps)

def _scatter_add(tgt, idx, src, axis=0):
    return tgt.at[idx].add(src)

def _segment_sum(src, seg, n):
    return jax.ops.segment_sum(src, seg, n)
kernel_name = 'mk_early_fusion_d1_tok_img4096_r4_9c5c8c'

def setup_inputs(seed: int=0):
    np.random.seed(seed)
    _w = jnp.asarray

    def _rec_inputs():
        import jax
        import jax.numpy as jnp
        _rk = jax.random.key(seed)
        x = -0.00348982 + 0.707501 * jax.random.normal(jax.random.fold_in(_rk, 1), (16, 128, 64, 2), jnp.float32)
        txt = 6.73332e-06 + 0.02 * jax.random.normal(jax.random.fold_in(_rk, 2), (16, 77, 1024), jnp.float32)
        return (x, txt)
    x, txt = _rec_inputs()

    def _L0_tok_setup():
        import jax, jax.numpy as jnp
        import numpy as np
        H, N, S, CH, LEN = (128, 64, 128, 1, 1024)

        def _s4d_kernel(log_dt, C, B, inv_A_real, A_imag, L):
            dt = jnp.exp(log_dt)
            Cc = C[..., 0] + 1j * C[..., 1]
            Bc = B[..., 0] + 1j * B[..., 1]
            A = -jnp.exp(inv_A_real) + 1j * A_imag
            rep = H // A.shape[0]
            A = jnp.tile(A, (rep, 1))
            Bc = jnp.tile(Bc, (rep, 1))
            dtA = A * dt[:, None]
            Cc = Bc[None, :, :] * Cc
            Cc = Cc * (jnp.exp(dtA) - 1.0) / A
            ell = jnp.arange(L, dtype=jnp.float32)
            V = jnp.exp(dtA[:, :, None] * ell)
            K = 2.0 * jnp.einsum('chn,hnl->chl', Cc, V).real
            return K.astype(jnp.float32)
        key = jax.random.key(seed)
        k1, k2 = jax.random.split(key, 2)
        log_dt = jax.random.uniform(k1, (H,), minval=float(np.log(0.001)), maxval=float(np.log(0.1))).astype(jnp.float32)
        inv_A_real = jnp.full((S, N), float(np.log(0.5)), dtype=jnp.float32)
        A_imag = jnp.tile((np.pi * jnp.arange(N, dtype=jnp.float32))[None, :], (S, 1))
        B = jnp.stack([jnp.ones((S, N), jnp.float32), jnp.zeros((S, N), jnp.float32)], axis=-1)
        C = (jax.random.normal(k2, (CH, H, N, 2)) * 0.5 ** 0.5).astype(jnp.float32)
        return {'log_dt': log_dt, 'C': C, 'B': B, 'inv_A_real': inv_A_real, 'A_imag': A_imag, 'L': LEN}
    _L0_tok_all = _L0_tok_setup()
    _L0_tok_in = {k: v for k, v in _L0_tok_all.items() if k in ('log_dt', 'B', 'inv_A_real', 'A_imag')}
    del _L0_tok_all

    def _L0_attn_setup():
        import math
        import jax, jax.numpy as jnp
        import numpy as np
        NUM_HEADS = 32
        HIDDEN = 1024
        HEAD_DIM = HIDDEN // NUM_HEADS
        NEG_INF = -1e+30

        def _alibi_slopes(n: int) -> jnp.ndarray:
            cp2 = 2 ** math.floor(math.log2(n))
            base = 2.0 ** (-2.0 ** (-(math.log2(cp2) - 3)))
            slopes = base ** np.arange(1, cp2 + 1, dtype=np.float64)
            if cp2 != n:
                extra_base = 2.0 ** (-2.0 ** (-(math.log2(2 * cp2) - 3)))
                rem = min(cp2, n - cp2)
                extra = extra_base ** np.arange(1, 1 + 2 * rem, 2, dtype=np.float64)
                slopes = np.concatenate([slopes, extra])
            return jnp.asarray(slopes, dtype=jnp.float32)
        key = jax.random.key(seed)
        k1, k2, k3 = jax.random.split(key, 3)
        B, S = (2, 512)
        hidden_states = jax.random.normal(k1, (B, S, HIDDEN), dtype=jnp.float32)
        Wqkv = jax.random.normal(k2, (HIDDEN, NUM_HEADS * HEAD_DIM + 2 * HEAD_DIM), dtype=jnp.float32) * 0.02
        Wo = jax.random.normal(k3, (HIDDEN, HIDDEN), dtype=jnp.float32) * 0.02
        return {'hidden_states': hidden_states, 'Wqkv': Wqkv, 'Wo': Wo}
    _L0_attn_all = _L0_attn_setup()
    _L0_attn_in = {k: v for k, v in _L0_attn_all.items() if k in ('Wqkv', 'Wo')}
    del _L0_attn_all

    def _L0_ffn_setup():
        import jax, jax.numpy as jnp
        import numpy as np
        SCALING = 32.0 / 16.0
        key = jax.random.key(seed)
        ks = jax.random.split(key, 7)
        B, T, D, O, R, E = (4, 512, 1024, 1024, 16, 8)
        x = jax.random.normal(ks[0], (B, T, D), dtype=jnp.float32)
        base_W = jax.random.normal(ks[1], (O, D), dtype=jnp.float32) * D ** (-0.5)
        base_b = jax.random.normal(ks[2], (O,), dtype=jnp.float32) * 0.01
        router_W = jax.random.normal(ks[3], (2 * E - 1, D), dtype=jnp.float32) * D ** (-0.5)
        router_b = jax.random.normal(ks[4], (2 * E - 1,), dtype=jnp.float32) * 0.01
        A = jax.random.normal(ks[5], (E, R, D), dtype=jnp.float32) * D ** (-0.5)
        Bm = jax.random.normal(ks[6], (E, O, R), dtype=jnp.float32) * R ** (-0.5)
        assigned_idx = 0
        others = [i for i in range(E) if i != assigned_idx]
        expert_map = jnp.array([assigned_idx] * E + others, dtype=jnp.int32)
        return {'x': x, 'base_W': base_W, 'base_b': base_b, 'router_W': router_W, 'router_b': router_b, 'A': A, 'B': Bm, 'expert_map': expert_map}
    _L0_ffn_all = _L0_ffn_setup()
    _L0_ffn_in = {k: v for k, v in _L0_ffn_all.items() if k in ('base_W', 'base_b', 'router_W', 'router_b', 'A', 'B', 'expert_map')}
    del _L0_ffn_all
    return {'x': x, 'txt': txt, 'L0_tok_log_dt': _L0_tok_in['log_dt'], 'L0_tok_B': _L0_tok_in['B'], 'L0_tok_inv_A_real': _L0_tok_in['inv_A_real'], 'L0_tok_A_imag': _L0_tok_in['A_imag'], 'L0_attn_Wqkv': _L0_attn_in['Wqkv'], 'L0_attn_Wo': _L0_attn_in['Wo'], 'L0_ffn_base_W': _L0_ffn_in['base_W'], 'L0_ffn_base_b': _L0_ffn_in['base_b'], 'L0_ffn_router_W': _L0_ffn_in['router_W'], 'L0_ffn_router_b': _L0_ffn_in['router_b'], 'L0_ffn_A': _L0_ffn_in['A'], 'L0_ffn_B': _L0_ffn_in['B'], 'L0_ffn_expert_map': _L0_ffn_in['expert_map']}

def reference(x, txt, L0_tok_log_dt, L0_tok_B, L0_tok_inv_A_real, L0_tok_A_imag, L0_attn_Wqkv, L0_attn_Wo, L0_ffn_base_W, L0_ffn_base_b, L0_ffn_router_W, L0_ffn_router_b, L0_ffn_A, L0_ffn_B, L0_ffn_expert_map):
    import jax
    import jax.numpy as jnp

    def _L0_tok_ref(log_dt, C, B, inv_A_real, A_imag, L):
        import jax, jax.numpy as jnp
        import numpy as np
        H, N, S, CH, LEN = (128, 64, 128, 1, 1024)

        def _s4d_kernel(log_dt, C, B, inv_A_real, A_imag, L):
            dt = jnp.exp(log_dt)
            Cc = C[..., 0] + 1j * C[..., 1]
            Bc = B[..., 0] + 1j * B[..., 1]
            A = -jnp.exp(inv_A_real) + 1j * A_imag
            rep = H // A.shape[0]
            A = jnp.tile(A, (rep, 1))
            Bc = jnp.tile(Bc, (rep, 1))
            dtA = A * dt[:, None]
            Cc = Bc[None, :, :] * Cc
            Cc = Cc * (jnp.exp(dtA) - 1.0) / A
            ell = jnp.arange(L, dtype=jnp.float32)
            V = jnp.exp(dtA[:, :, None] * ell)
            K = 2.0 * jnp.einsum('chn,hnl->chl', Cc, V).real
            return K.astype(jnp.float32)
        return _s4d_kernel(log_dt, C, B, inv_A_real, A_imag, L)

    def _L0_attn_ref(hidden_states, Wqkv, Wo):
        import math
        import jax, jax.numpy as jnp
        import numpy as np
        NUM_HEADS = 32
        HIDDEN = 1024
        HEAD_DIM = HIDDEN // NUM_HEADS
        NEG_INF = -1e+30

        def _alibi_slopes(n: int) -> jnp.ndarray:
            cp2 = 2 ** math.floor(math.log2(n))
            base = 2.0 ** (-2.0 ** (-(math.log2(cp2) - 3)))
            slopes = base ** np.arange(1, cp2 + 1, dtype=np.float64)
            if cp2 != n:
                extra_base = 2.0 ** (-2.0 ** (-(math.log2(2 * cp2) - 3)))
                rem = min(cp2, n - cp2)
                extra = extra_base ** np.arange(1, 1 + 2 * rem, 2, dtype=np.float64)
                slopes = np.concatenate([slopes, extra])
            return jnp.asarray(slopes, dtype=jnp.float32)
        B, S, H = hidden_states.shape
        nH, d = (NUM_HEADS, HEAD_DIM)
        scale = d ** (-0.5)
        qkv = hidden_states @ Wqkv
        q = qkv[..., :nH * d].reshape(B, S, nH, d)
        k = qkv[..., nH * d:nH * d + d]
        v = qkv[..., nH * d + d:]
        scores = jnp.einsum('bqhd,bkd->bhqk', q, k) * scale
        pos_q = jnp.arange(S)[:, None]
        pos_k = jnp.arange(S)[None, :]
        slopes = _alibi_slopes(nH)
        alibi = slopes[:, None, None] * (pos_k - pos_q).astype(jnp.float32)
        causal = pos_k <= pos_q
        scores = jnp.where(causal[None, None], scores + alibi[None], NEG_INF)
        probs = jax.nn.softmax(scores, axis=-1)
        attn = jnp.einsum('bhqk,bkd->bqhd', probs, v).reshape(B, S, H)
        return attn @ Wo

    def _L0_ffn_ref(x, base_W, base_b, router_W, router_b, A, B, expert_map):
        import jax, jax.numpy as jnp
        import numpy as np
        SCALING = 32.0 / 16.0
        E = A.shape[0]
        base_out = jnp.einsum('btd,od->bto', x, base_W) + base_b
        logits = jnp.einsum('btd,nd->btn', x, router_W) + router_b
        probs = jax.nn.softmax(logits, axis=-1)
        topk_p, topk_i = jax.lax.top_k(probs, E)
        mapped = expert_map[topk_i]
        onehot = (mapped[..., None] == jnp.arange(E)).astype(x.dtype)
        w = jnp.einsum('btk,btke->bte', topk_p, onehot)
        h = jnp.einsum('btd,erd->bter', x, A)
        lora = jnp.einsum('bter,eor->bto', h * w[..., None], B) * SCALING
        return base_out + lora
    h = _L0_tok_ref(L0_tok_log_dt, x, L0_tok_B, L0_tok_inv_A_real, L0_tok_A_imag, 1024)
    h = jnp.concatenate([h, txt], axis=1)
    h = h + _L0_attn_ref(_layernorm(h, axis=-1), L0_attn_Wqkv, L0_attn_Wo)
    h = h + _L0_ffn_ref(_layernorm(h, axis=-1), L0_ffn_base_W, L0_ffn_base_b, L0_ffn_router_W, L0_ffn_router_b, L0_ffn_A, L0_ffn_B, L0_ffn_expert_map)
    return h

_drawn_inputs = setup_inputs


def setup_inputs(seed=0):
    import zlib

    import numpy as np

    out = dict(_drawn_inputs(seed))
    spreads = {'L0_tok_inv_A_real': (-0.6931471824645996, 0.2)}
    factors = {'L0_ffn_base_b': 8.0, 'L0_ffn_router_b': 5.312}
    for name, (base, spread) in spreads.items():
        noise = np.random.default_rng([zlib.crc32(name.encode()), seed]).standard_normal(out[name].shape)
        drawn = base * np.exp(spread * noise) if base else spread * noise
        out[name] = jnp.asarray(drawn.astype(out[name].dtype))
    for name, factor in factors.items():
        out[name] = (out[name] * factor).astype(out[name].dtype)
    return out
```

```python
import math
from contextlib import ExitStack

import numpy as np

import concourse.bass as bass
from concourse import mybir

F32, F32R, I32 = mybir.dt.float32, mybir.dt.float32r, mybir.dt.int32
ALU, ACT, AX = mybir.AluOpType, mybir.ActivationFunctionType, mybir.AxisListType

SEQS, CH, STATES = 16, 128, 64
TXT, DM = 77, 1024
S = CH + TXT
TOK = SEQS * S
HEADS, HD = 32, 32
KC = DM // 128
EXPERTS, RANK, ROUTES = 8, 16, 15
ER = EXPERTS * RANK
EPS = 1e-5

AH = DM // 128
ROUND = 1.5 * 2.0 ** 23
TWO_PI = 6.28318
HCH = 16
MIX_STEPS = CH // HCH

PAIRS = SEQS // 2
PT = 2 * S
SLOTS = 10
BANK_USES = 18
GH = 8
UNITS = 8
TILES = [(0, 0, CH), (0, CH, TXT), (1, 0, CH), (1, CH, TXT)]

FULL = TOK // 128
REST = TOK - FULL * 128
RSQRT_GUESS = float(0x5F3759DF)
NEWTON = 3


def wait_count(eng, sem, count):
    if isinstance(count, int) and count <= 0:
        return
    eng.wait_ge(sem, count)


def wait_apart(eng, sem, count, met, met_count=1):
    if isinstance(count, int):
        wait_count(eng, sem, count)
        return
    value = eng.to_reg(count)
    eng.wait_ge(met, met_count)
    eng.wait_ge(sem, value)


class Chain:

    def __init__(self, eng, sem, base=0, met=None):
        self.eng, self.sem, self.base, self.n, self.met = eng, sem, base, 0, met

    def done(self, ins, apart=False):
        self.n += 1
        ins.then_inc(self.sem, 1)
        if apart:
            wait_apart(self.eng, self.sem, self.base + self.n, self.met)
        else:
            self.eng.wait_ge(self.sem, self.base + self.n)


def rsqrt_newton(nc, link, y, v, t):
    link(nc.vector.tensor_scalar(y.bitcast(I32), v.bitcast(I32), -0.5, RSQRT_GUESS, ALU.mult, ALU.add))
    for _ in range(NEWTON):
        link(nc.vector.tensor_tensor(t, y, y, ALU.mult))
        link(nc.vector.scalar_tensor_tensor(out=t, in0=t, scalar=-0.5, in1=v, op0=ALU.mult, op1=ALU.mult))
        link(nc.vector.scalar_tensor_tensor(out=y, in0=t, scalar=1.5, in1=y, op0=ALU.add, op1=ALU.mult))


RSQRT_LINKS = 1 + 3 * NEWTON


def exp_exact(nc, link, y, x, n, r):
    v = nc.vector
    link(v.tensor_scalar(n, x, 1.0 / math.log(2.0), ROUND, ALU.mult, ALU.add))
    link(v.tensor_scalar(n, n, ROUND, None, ALU.subtract))
    link(v.scalar_tensor_tensor(out=r, in0=n, scalar=-0.693359375, in1=x, op0=ALU.mult, op1=ALU.add))
    link(v.scalar_tensor_tensor(out=r, in0=n, scalar=0.693359375 - math.log(2.0), in1=r, op0=ALU.mult, op1=ALU.add))
    link(v.tensor_scalar(y, r, 1.0 / 5040, None, ALU.mult))
    for k in (6, 5, 4, 3, 2, 1):
        link(v.scalar_tensor_tensor(out=y, in0=y, scalar=1.0 / math.factorial(k), in1=r, op0=ALU.add, op1=ALU.mult))
    link(v.tensor_scalar(n.bitcast(I32), n, 2.0 ** 23, 127 * 2.0 ** 23, ALU.mult, ALU.add))
    link(v.scalar_tensor_tensor(out=y, in0=y, scalar=1.0, in1=n, op0=ALU.add, op1=ALU.mult))


def mixer_block(nc, ctx, io, W):
    def sb(name, shape, dt=F32):
        return ctx.enter_context(nc.sbuf_tensor(name, shape, dt))

    def sem(name):
        return ctx.enter_context(nc.semaphore(name))

    xre, xim = sb("xre", [128, CH, SEQS]), sb("xim", [128, CH, SEQS])
    par = sb("par", [128, 5, CH])
    bvals, avals, quarter = sb("bvals", [128, 128]), sb("avals", [128, AH]), sb("quarter", [128, 3])
    small = sb("small", [128, 16, CH])
    tab = sb("tab", [128, 6, CH, AH])
    G1, G2 = tab[:, 4], tab[:, 5]
    turn_b, frac_b, mag_b = sb("turn_b", [128, HCH, 128]), sb("frac_b", [128, HCH, 128]), sb("mag_b", [128, HCH, 128])
    Qt, X = sb("Qt", [128, 2, HCH, 128]), sb("X", [128, 2, HCH, SEQS, AH])
    X2 = sb("X2", [128, HCH, SEQS, AH])
    Y = sb("Y", [128, HCH, 128])
    stage = sb("w_stage", [128, 2, DM])
    ps = [ctx.enter_context(nc.psum_tensor(f"mix_ps{i}", [128, 4, 128], F32)) for i in range(HCH // 4)]

    loaded, txt_copied = sem("mix_loaded"), sem("txt_copied")
    w_loaded = [sem("w_loaded0"), sem("w_loaded1")]
    w_hi, w_lo = sem("w_hi"), sem("w_lo")
    chain, act_chain, pool_chain = sem("mix_dve_chain"), sem("mix_act_chain"), sem("mix_pool_chain")
    re_ready, tanh_ready = sem("re_ready"), sem("tanh_ready")
    ph_ready, sin_ready, tab_ready = sem("ph_ready"), sem("sin_ready"), sem("tab_ready")
    turns_ready, frac_ready, wave_ready = sem("turns_ready"), sem("frac_ready"), sem("wave_ready")
    q_ready, x2_ready, x_ready = sem("q_ready"), sem("x2_ready"), sem("x_ready")
    mix_done, y_copied = sem("mix_done"), sem("y_copied")
    y_stored = sem("y_stored")

    LDT, BRE, BIM, IAR, AIM = (par[:, i] for i in range(5))
    DT, ARE, RE, TURNS, TH, F_D, SIN1, SIN2, T0, T1, T2, T3, DRE, DIM_, INV, T4 = (small[:, i] for i in range(16))
    PIECES = KC + 1
    h_rows = io["h_dram"].rearrange("(c s) (a b) -> c a s b", s=S, b=128)

    def piece(dst, k):
        return dst[:, k * DM:(k + 1) * DM]

    with nc.Block() as block:
        @block.sync
        def _(sp):
            for half in (slice(0, 64), slice(64, 128)):
                for i, name in enumerate(("log_dt", "B_re", "B_im", "inv_A_real", "A_imag")):
                    sp.dma_start(par[half, i, :], io[name]).then_inc(loaded, 16)
                sp.dma_start(xre[half], io["x_re"]).then_inc(loaded, 16)
                sp.dma_start(xim[half], io["x_im"]).then_inc(loaded, 16)
            sp.dma_start(bvals[:], io["bvals"]).then_inc(loaded, 16)
            sp.dma_start(avals[:], io["avals"]).then_inc(loaded, 16)
            sp.dma_start(quarter[:], io["quarter"]).then_inc(loaded, 16)
            sp.dma_start(W["ident"][:], io["ident"]).then_inc(loaded, 16)
            sp.dma_start(io["h_dram"].rearrange("(c s) d -> c s d", s=S)[:, CH:S, :], io["txt"]).then_inc(txt_copied, 16)

            def load_piece(k):
                if k >= 2:
                    sp.wait_ge(w_lo, k - 1)
                if k < KC:
                    sp.dma_start(stage[:, k % 2, :], io["Wqkv"][k * 128:(k + 1) * 128, 0:DM]).then_inc(w_loaded[k % 2], 64)
                else:
                    kv = stage[:, k % 2, :].rearrange("p (k m) -> p k m", m=128)
                    src = io["Wqkv"][:, DM:DM + 2 * HD].rearrange("(k p) m -> p k m", p=128)
                    for q in range(4):
                        sp.dma_start(kv[:, :, q * HD:(q + 1) * HD],
                                     src[:, :, (q // 3) * HD:(q // 3 + 1) * HD]).then_inc(w_loaded[k % 2], 16)

            load_piece(0)
            load_piece(1)
            for step in range(MIX_STEPS):
                if step + 2 < PIECES:
                    load_piece(step + 2)
                sp.wait_ge(y_copied, step + 1)
                for c in range(SEQS):
                    sp.dma_start(h_rows[c][:, step * HCH:(step + 1) * HCH, :],
                                 Y[c * AH:(c + 1) * AH]).then_inc(y_stored, 16)
            sp.wait_ge(y_stored, 16 * SEQS * MIX_STEPS)
            sp.wait_ge(txt_copied, 16)

        LOADS = 18

        @block.scalar
        def _(act):
            act.wait_ge(loaded, 16 * LOADS)
            act.wait_ge(re_ready, 1)
            nc.scalar.activation(TH, RE, ACT.Tanh, scale=0.5).then_inc(tanh_ready, 1)
            act.wait_ge(ph_ready, 1)
            nc.scalar.activation(SIN1, F_D, ACT.Sin, scale=-TWO_PI / 2).then_inc(sin_ready, 1)
            nc.scalar.activation(SIN2, F_D, ACT.Sin, scale=-TWO_PI).then_inc(sin_ready, 1)
            act.wait_ge(ph_ready, 3)
            nc.scalar.activation(tab[:, 1], tab[:, 1], ACT.Sin, scale=-TWO_PI, bias=quarter[:, 2:3]).then_inc(sin_ready, 1)
            nc.scalar.activation(tab[:, 2], tab[:, 2], ACT.Sin, scale=-TWO_PI).then_inc(sin_ready, 1)
            nc.scalar.activation(tab[:, 3], tab[:, 3], ACT.Exp).then_inc(sin_ready, 1)

            def split_hi(k):
                act.wait_ge(w_loaded[k % 2], 64 * (k // 2 + 1))
                nc.scalar.activation(piece(W["wq_hi"], k), stage[:, k % 2, :], ACT.Copy).then_inc(w_hi, 1)

            def copy_out(step):
                if step >= 1:
                    act.wait_ge(y_stored, 16 * SEQS * step)
                for q in range(HCH // 4):
                    act.wait_ge(mix_done, step * (HCH // 4) + q + 1)
                    last = nc.scalar.activation(Y[:, 4 * q:4 * q + 4, :], ps[q][:], ACT.Copy)
                last.then_inc(y_copied, 1)

            for step in range(MIX_STEPS):
                if step >= 1:
                    act.wait_ge(q_ready, step)
                for j in range(HCH):
                    h = step * HCH + j
                    last = nc.scalar.activation(mag_b[:, j, :], bvals[:], ACT.Exp, scale=RE[:, h:h + 1])
                last.then_inc(act_chain, 1)
                act.wait_ge(frac_ready, step + 1)
                nc.scalar.activation(frac_b[:], frac_b[:], ACT.Sin, scale=-TWO_PI, bias=quarter[:, 1:2]).then_inc(wave_ready, 1)
                split_hi(step)
                if step >= 1:
                    copy_out(step - 1)
            copy_out(MIX_STEPS - 1)
            split_hi(PIECES - 1)

        @block.gpsimd
        def _(pool):
            pool.wait_ge(tab_ready, 2)
            for step in range(MIX_STEPS):
                hs = slice(step * HCH, (step + 1) * HCH)
                if step >= 1:
                    pool.wait_ge(frac_ready, step)
                nc.gpsimd.tensor_tensor(turn_b[:], TURNS[:, hs].unsqueeze(2).to_broadcast((128, HCH, 128)),
                                        bvals[:].unsqueeze(1).to_broadcast((128, HCH, 128)), ALU.mult).then_inc(turns_ready, 1)
                if step >= 1:
                    pool.wait_ge(x_ready, step)
                for j in range(HCH):
                    h = step * HCH + j
                    last = nc.gpsimd.tensor_tensor(X2[:, j], xim[:, h, :].unsqueeze(2).to_broadcast((128, SEQS, AH)),
                                                   G2[:, h, :].unsqueeze(1).to_broadcast((128, SEQS, AH)), ALU.mult)
                last.then_inc(x2_ready, 1)
                pool.wait_ge(w_hi, step + 1)
                nc.gpsimd.tensor_tensor(piece(W["wq_lo"], step), stage[:, step % 2, :],
                                        piece(W["wq_hi"], step).bitcast(F32), ALU.subtract).then_inc(w_lo, 1)
            pool.wait_ge(w_hi, PIECES)
            k = PIECES - 1
            nc.gpsimd.tensor_tensor(piece(W["wq_lo"], k), stage[:, k % 2, :],
                                    piece(W["wq_hi"], k).bitcast(F32), ALU.subtract).then_inc(w_lo, 1)
            pool.wait_ge(w_lo, PIECES)

        @block.vector
        def _(dve):
            link = Chain(dve, chain).done
            v = nc.vector
            dve.wait_ge(loaded, 16 * LOADS)
            exp_exact(nc, link, DT, LDT, T0, T1)
            exp_exact(nc, link, ARE, IAR, T0, T1)
            link(v.tensor_scalar(ARE, ARE, -1.0, None, ALU.mult))
            v.tensor_tensor(RE, ARE, DT, ALU.mult).then_inc(re_ready, 1)
            link(v.tensor_tensor(TURNS, AIM, DT, ALU.mult))
            link(v.tensor_scalar(TURNS, TURNS, 1.0 / (2.0 * math.pi), None, ALU.mult))
            link(v.tensor_scalar(F_D, TURNS, ROUND, None, ALU.add))
            v.scalar_tensor_tensor(out=F_D, in0=F_D, scalar=ROUND, in1=TURNS, op0=ALU.subtract, op1=ALU.subtract).then_inc(ph_ready, 1)
            tb, ab = TURNS.unsqueeze(2).to_broadcast((128, CH, AH)), avals[:].unsqueeze(1).to_broadcast((128, CH, AH))
            link(v.tensor_tensor(tab[:, 0], tb, ab, ALU.mult))
            link(v.tensor_scalar(tab[:, 1], tab[:, 0], 0.25, ROUND, ALU.add, ALU.add))
            link(v.tensor_scalar(tab[:, 2], tab[:, 0], ROUND, None, ALU.add))
            v.scalar_tensor_tensor(out=tab[:, 1], in0=tab[:, 1], scalar=ROUND, in1=tab[:, 0], op0=ALU.subtract, op1=ALU.subtract).then_inc(ph_ready, 1)
            dve.wait_ge(re_ready, 1)
            link(v.tensor_tensor(tab[:, 3], RE.unsqueeze(2).to_broadcast((128, CH, AH)), ab, ALU.mult))
            v.scalar_tensor_tensor(out=tab[:, 2], in0=tab[:, 2], scalar=ROUND, in1=tab[:, 0], op0=ALU.subtract, op1=ALU.subtract).then_inc(ph_ready, 1)
            dve.wait_ge(tanh_ready, 1)
            link(v.tensor_scalar(T0, TH, -1.0, 1.0, ALU.mult, ALU.add))
            link(v.reciprocal(T0, T0))
            link(v.scalar_tensor_tensor(out=T0, in0=TH, scalar=2.0, in1=T0, op0=ALU.mult, op1=ALU.mult))
            link(v.tensor_scalar(T1, T0, 1.0, None, ALU.add))
            dve.wait_ge(sin_ready, 2)
            link(v.tensor_tensor(T2, SIN1, SIN1, ALU.mult))
            link(v.scalar_tensor_tensor(out=T2, in0=T2, scalar=-2.0, in1=T1, op0=ALU.mult, op1=ALU.mult))
            link(v.tensor_tensor(T0, T0, T2, ALU.add))
            link(v.tensor_tensor(T1, T1, SIN2, ALU.mult))
            link(v.tensor_tensor(T2, ARE, ARE, ALU.mult))
            link(v.tensor_tensor(T3, AIM, AIM, ALU.mult))
            link(v.tensor_tensor(T2, T2, T3, ALU.add))
            link(v.reciprocal(INV, T2))
            link(v.tensor_scalar(INV, INV, 2.0, None, ALU.mult))
            link(v.tensor_tensor(T2, T0, ARE, ALU.mult))
            link(v.tensor_tensor(T3, T1, AIM, ALU.mult))
            link(v.tensor_tensor(T2, T2, T3, ALU.add))
            link(v.tensor_tensor(T3, T1, ARE, ALU.mult))
            link(v.tensor_tensor(T4, T0, AIM, ALU.mult))
            link(v.tensor_tensor(T3, T3, T4, ALU.subtract))
            link(v.tensor_tensor(T2, T2, INV, ALU.mult))
            link(v.tensor_tensor(T3, T3, INV, ALU.mult))
            link(v.tensor_tensor(T0, BRE, T2, ALU.mult))
            link(v.tensor_tensor(T1, BIM, T3, ALU.mult))
            link(v.tensor_tensor(DRE, T0, T1, ALU.subtract))
            link(v.tensor_tensor(T0, BRE, T3, ALU.mult))
            link(v.tensor_tensor(T1, BIM, T2, ALU.mult))
            link(v.tensor_tensor(DIM_, T0, T1, ALU.add))
            dve.wait_ge(sin_ready, 5)
            ta, tb2 = (X2[:, 8 * i:8 * i + 8].rearrange("p h c a -> p (h c a)").rearrange("p (h a) -> p h a", a=AH) for i in range(2))
            dre, dim = (z.unsqueeze(2).to_broadcast((128, CH, AH)) for z in (DRE, DIM_))
            link(v.tensor_tensor(tab[:, 1], tab[:, 1], tab[:, 3], ALU.mult))
            link(v.tensor_tensor(tab[:, 2], tab[:, 2], tab[:, 3], ALU.mult))
            link(v.tensor_tensor(ta, dre, tab[:, 1], ALU.mult))
            link(v.tensor_tensor(tb2, dim, tab[:, 2], ALU.mult))
            link(v.tensor_tensor(tab[:, 0], ta, tb2, ALU.subtract))
            link(v.tensor_tensor(ta, dre, tab[:, 2], ALU.mult))
            link(v.tensor_tensor(tb2, dim, tab[:, 1], ALU.mult))
            link(v.tensor_tensor(tab[:, 3], ta, tb2, ALU.add))
            top, low = slice(0, 64), slice(64, 128)
            v.tensor_copy(tab[top, 4], tab[top, 0]).then_inc(chain, 1)
            v.tensor_scalar(tab[low, 4], tab[low, 3], -1.0, None, ALU.mult).then_inc(chain, 1)
            v.tensor_scalar(tab[top, 5], tab[top, 3], -1.0, None, ALU.mult).then_inc(tab_ready, 1)
            v.tensor_scalar(tab[low, 5], tab[low, 0], -1.0, None, ALU.mult).then_inc(tab_ready, 1)
            dve.wait_ge(tab_ready, 2)
            steps = Chain(dve, sem("mix_step_chain"))
            for step in range(MIX_STEPS):
                par2 = step % 2
                dve.wait_ge(turns_ready, step + 1)
                if step >= 1:
                    dve.wait_ge(q_ready, step)
                steps.done(v.tensor_scalar(frac_b[:], turn_b[:], quarter[:, 0:1], ROUND, ALU.add, ALU.add))
                v.scalar_tensor_tensor(out=frac_b[:], in0=frac_b[:], scalar=ROUND, in1=turn_b[:],
                                       op0=ALU.subtract, op1=ALU.subtract).then_inc(frac_ready, 1)
                if step >= 2:
                    dve.wait_ge(mix_done, (step - 1) * (HCH // 4))
                for j in range(HCH):
                    h = step * HCH + j
                    last = v.tensor_tensor(X[:, par2, j], xre[:, h, :].unsqueeze(2).to_broadcast((128, SEQS, AH)),
                                           G1[:, h, :].unsqueeze(1).to_broadcast((128, SEQS, AH)), ALU.mult)
                steps.done(last)
                dve.wait_ge(x2_ready, step + 1)
                v.tensor_tensor(X[:, par2], X[:, par2], X2[:], ALU.add).then_inc(x_ready, 1)
                dve.wait_ge(wave_ready, step + 1)
                dve.wait_ge(act_chain, step + 1)
                v.tensor_tensor(Qt[:, par2], frac_b[:], mag_b[:], ALU.mult).then_inc(q_ready, 1)

        @block.tensor
        def _(pe):
            for step in range(MIX_STEPS):
                pe.wait_ge(x_ready, step + 1)
                pe.wait_ge(q_ready, step + 1)
                if step >= 1:
                    pe.wait_ge(y_copied, step)
                for j in range(HCH):
                    last = nc.tensor.matmul(ps[j // 4][:, j % 4, :], X[:, step % 2, j].rearrange("p c a -> p (c a)"),
                                            Qt[:, step % 2, j, :], start=True, stop=True)
                    if j % 4 == 3:
                        last.then_inc(mix_done, 1)


def attention_block(nc, ctx, io, W):
    def sb(name, shape, dt=F32):
        return ctx.enter_context(nc.sbuf_tensor(name, shape, dt))

    def pb(name, shape):
        return ctx.enter_context(nc.psum_tensor(name, shape, F32))

    def sem(name):
        return ctx.enter_context(nc.semaphore(name))

    ident = W["ident"]
    wq = [W["wq_hi"][:, 0:KC * DM].rearrange("p (k m) -> p k m", k=KC), W["wq_lo"][:, 0:KC * DM].rearrange("p (k m) -> p k m", k=KC)]
    wkv = [w[:, KC * DM:(KC + 1) * DM].rearrange("p (k m) -> p k m", k=KC) for w in (W["wq_hi"], W["wq_lo"])]
    ht = sb("ht", [128, 4, DM])
    stats, mv = sb("stats", [128, 4, 2, 6]), sb("mv", [128, 4, 2])
    rstd, rtmp, veps = sb("rstd", [128, 4]), sb("rtmp", [128, 4]), sb("veps", [128, 4])
    xT = [sb("xT_hi", [128, KC, PT], F32R), sb("xT_lo", [128, KC, PT], F32R)]
    q_hi, q_lo = sb("q_hi", [128, 2, PT], F32R), sb("q_lo", [128, 2, PT], F32R)
    QR = 3 * HD + 4
    Qs = sb("Qs", [128, 2, GH, PT], F32R)
    Ks = sb("Ks", [128, 2, 2, S + 1], F32R)
    crow = sb("crow", [128, 16 + 4 * (S + 1)])
    vT = sb("vT", [128, PT])
    V0, V1 = sb("V0", [128, 2, HD]), sb("V1", [128, 2, HD])
    mask = sb("mask", [128, 2 * 128])
    P = sb("P", [128, 2, GH, CH + S])
    nmax, den, rden = (sb(n, [128, 2, 2, 2, 4]) for n in ("nmax", "den", "rden"))
    PT0, PT1 = sb("PT0", [128, 2, GH, S]), sb("PT1", [128, 2, GH, TXT])
    att = sb("att", [128, 2, 2, S])

    sc = [pb(f"sc{i}", [128, 512]) for i in range(2)]
    pt = [pb(f"pt{i}", [128, 512]) for i in range(2)]
    av = [pb(f"av{i}", [128, 512]) for i in range(2)]
    pr = [pb(f"pr{i}", [128, 512]) for i in range(2)]

    const_loaded, const_ready = sem("att_const_loaded"), sem("att_const_ready")
    h_loaded = [sem(f"h_loaded{i}") for i in range(4)]
    chain = sem("att_dve_chain")
    xn_ready = sem("xn_ready")
    proj_done, hi_written, bank_read = sem("proj_done"), sem("hi_written"), sem("bank_read")
    q_stacked = [sem("q_stacked0"), sem("q_stacked1")]
    scores_done, scores_biased, exp_done = sem("scores_done"), sem("scores_biased"), sem("exp_done")
    recip_done, probs_ready = sem("recip_done"), sem("probs_ready")
    transposed, pT_copied = sem("transposed"), sem("pT_copied")
    av_done, att_copied = sem("av_done"), sem("att_copied")
    att_stored = [sem("att_stored0"), sem("att_stored1")]
    k_split = sem("k_split")

    SCALE = HD ** -0.5
    STACKS = 12
    MAIN = ["ln", ("q", 0), ("q", 1), "kv", ("q", 2), ("q", 3), ("q", 4), ("q", 5), ("q", 6), ("q", 7)]
    USE = {0: 8, 1: 9, 2: 11, 3: 13, 4: 14, 5: 15, 6: 16, 7: 17}
    KV_USE, VT_USE = 10, 12
    V_SLOT = 5

    def hi_count(use):
        return use + 1 if use < VT_USE else use

    def att_unit(slot, lag):
        j = slot - 5 - lag
        if j >= 0:
            return (0, j) if j < UNITS else None
        return (1, j + SLOTS) if j + SLOTS < UNITS else None

    def visit(body, after=None):
        def run(eng):
            body(0, True, False)
            with eng.Fori(1, PAIRS - 1) as p:
                body(p, False, False)
            body(PAIRS - 1, False, True)
            body(PAIRS, False, None)
        return run

    def slots(p, first, last):
        for slot in range(SLOTS):
            def unit(lag, slot=slot):
                found = att_unit(slot, lag)
                if found is None:
                    return None
                back, j = found
                if (back and first) or (not back and last is None):
                    return None
                return (p - back, j)
            yield slot, (MAIN[slot] if last is not None else None), unit(0), unit(1), unit(2)

    with nc.Block() as block:
        @block.sync
        def _(sp):
            sp.dma_start(mask[:], io["mask"]).then_inc(const_loaded, 16)
            sp.dma_start(crow[96:100, :], io["rows"]).then_inc(const_loaded, 16)

            def load_h(p, s):
                c, t0, n = TILES[s]
                r0 = p * PT + (c * S + t0)
                sp.dma_start(ht[0:n, s, :], io["h_dram"][bass.ds(r0, n), :]).then_inc(h_loaded[s], 16)

            def stack_q(p, k):
                g, r = k // 2, k % 2
                wait_apart(sp, bank_read, BANK_USES * p + USE[k] + 1, const_loaded, 32)
                wait_count(sp, scores_done, 64 * p + 16 * g - 16)
                for j in range(4):
                    for row, src in ((0, q_hi), (HD, q_hi), (2 * HD, q_lo)):
                        sp.dma_start(Qs[row:row + HD, g % 2, 4 * r + j, :].bitcast(F32), src[HD * j:HD * j + HD, r, :].bitcast(F32)).then_inc(q_stacked[r], 16)

            def store_att(p, j):
                g, b = j // 2, j % 2
                sp.wait_ge(att_copied, 8 * p + j + 1)
                dst = io["att_dram"].rearrange("(k p) t -> p k t", p=128)[:, 2 * g:2 * g + 2, bass.ds(p * PT + b * S, S)]
                sp.dma_start(dst, att[:, b, :, :]).then_inc(att_stored[b], 16)

            def body(p, first, last):
                for slot, main, sj, tj, aj in slots(p, first, last):
                    if main is not None and slot >= 1 and isinstance(MAIN[slot - 1], tuple):
                        stack_q(p, MAIN[slot - 1][1])
                    if slot == 0 and not first:
                        stack_q(p - 1, 7)
                    if slot in (1, 2) and last is False:
                        for s in (2 * slot - 2, 2 * slot - 1):
                            sp.wait_ge(proj_done, BANK_USES * p + 2 * (s + 1))
                            load_h(p + 1, s)
                    if aj is not None:
                        store_att(*aj)
            for s in range(4):
                load_h(0, s)
            visit(body)(sp)
            for s in att_stored:
                sp.wait_ge(s, 16 * PAIRS * UNITS // 2)

        @block.tensor
        def _(pe):
            def scores(p, j, i):
                g, b = j // 2, j % 2
                if i == 0:
                    for q in q_stacked:
                        pe.wait_ge(q, 16 * STACKS * (4 * p + g + 1))
                    if j == 0:
                        pe.wait_ge(bank_read, BANK_USES * p + KV_USE + 1)
                n = 64 * p + 8 * j + i
                wait_count(pe, scores_biased, n - 1)
                bank, q = sc[i % 2], Qs[0:QR, g % 2, i, b * S:(b + 1) * S]
                nc.tensor.matmul(bank[:, 0:CH], q[:, 0:CH], Ks[0:QR, g // 2, b, 0:CH], start=True, stop=True)
                nc.tensor.matmul(bank[0:TXT, CH:CH + S + 1], q[:, CH:S], Ks[0:QR, g // 2, b, :],
                                 start=True, stop=True).then_inc(scores_done, 1)

            def turn(p, j, i):
                if i % 4 == 0:
                    pe.wait_ge(probs_ready, 16 * p + 2 * j + i // 4 + 1)
                wait_count(pe, pT_copied, 64 * p + 8 * j + i - 1)
                bank, src = pt[i % 2], P[:, j % 2, i, :]
                nc.tensor.transpose(bank[:, 0:CH], src[:, 0:CH], ident[:])
                nc.tensor.transpose(bank[:, CH:S], src[0:TXT, CH:2 * CH], ident[0:TXT, 0:TXT])
                nc.tensor.transpose(bank[0:TXT, S + 1:S + 1 + TXT], src[0:TXT, 2 * CH:CH + S],
                                    ident[0:TXT, 0:TXT]).then_inc(transposed, 1)

            def values(p, j):
                b, o = j % 2, av[j % 2]
                pe.wait_ge(pT_copied, 64 * p + 8 * (j + 1))
                wait_count(pe, att_copied, 8 * p + j - 1)
                if j == 0:
                    pe.wait_ge(bank_read, BANK_USES * p + VT_USE + 1)
                for q in range(4):
                    rows = slice(32 * q, 32 * q + 32)
                    nc.tensor.matmul(o[rows, 0:2 * S], V0[:, b, :], PT0[:, j % 2, q:q + 5:4, :], start=True, stop=False)
                for q in range(4):
                    rows = slice(32 * q, 32 * q + 32)
                    last = nc.tensor.matmul(o[rows, 0:2 * S].rearrange("p (c t) -> p c t", c=2)[:, :, CH:S],
                                            V1[0:TXT, b, :], PT1[0:TXT, j % 2, q:q + 5:4, :], start=False, stop=True)
                last.then_inc(av_done, 1)

            def three(out, w, cols, i):
                for m, (a, x) in enumerate(((0, 0), (0, 1), (1, 0))):
                    last = nc.tensor.matmul(out, w[a][:, i, cols], xT[x][:, i, :], start=(i == 0 and m == 0),
                                            stop=(i == KC - 1 and m == 2))
                return last

            def main_step(p, slot, what, i):
                if what == "ln":
                    wait_count(pe, bank_read, BANK_USES * p + i - 1)
                    s, half = i // 2, i % 2
                    if half == 0:
                        pe.wait_ge(xn_ready, 4 * p + s + 1)
                    n = TILES[s][2]
                    for q in range(4):
                        last = nc.tensor.transpose(pr[i % 2][:, 128 * q:128 * q + n],
                                                   ht[0:n, s, (4 * half + q) * 128:(4 * half + q + 1) * 128], ident[0:n, 0:n])
                    last.then_inc(proj_done, 1)
                    return
                use = KV_USE if what == "kv" else USE[what[1]]
                if i == 0:
                    if slot == V_SLOT:
                        wait_apart(pe, bank_read, BANK_USES * p + VT_USE - 1, const_ready)
                        for c in range(2):
                            nc.tensor.transpose(pr[VT_USE % 2][:, 64 * c:64 * c + HD], vT[96:128, c * S:c * S + CH], ident[96:128, 96:128])
                            last = nc.tensor.transpose(pr[VT_USE % 2][0:TXT, 64 * c + HD:64 * c + 2 * HD],
                                                       vT[96:128, c * S + CH:(c + 1) * S], ident[96:128, 96:128])
                        last.then_inc(proj_done, 1)
                    pe.wait_ge(bank_read, BANK_USES * p + max(use - 1, 8))
                if what == "kv":
                    last = three(pr[use % 2][:, 0:PT], wkv, slice(0, 128), i)
                else:
                    last = three(pr[use % 2][:, 0:PT], wq, slice(128 * what[1], 128 * what[1] + 128), i)
                if i == KC - 1:
                    last.then_inc(proj_done, 1)

            def body(p, first, last):
                for slot, main, sj, tj, aj in slots(p, first, last):
                    for i in range(GH):
                        if sj is not None:
                            scores(*sj, i)
                        if main is not None:
                            main_step(p, slot, main, i)
                        turning = tj if i >= 4 else aj
                        if turning is not None:
                            turn(*turning, (i + 4) % GH)
                        if i == 5 and aj is not None:
                            values(*aj)
            pe.wait_ge(const_ready, 1)
            visit(body)(pe)

        @block.scalar
        def _(act):
            def exp_head(p, j, i):
                act.wait_ge(scores_biased, 64 * p + 8 * j + i + 1)
                for t, (rows, cols) in enumerate(((slice(0, CH), slice(0, CH)), (slice(0, TXT), slice(CH, CH + S)))):
                    at = (rows, j % 2, i // 4, t, slice(i % 4, i % 4 + 1))
                    last = nc.scalar.activation(P[rows, j % 2, i, cols], P[rows, j % 2, i, cols], ACT.Exp, scale=-1.0,
                                                bias=nmax[at], accum_out=den[at])
                last.then_inc(exp_done, 1)

            def hi_part(p, slot, i):
                what = MAIN[slot]
                if what == "ln":
                    s, half = i // 2, i % 2
                    c, t0, n = TILES[s]
                    act.wait_ge(proj_done, BANK_USES * p + i + 1)
                    src = pr[i % 2][:, :].rearrange("p (q t) -> p q t", q=4)[:, :, 0:n]
                    nc.scalar.activation(xT[0][:, 4 * half:4 * half + 4, c * S + t0:c * S + t0 + n], src, ACT.Copy).then_inc(hi_written, 1)
                elif what == "kv":
                    act.wait_ge(proj_done, BANK_USES * p + KV_USE + 1)
                    wait_count(act, scores_done, 64 * p)
                    src = pr[KV_USE % 2]
                    for v in range(2):
                        nc.scalar.activation(Ks[0:96, v, :, 0:S], src[0:96, 0:PT].rearrange("p (b t) -> p b t", b=2), ACT.Copy)
                    nc.scalar.activation(vT[96:128, :], src[96:128, 0:PT], ACT.Copy).then_inc(hi_written, 1)
                else:
                    k = what[1]
                    act.wait_ge(proj_done, BANK_USES * p + USE[k] + 1)
                    wait_count(act, q_stacked[k % 2], 16 * STACKS * (4 * p + k // 2))
                    nc.scalar.activation(q_hi[:, k % 2, :], pr[USE[k] % 2][:, 0:PT], ACT.Copy, scale=-SCALE).then_inc(hi_written, 1)

            def body(p, first, last):
                for slot, main, sj, tj, aj in slots(p, first, last):
                    if slot == 0 and not first:
                        hi_part(p - 1, SLOTS - 1, 0)
                    if slot >= 2 and main is not None:
                        hi_part(p, slot - 1, 0)
                    for i in range(GH):
                        if slot == 0 and main is not None:
                            hi_part(p, 0, i)
                        if sj is not None:
                            exp_head(*sj, i)
                        if i == 7 and aj is not None:
                            q, j = aj
                            act.wait_ge(av_done, 8 * q + j + 1)
                            wait_count(act, att_stored[j % 2], 16 * (4 * q + j // 2))
                            nc.scalar.activation(att[:, j % 2].rearrange("p c t -> p (c t)"), av[j % 2][:, 0:2 * S], ACT.Copy).then_inc(att_copied, 1)
            act.wait_ge(const_ready, 1)
            visit(body)(act)

        @block.gpsimd
        def _(pool):
            def body(p, first, last):
                for slot, main, sj, tj, aj in slots(p, first, last):
                    for unit, half in ((tj, 0), (tj, 1)):
                        if unit is None:
                            continue
                        q, j = unit
                        pool.wait_ge(recip_done, 16 * q + 2 * j + half + 1)
                        for t, (n, cols) in enumerate(((CH, slice(0, CH)), (TXT, slice(CH, CH + S)))):
                            w = P[0:n, j % 2, 4 * half:4 * half + 4, cols]
                            r = rden[0:n, j % 2, half, t, :].unsqueeze(2).to_broadcast((n, 4, cols.stop - cols.start))
                            lastp = nc.gpsimd.tensor_tensor(w, w, r, ALU.mult)
                        lastp.then_inc(probs_ready, 1)
            visit(body)(pool)

        CHAINS = 8 + 4 + 1 + RSQRT_LINKS

        @block.vector
        def _(dve):
            v = nc.vector

            def bias_head(p, j, i):
                wait_count(dve, transposed, 64 * p + 8 * (j - 2) + i + 1)
                wait_apart(dve, scores_done, 64 * p + 8 * j + i + 1, const_loaded, 32)
                for t, (n, cols, m) in enumerate(((CH, slice(0, CH), slice(CH, 2 * CH)), (TXT, slice(CH, CH + S), slice(0, S)))):
                    lastv = v.tensor_tensor_reduce(P[0:n, j % 2, i, cols], sc[i % 2][0:n, cols], mask[0:n, m], 1.0, 3.0e38,
                                                   ALU.add, ALU.min, nmax[0:n, j % 2, i // 4, t, i % 4:i % 4 + 1])
                lastv.then_inc(scores_biased, 1)

            def recip(p, j, half):
                dve.wait_ge(exp_done, 64 * p + 8 * j + 4 * half + 4)
                v.reciprocal(rden[:, j % 2, half], den[:, j % 2, half]).then_inc(recip_done, 1)

            def copy_turned(p, j, i):
                dve.wait_ge(transposed, 64 * p + 8 * j + i + 1)
                if i == 0:
                    wait_count(dve, av_done, 8 * p + j - 1)
                v.tensor_copy(PT0[:, j % 2, i, :], pt[i % 2][:, 0:S])
                v.tensor_copy(PT1[0:TXT, j % 2, i, :], pt[i % 2][0:TXT, S + 1:S + 1 + TXT]).then_inc(pT_copied, 1)

            def lo_part(p, slot, i):
                what = MAIN[slot]
                if what == "ln":
                    s, half = i // 2, i % 2
                    c, t0, n = TILES[s]
                    dve.wait_ge(hi_written, (BANK_USES - 1) * p + i + 1)
                    at = (slice(None), slice(4 * half, 4 * half + 4), slice(c * S + t0, c * S + t0 + n))
                    src = pr[i % 2][:, :].rearrange("p (q t) -> p q t", q=4)[:, :, 0:n]
                    v.tensor_tensor(xT[1][at], src, xT[0][at].bitcast(F32), ALU.subtract).then_inc(bank_read, 1)
                elif what == "kv":
                    dve.wait_ge(hi_written, (BANK_USES - 1) * p + hi_count(KV_USE))
                    src = pr[KV_USE % 2][HD:2 * HD, 0:PT].rearrange("p (b t) -> p b t", b=2)
                    for var in range(2):
                        at = Ks[HD:2 * HD, var, :, 0:S]
                        lastv = v.tensor_tensor(at, src, at.bitcast(F32), ALU.subtract)
                    lastv.then_inc(bank_read, 1)
                else:
                    k = what[1]
                    dve.wait_ge(hi_written, (BANK_USES - 1) * p + hi_count(USE[k]))
                    v.scalar_tensor_tensor(out=q_lo[:, k % 2, :], in0=pr[USE[k] % 2][:, 0:PT], scalar=-SCALE,
                                           in1=q_hi[:, k % 2, :].bitcast(F32), op0=ALU.mult, op1=ALU.subtract).then_inc(bank_read, 1)

            def copy_v(p):
                dve.wait_ge(proj_done, BANK_USES * p + VT_USE + 1)
                wait_count(dve, av_done, 8 * p)
                src = pr[VT_USE % 2][:, 0:128].rearrange("p (b t d) -> p b t d", b=2, t=2)
                v.tensor_copy(V0[:], src[:, :, 0, :])
                v.tensor_copy(V1[0:TXT], src[0:TXT, :, 1, :]).then_inc(bank_read, 1)

            def ln_stats(p, s, link):
                n = TILES[s][2]
                dve.wait_ge(h_loaded[s], 16 * (p + 1))
                link(v.bn_stats(stats[0:n, s, 0, :], ht[0:n, s, 0:512]))
                link(v.bn_stats(stats[0:n, s, 1, :], ht[0:n, s, 512:1024]), apart=True)
                link(v.bn_aggr(mv[0:n, s, :], stats[0:n, s].rearrange("p a b -> p (a b)")))

            def ln_rstd(link):
                link(v.tensor_scalar(veps[:], mv[:, :, 1], EPS, None, ALU.add))
                rsqrt_newton(nc, link, rstd[:], veps[:], rtmp[:])

            def ln_apply(p, s):
                n = TILES[s][2]
                v.tensor_scalar(ht[0:n, s, :], ht[0:n, s, :], mv[0:n, s, 0:1], rstd[0:n, s:s + 1],
                                ALU.subtract, ALU.mult).then_inc(xn_ready, 1)

            def body(p, first, last):
                link = Chain(dve, chain, CHAINS * (p + 1) if last is False else 0, const_ready).done
                for slot, main, sj, tj, aj in slots(p, first, last):
                    for i in range(GH):
                        if sj is not None:
                            bias_head(*sj, i)
                        if i == 0 and slot == 0 and not first:
                            lo_part(p - 1, SLOTS - 1, 0)
                        if i == 0 and slot >= 2 and main is not None:
                            lo_part(p, slot - 1, 0)
                        if i == 2 and slot == V_SLOT and main is not None:
                            copy_v(p)
                        if slot == 0 and main is not None:
                            lo_part(p, 0, i)
                        if i in (0, 3) and tj is not None:
                            recip(*tj, i // 3)
                        if last is False:
                            if slot in (6, 7) and i in (3, 5):
                                ln_stats(p + 1, 2 * (slot - 6) + (i - 3) // 2, link)
                            if slot == 8 and i == 3:
                                ln_rstd(link)
                            if slot == 9 and i >= 4:
                                ln_apply(p + 1, i - 4)
                        turning = tj if i >= 4 else aj
                        if turning is not None:
                            copy_turned(*turning, (i + 4) % GH)

            first = Chain(dve, sem("att_setup_chain"))
            dve.wait_ge(const_loaded, 32)
            v.memset(den[:], 1.0)
            v.memset(mv[:], 1.0)
            first.done(v.memset(Ks[:].bitcast(F32), 0.0))
            v.tensor_copy(Ks[96:100], crow[96:100, 16:16 + 4 * (S + 1)].rearrange("p (v b t) -> p v b t", v=2, b=2))
            first.done(v.tensor_copy(Qs[96:100].rearrange("p s h t -> p (s h) t"),
                                     crow[96:100, 0:16].unsqueeze(2).to_broadcast((4, 16, PT))))
            link = Chain(dve, chain).done
            for s in range(4):
                ln_stats(0, s, link)
            ln_rstd(link)
            for s in range(4):
                ln_apply(0, s)
            v.memset(rtmp[:, 0:1], 0.0).then_inc(const_ready, 1)
            visit(body)(dve)


def mlp_block(nc, ctx, io, W):
    def sb(name, shape, dt=F32):
        return ctx.enter_context(nc.sbuf_tensor(name, shape, dt))

    def pb(name):
        return ctx.enter_context(nc.psum_tensor(name, [128, 512], F32))

    def sem(name):
        return ctx.enter_context(nc.semaphore(name))

    ident = W["ident"]
    ARW = 144
    PIECES = 2 * KC + 3
    SIZES = [DM] * (2 * KC) + [KC * ARW // 2] * 2 + [DM]
    OFFS = [sum(SIZES[:k]) for k in range(PIECES + 1)]
    w_hi, w_lo = sb("w2_hi", [128, OFFS[-1]], F32R), sb("w2_lo", [128, OFFS[-1]], F32R)
    RING = 3
    stage = sb("w2_stage", [128, RING, DM])

    def part(lo, n, w):
        return [t[:, OFFS[lo]:OFFS[lo] + n * w].rearrange("p (k m) -> p k m", k=n) for t in (w_hi, w_lo)]

    wo, wb, war, wB = part(0, KC, DM), part(KC, KC, DM), part(2 * KC, KC, ARW), part(2 * KC + 2, 1, DM)
    base_b, rout_b = sb("base_b", [128, DM]), sb("rout_b", [128, ROUTES])
    emap, emapf, sel_map = sb("emap", [128, ROUTES], I32), sb("emapf", [128, ROUTES]), sb("sel_map", [128, EXPERTS, ROUTES])
    at = sb("at", [128, 2, KC, 128])
    aT = [sb("aT_hi", [128, KC, 128], F32R), sb("aT_lo", [128, KC, 128], F32R)]
    h2 = sb("h2", [128, 2, DM])
    xn = sb("xn", [128, DM])
    xT = [sb("x2T_hi", [128, KC, 128], F32R), sb("x2T_lo", [128, KC, 128], F32R)]
    stats, mv, rstd, rtmp, veps = sb("stats2", [128, 2, 6]), sb("mv2", [128, 2]), sb("rstd2", [128, 1]), sb("rtmp2", [128, 1]), sb("veps2", [128, 1])
    lg, m8, nm = sb("lg", [128, ROUTES]), sb("m8", [128, 8]), sb("nm", [128, 1])
    ex, e8, er, dn, rd = sb("ex", [128, ROUTES]), sb("e8", [128, 8]), sb("er", [128, ROUTES]), sb("dn", [128, 1]), sb("rd", [128, 1])
    wsel, w8 = sb("wsel", [128, EXPERTS, ROUTES]), sb("w8", [128, EXPERTS])
    z = sb("z", [128, ER])
    zT = [sb("zT_hi", [128, 128], F32R), sb("zT_lo", [128, 128], F32R)]

    wo_ps, x_ps, base_ps = [pb("wo0"), pb("wo1")], [pb("x0"), pb("x1")], [pb("b0"), pb("b1")]
    ar_ps, z_ps = pb("ar"), pb("zp")

    const_loaded, w_loaded = sem("mlp_const_loaded"), [sem(f"w2_loaded{i}") for i in range(RING)]
    hi_split, lo_split = sem("w2_hi_done"), sem("w2_lo_done")
    a_loaded, r_loaded = [sem("a_loaded0"), sem("a_loaded1")], [sem("r_loaded0"), sem("r_loaded1")]
    a_hi, a_lo, wo_done, wo_read = sem("a_hi"), sem("a_lo"), sem("wo_done"), sem("wo_read")
    x_ready, biased = sem("x2_ready"), sem("h2_biased")
    xT_done, xT_hi, xT_lo = sem("x2T_done"), sem("x2T_hi_done"), sem("x2T_lo_done")
    ar_done, logits_ready, exp_ready, z_ready = sem("ar_done"), sem("logits_ready"), sem("router_exp"), sem("z_ready")
    zT_done, zT_hi, zT_lo = sem("zT_done"), sem("zT_hi_done"), sem("zT_lo_done")
    base_done, out_ready, setup, chain = sem("base_done"), sem("out_ready"), sem("mlp_setup"), sem("mlp_chain")
    out_stored = [sem("out_stored0"), sem("out_stored1")]
    LAST = FULL

    def visit(eng, body):
        size = lambda t: 128 if t < FULL else (REST if t == FULL else 0)
        pairs = (FULL - 2) // 2
        for t in range(2):
            body(t, t % 2, t // 2, 128, 128, 128)
        with eng.Fori(1, pairs) as i:
            for par in range(2):
                body(i * 2 + par, par, i, 128, 128, 128)
        for t in range(2 * pairs, FULL + 1):
            body(t, t % 2, t // 2, size(t), size(t + 1), size(t + 2))

    with nc.Block() as block:
        @block.sync
        def _(sp):
            sp.dma_start(base_b[:], io["base_b"].partition_broadcast(128)).then_inc(const_loaded, 16)
            sp.dma_start(rout_b[:], io["router_b"].partition_broadcast(128)).then_inc(const_loaded, 16)
            sp.dma_start(emap[:], io["expert_map"].partition_broadcast(128)).then_inc(const_loaded, 16)

            def load_att(t, par, n):
                wait_count(sp, a_lo, t - 1)
                sp.dma_start(at[:, par, :, 0:n], io["att_dram"].rearrange("(k p) t -> p k t", p=128)[:, :, bass.ds(t * 128, n)]).then_inc(a_loaded[par], 16)

            def load_res(t, par, n):
                sp.dma_start(h2[0:n, par, :], io["h_dram"][bass.ds(t * 128, n), :]).then_inc(r_loaded[par], 16)

            srcs = [io["Wo"][k * 128:(k + 1) * 128, :] for k in range(KC)] + [io["base_WT"][k * 128:(k + 1) * 128, :] for k in range(KC)]
            srcs += [io["ARW"][:, k * KC // 2:(k + 1) * KC // 2, :] for k in range(2)] + [io["BT"]]
            load_att(0, 0, 128)
            load_res(0, 0, 128)
            for k in range(PIECES):
                if k >= RING:
                    sp.wait_ge(lo_split, k - RING + 1)
                dst = stage[:, k % RING, 0:SIZES[k]]
                if len(srcs[k].shape) == 3:
                    dst = dst.rearrange("p (k m) -> p k m", m=ARW)
                sp.dma_start(dst, srcs[k]).then_inc(w_loaded[k % RING], 16)
                if k == 3:
                    load_att(1, 1, 128)
                    load_res(1, 1, 128)

            def body(t, par, half_t, n, n1, n2):
                if n2:
                    load_att(t + 2, par, n2)
                sp.wait_ge(out_ready, t + 1)
                sp.dma_start(io["out"][bass.ds(t * 128, n), :], h2[0:n, par, :]).then_inc(out_stored[par], 16)
                if n2:
                    sp.wait_ge(out_stored[par], 16 * half_t + 16)
                    load_res(t + 2, par, n2)
            visit(sp, body)
            sp.wait_ge(out_stored[0], 16 * ((FULL + 2) // 2))
            sp.wait_ge(out_stored[1], 16 * ((FULL + 1) // 2))

        @block.tensor
        def _(pe):
            def three(bank, n, lhs, w, cols, K, start=True, stop=True):
                for k in range(K):
                    for m, (a, b) in enumerate(((0, 0), (0, 1), (1, 0))):
                        last = nc.tensor.matmul(bank[0:n, 0:cols.stop - cols.start], lhs[a][:, k, 0:n], w[b][:, k, cols],
                                                start=(start and k == 0 and m == 0), stop=(stop and k == K - 1 and m == 2))
                return last

            def attn_out(t, n, first=False):
                pe.wait_ge(a_lo, t + 1)
                wait_count(pe, wo_read, t)
                if first:
                    pe.wait_ge(lo_split, KC)
                three(wo_ps[0], n, aT, wo, slice(0, 512), KC)
                three(wo_ps[1], n, aT, wo, slice(512, 1024), KC).then_inc(wo_done, 1)

            def transpose_x(t, n):
                pe.wait_ge(x_ready, t + 1)
                wait_count(pe, xT_lo, 2 * t)
                for half in range(2):
                    for q in range(4):
                        last = nc.tensor.transpose(x_ps[half][:, 128 * q:128 * q + n], xn[0:n, (4 * half + q) * 128:(4 * half + q + 1) * 128], ident[0:n, 0:n])
                    last.then_inc(xT_done, 1)

            def body(t, par, half_t, n, n1, n2):
                first = isinstance(t, int) and t == 0
                pe.wait_ge(xT_lo, 2 * t + 2)
                if first:
                    pe.wait_ge(lo_split, PIECES)
                wait_count(pe, z_ready, t)
                three(ar_ps, n, xT, war, slice(0, ARW), KC).then_inc(ar_done, 1)
                if n1:
                    attn_out(t + 1, n1)
                wait_count(pe, out_ready, t)
                for half in range(2):
                    last = three(base_ps[half], n, xT, wb, slice(512 * half, 512 * half + 512), KC, stop=False)
                if n1:
                    transpose_x(t + 1, n1)
                pe.wait_ge(z_ready, t + 1)
                nc.tensor.transpose(z_ps[:, 0:n], z[0:n, :], ident[0:n, 0:n]).then_inc(zT_done, 1)
                pe.wait_ge(zT_lo, t + 1)
                zz = [q[:, 0:n].unsqueeze(1) for q in zT]
                for half in range(2):
                    last = three(base_ps[half], n, zz, wB, slice(512 * half, 512 * half + 512), 1, start=False)
                last.then_inc(base_done, 1)
            attn_out(0, 128, first=True)
            transpose_x(0, 128)
            visit(pe, body)

        @block.scalar
        def _(act):
            def x_hi(t, n):
                for half in range(2):
                    act.wait_ge(xT_done, 2 * t + half + 1)
                    src = x_ps[half][:, :].rearrange("p (q t) -> p q t", q=4)[:, :, 0:n]
                    nc.scalar.activation(xT[0][:, 4 * half:4 * half + 4, 0:n], src, ACT.Copy).then_inc(xT_hi, 1)

            def a_split(half_t, t, par, n):
                act.wait_ge(a_loaded[par], 16 * half_t + 16)
                wait_count(act, wo_done, t)
                nc.scalar.activation(aT[0][:, :, 0:n], at[:, par, :, 0:n], ACT.Copy).then_inc(a_hi, 1)

            def body(t, par, half_t, n, n1, n2):
                act.wait_ge(logits_ready, t + 1)
                nc.scalar.activation(ex[0:n], lg[0:n], ACT.Exp, bias=nm[0:n, 0:1], accum_out=dn[0:n, 0:1]).then_inc(exp_ready, 1)
                if n2:
                    a_split(half_t + 1, t + 2, par, n2)
                if n1:
                    x_hi(t + 1, n1)
                act.wait_ge(zT_done, t + 1)
                nc.scalar.activation(zT[0][:, 0:n], z_ps[:, 0:n], ACT.Copy).then_inc(zT_hi, 1)

            for k in range(PIECES):
                act.wait_ge(w_loaded[k % RING], 16 * (k // RING + 1))
                o = slice(OFFS[k], OFFS[k + 1])
                nc.scalar.activation(w_hi[:, o], stage[:, k % RING, 0:SIZES[k]], ACT.Copy).then_inc(hi_split, 1)
                if k == 1:
                    a_split(0, 0, 0, 128)
            a_split(0, 1, 1, 128)
            x_hi(0, 128)
            visit(act, body)

        @block.gpsimd
        def _(pool):
            def add_bias(t, par, n):
                pool.wait_ge(x_ready, t + 1)
                nc.gpsimd.tensor_tensor(h2[0:n, par, :], h2[0:n, par, :], base_b[0:n, :], ALU.add).then_inc(biased, 1)

            def body(t, par, half_t, n, n1, n2):
                if n1:
                    add_bias(t + 1, 1 - par, n1)
            pool.wait_ge(const_loaded, 48)
            add_bias(0, 0, 128)
            visit(pool, body)

        LINKS = (5 + RSQRT_LINKS) + 9

        @block.vector
        def _(dve):
            v = nc.vector

            def residual_ln(t, par, half_t, n, link):
                dve.wait_ge(wo_done, t + 1)
                dve.wait_ge(r_loaded[par], 16 * half_t + 16)
                link.done(v.tensor_tensor(h2[0:n, par, 0:512], wo_ps[0][0:n, :], h2[0:n, par, 0:512], ALU.add))
                v.tensor_tensor(h2[0:n, par, 512:1024], wo_ps[1][0:n, :], h2[0:n, par, 512:1024], ALU.add).then_inc(wo_read, 1)
                dve.wait_ge(wo_read, t + 1)
                link.done(v.bn_stats(stats[0:n, 0, :], h2[0:n, par, 0:512]))
                link.done(v.bn_stats(stats[0:n, 1, :], h2[0:n, par, 512:1024]), apart=True)
                link.done(v.bn_aggr(mv[0:n, :], stats[0:n].rearrange("p a b -> p (a b)")))
                link.done(v.tensor_scalar(veps[0:n], mv[0:n, 1:2], EPS, None, ALU.add))
                rsqrt_newton(nc, link.done, rstd[0:n], veps[0:n], rtmp[0:n])
                wait_count(dve, xT_done, 2 * t)
                v.tensor_scalar(xn[0:n, :], h2[0:n, par, :], mv[0:n, 0:1], rstd[0:n, 0:1], ALU.subtract, ALU.mult).then_inc(x_ready, 1)

            def att_lo(t, par, n):
                dve.wait_ge(a_hi, t + 1)
                v.tensor_tensor(aT[1][:, :, 0:n], at[:, par, :, 0:n], aT[0][:, :, 0:n].bitcast(F32), ALU.subtract).then_inc(a_lo, 1)

            def x_lo(t, n):
                for half in range(2):
                    dve.wait_ge(xT_hi, 2 * t + half + 1)
                    src = x_ps[half][:, :].rearrange("p (q t) -> p q t", q=4)[:, :, 0:n]
                    c = slice(4 * half, 4 * half + 4)
                    v.tensor_tensor(xT[1][:, c, 0:n], src, xT[0][:, c, 0:n].bitcast(F32), ALU.subtract).then_inc(xT_lo, 1)

            def router(t, n, link):
                dve.wait_ge(ar_done, t + 1)
                link.done(v.tensor_tensor(lg[0:n], ar_ps[0:n, ER:ER + ROUTES], rout_b[0:n], ALU.add), apart=True)
                link.done(v.max(m8[0:n], lg[0:n]))
                v.tensor_scalar(nm[0:n], m8[0:n, 0:1], -1.0, None, ALU.mult).then_inc(logits_ready, 1)
                wait_apart(dve, exp_ready, t + 1, setup)
                link.done(v.max(e8[0:n], ex[0:n]), apart=True)
                link.done(v.match_replace(er[0:n], e8[0:n], ex[0:n], 0.0))
                link.done(v.tensor_tensor(er[0:n], ex[0:n], er[0:n], ALU.subtract))
                link.done(v.tensor_tensor(wsel[0:n], er[0:n].unsqueeze(1).to_broadcast((n, EXPERTS, ROUTES)), sel_map[0:n], ALU.mult))
                link.done(v.tensor_reduce(w8[0:n], wsel[0:n], AX.X, ALU.add))
                link.done(v.reciprocal(rd[0:n], dn[0:n]))
                link.done(v.tensor_scalar(rd[0:n], rd[0:n], 2.0, None, ALU.mult))
                wait_count(dve, zT_done, t)
                v.scalar_tensor_tensor(out=z[0:n].rearrange("p (e r) -> p e r", e=EXPERTS),
                                       in0=ar_ps[0:n, 0:ER].rearrange("p (e r) -> p e r", e=EXPERTS), scalar=rd[0:n, 0:1],
                                       in1=w8[0:n].unsqueeze(2).to_broadcast((n, EXPERTS, RANK)), op0=ALU.mult, op1=ALU.mult).then_inc(z_ready, 1)

            def body(t, par, half_t, n, n1, n2):
                link = Chain(dve, chain, LINKS * t + (5 + RSQRT_LINKS), setup)
                router(t, n, link)
                if n1:
                    residual_ln(t + 1, 1 - par, half_t + par, n1, link)
                if n2:
                    att_lo(t + 2, par, n2)
                if n1:
                    x_lo(t + 1, n1)
                dve.wait_ge(zT_hi, t + 1)
                v.tensor_tensor(zT[1][:, 0:n], z_ps[:, 0:n], zT[0][:, 0:n].bitcast(F32), ALU.subtract).then_inc(zT_lo, 1)
                dve.wait_ge(base_done, t + 1)
                dve.wait_ge(biased, t + 1)
                for half in range(2):
                    c = slice(512 * half, 512 * half + 512)
                    last = v.tensor_tensor(h2[0:n, par, c], base_ps[half][0:n, :], h2[0:n, par, c], ALU.add)
                last.then_inc(out_ready, 1)

            first = Chain(dve, setup)
            dve.wait_ge(const_loaded, 48)
            first.done(v.tensor_copy(emapf[:], emap[:]))
            for e in range(EXPERTS):
                last = v.tensor_scalar(sel_map[:, e, :], emapf[:], float(e), None, ALU.is_equal)
            first.done(last)
            for k in range(PIECES):
                dve.wait_ge(hi_split, k + 1)
                o = slice(OFFS[k], OFFS[k + 1])
                v.tensor_tensor(w_lo[:, o], stage[:, k % RING, 0:SIZES[k]], w_hi[:, o].bitcast(F32), ALU.subtract).then_inc(lo_split, 1)
                if k == 1:
                    att_lo(0, 0, 128)
                if k == KC + 2:
                    residual_ln(0, 0, 0, 128, Chain(dve, chain))
            att_lo(1, 1, 128)
            x_lo(0, 128)
            visit(dve, body)


def build(nc, io):
    with ExitStack() as whole:
        W = {"ident": whole.enter_context(nc.sbuf_tensor("ident", [128, 128], F32))}
        with ExitStack() as two:
            for n in ("wq_hi", "wq_lo"):
                W[n] = two.enter_context(nc.sbuf_tensor(n, [128, (KC + 1) * DM], F32R))
            with ExitStack() as ctx:
                mixer_block(nc, ctx, io, W)
            with ExitStack() as ctx:
                attention_block(nc, ctx, io, W)
        with ExitStack() as ctx:
            mlp_block(nc, ctx, io, W)


def constants():
    f = np.float32
    base = 2.0 ** (-2.0 ** (-(math.log2(HEADS) - 3)))
    slopes = (base ** np.arange(1, HEADS + 1, dtype=np.float64)).astype(f)
    hi = (((slopes.view(np.uint32) + np.uint32(0x800)) & np.uint32(0xFFFFF000))).view(f)
    lo = slopes - hi
    rows = np.zeros((4, 16 + 4 * (S + 1)), f)
    for slot in range(2):
        for late in range(2):
            g = slot + 2 * late
            rows[2 * late, slot * GH:(slot + 1) * GH] = hi[g * GH:(g + 1) * GH]
            rows[2 * late + 1, slot * GH:(slot + 1) * GH] = lo[g * GH:(g + 1) * GH]
    pos = np.zeros((2, 2, S + 1), f)
    pos[:, :, :S] = -np.arange(S, dtype=f)
    zero = np.zeros_like(pos[0])
    for late in range(2):
        both = np.stack([pos[0] if late == 0 else zero, pos[0] if late == 1 else zero])
        rows[2 * late:2 * late + 2, 16:] = both.reshape(-1)
    k, p = np.arange(256)[None, :] - 128, np.arange(128)[:, None]
    quarter = np.zeros((128, 3), f)
    quarter[0:64, 0], quarter[0:64, 1], quarter[:, 2] = 0.25, TWO_PI / 4, TWO_PI / 4
    return {
        "bvals": np.broadcast_to(np.arange(128, dtype=f), (128, 128)).copy(),
        "avals": np.broadcast_to(128 * np.arange(AH, dtype=f), (128, AH)).copy(),
        "quarter": quarter,
        "ident": np.eye(128, dtype=f),
        "mask": np.where(k > p, f(1e30), f(0)).astype(f),
        "rows": rows,
    }


def kernel(**inputs):
    import concourse.bacc as bacc
    from concourse.bass_utils import run_bass_kernel_spmd

    g = {k: np.asarray(v) for k, v in inputs.items()}
    x = g["x"]
    arw = np.zeros((DM, 144), np.float32)
    arw[:, 0:ER] = g["L0_ffn_A"].reshape(ER, DM).T
    arw[:, ER:ER + ROUTES] = g["L0_ffn_router_W"].T
    laid = {
        "x_re": x[..., 0].transpose(2, 1, 0),
        "x_im": x[..., 1].transpose(2, 1, 0),
        "txt": g["txt"],
        "log_dt": np.broadcast_to(g["L0_tok_log_dt"], (64, CH)),
        "B_re": g["L0_tok_B"][..., 0].T,
        "B_im": g["L0_tok_B"][..., 1].T,
        "inv_A_real": g["L0_tok_inv_A_real"].T,
        "A_imag": g["L0_tok_A_imag"].T,
        "Wqkv": g["L0_attn_Wqkv"],
        "Wo": g["L0_attn_Wo"],
        "base_WT": g["L0_ffn_base_W"].T,
        "base_b": g["L0_ffn_base_b"],
        "router_b": g["L0_ffn_router_b"],
        "ARW": arw.reshape(KC, 128, 144).transpose(1, 0, 2),
        "BT": g["L0_ffn_B"].transpose(0, 2, 1).reshape(ER, DM),
        "expert_map": g["L0_ffn_expert_map"],
        **constants(),
    }
    nc = bacc.Bacc("TRN2", target_bir_lowering=False, num_devices=1)
    arrays, io = {}, {}
    for name, a in laid.items():
        a = np.ascontiguousarray(a)
        arrays[f"in_{name}"] = a
        io[name] = nc.dram_tensor(f"in_{name}", a.shape, mybir.dt.from_np(a.dtype), kind="ExternalInput").ap()
    io["h_dram"] = nc.dram_tensor("h_dram", (TOK, DM), F32, kind="Internal").ap()
    io["att_dram"] = nc.dram_tensor("att_dram", (DM, TOK), F32, kind="Internal").ap()
    io["out"] = nc.dram_tensor("out_0", (TOK, DM), F32, kind="ExternalOutput").ap()
    build(nc, io)
    r = run_bass_kernel_spmd(nc, [arrays], core_ids=[0])
    return r.results[0]["out_0"].reshape(SEQS, S, DM)
```

```python
import math
from contextlib import ExitStack

import numpy as np

import concourse.bass as bass
from concourse import mybir

F32, F32R, I32 = mybir.dt.float32, mybir.dt.float32r, mybir.dt.int32
ALU, ACT, AX = mybir.AluOpType, mybir.ActivationFunctionType, mybir.AxisListType

SEQS, CH, STATES = 16, 128, 64
TXT, DM = 77, 1024
S = CH + TXT
TOK = SEQS * S
HEADS, HD = 32, 32
KC = DM // 128
EXPERTS, RANK, ROUTES = 8, 16, 15
ER = EXPERTS * RANK
EPS = 1e-5

AH = DM // 128
ROUND = 1.5 * 2.0 ** 23
TWO_PI = 6.28318
HCH = 16
MIX_STEPS = CH // HCH

PAIRS = SEQS // 2
PT = 2 * S
SLOTS = 10
BANKS = 3
BANK_USES = 18
GH = 8
UNITS = 8
TILES = [(0, 0, CH), (0, CH, TXT), (1, 0, CH), (1, CH, TXT)]

FULL = TOK // 128
REST = TOK - FULL * 128
RSQRT_GUESS = float(0x5F3759DF)
NEWTON = 3


def wait_count(eng, sem, count):
    if isinstance(count, int) and count <= 0:
        return
    eng.wait_ge(sem, count)


def wait_apart(eng, sem, count, met, met_count=1):
    if isinstance(count, int):
        wait_count(eng, sem, count)
        return
    value = eng.to_reg(count)
    eng.wait_ge(met, met_count)
    eng.wait_ge(sem, value)


class Chain:

    def __init__(self, eng, sem, base=0, met=None):
        self.eng, self.sem, self.base, self.n, self.met = eng, sem, base, 0, met

    def issued(self, ins):
        self.n += 1
        ins.then_inc(self.sem, 1)

    def wait(self, apart=False):
        if apart:
            wait_apart(self.eng, self.sem, self.base + self.n, self.met)
        else:
            self.eng.wait_ge(self.sem, self.base + self.n)

    def done(self, ins, apart=False):
        self.n += 1
        ins.then_inc(self.sem, 1)
        if apart:
            wait_apart(self.eng, self.sem, self.base + self.n, self.met)
        else:
            self.eng.wait_ge(self.sem, self.base + self.n)


RSQRT_LINKS = 1 + 3 * NEWTON


def rsqrt_step(nc, k, y, v, t):
    if k == 0:
        return nc.vector.tensor_scalar(y.bitcast(I32), v.bitcast(I32), -0.5, RSQRT_GUESS, ALU.mult, ALU.add)
    if k % 3 == 1:
        return nc.vector.tensor_tensor(t, y, y, ALU.mult)
    if k % 3 == 2:
        return nc.vector.scalar_tensor_tensor(out=t, in0=t, scalar=-0.5, in1=v, op0=ALU.mult, op1=ALU.mult)
    return nc.vector.scalar_tensor_tensor(out=y, in0=t, scalar=1.5, in1=y, op0=ALU.add, op1=ALU.mult)


def rsqrt_newton(nc, link, y, v, t):
    for k in range(RSQRT_LINKS):
        link(rsqrt_step(nc, k, y, v, t))


def exp_exact(nc, link, y, x, n, r):
    v = nc.vector
    link(v.tensor_scalar(n, x, 1.0 / math.log(2.0), ROUND, ALU.mult, ALU.add))
    link(v.tensor_scalar(n, n, ROUND, None, ALU.subtract))
    link(v.scalar_tensor_tensor(out=r, in0=n, scalar=-0.693359375, in1=x, op0=ALU.mult, op1=ALU.add))
    link(v.scalar_tensor_tensor(out=r, in0=n, scalar=0.693359375 - math.log(2.0), in1=r, op0=ALU.mult, op1=ALU.add))
    link(v.tensor_scalar(y, r, 1.0 / 5040, None, ALU.mult))
    for k in (6, 5, 4, 3, 2, 1):
        link(v.scalar_tensor_tensor(out=y, in0=y, scalar=1.0 / math.factorial(k), in1=r, op0=ALU.add, op1=ALU.mult))
    link(v.tensor_scalar(n.bitcast(I32), n, 2.0 ** 23, 127 * 2.0 ** 23, ALU.mult, ALU.add))
    link(v.scalar_tensor_tensor(out=y, in0=y, scalar=1.0, in1=n, op0=ALU.add, op1=ALU.mult))


def mixer_block(nc, ctx, io, W):
    def sb(name, shape, dt=F32):
        return ctx.enter_context(nc.sbuf_tensor(name, shape, dt))

    def sem(name):
        return ctx.enter_context(nc.semaphore(name))

    xre, xim = sb("xre", [128, CH, SEQS]), sb("xim", [128, CH, SEQS])
    par = sb("par", [128, 5, CH])
    bvals, avals, quarter = sb("bvals", [128, 128]), sb("avals", [128, AH]), sb("quarter", [128, 3])
    small = sb("small", [128, 16, CH])
    tab = sb("tab", [128, 6, CH, AH])
    G1, G2 = tab[:, 4], tab[:, 5]
    turn_b, frac_b, mag_b = sb("turn_b", [128, HCH, 128]), sb("frac_b", [128, HCH, 128]), sb("mag_b", [128, HCH, 128])
    Qt, X = sb("Qt", [128, 2, HCH, 128]), sb("X", [128, 2, HCH, SEQS, AH])
    X2 = sb("X2", [128, HCH, SEQS, AH])
    Y = sb("Y", [128, HCH, 128])
    stage = sb("w_stage", [128, 2, DM])
    ps = [ctx.enter_context(nc.psum_tensor(f"mix_ps{i}", [128, 4, 128], F32)) for i in range(HCH // 4)]

    loaded, txt_copied = sem("mix_loaded"), sem("txt_copied")
    w_loaded = [sem("w_loaded0"), sem("w_loaded1")]
    w_hi, w_lo = sem("w_hi"), sem("w_lo")
    chain, act_chain, pool_chain = sem("mix_dve_chain"), sem("mix_act_chain"), sem("mix_pool_chain")
    re_ready, tanh_ready = sem("re_ready"), sem("tanh_ready")
    ph_ready, sin_ready, tab_ready = sem("ph_ready"), sem("sin_ready"), sem("tab_ready")
    turns_ready, frac_ready, wave_ready = sem("turns_ready"), sem("frac_ready"), sem("wave_ready")
    q_ready, x2_ready, x_ready = sem("q_ready"), sem("x2_ready"), sem("x_ready")
    mix_done, y_copied = sem("mix_done"), sem("y_copied")
    y_stored = sem("y_stored")

    LDT, BRE, BIM, IAR, AIM = (par[:, i] for i in range(5))
    DT, ARE, RE, TURNS, TH, F_D, SIN1, SIN2, T0, T1, T2, T3, DRE, DIM_, INV, T4 = (small[:, i] for i in range(16))
    PIECES = KC + 1
    h_rows = io["h_dram"].rearrange("(c s) (a b) -> c a s b", s=S, b=128)

    def piece(dst, k):
        return dst[:, k * DM:(k + 1) * DM]

    with nc.Block() as block:
        @block.sync
        def _(sp):
            for half in (slice(0, 64), slice(64, 128)):
                for i, name in enumerate(("log_dt", "B_re", "B_im", "inv_A_real", "A_imag")):
                    sp.dma_start(par[half, i, :], io[name]).then_inc(loaded, 16)
                sp.dma_start(xre[half], io["x_re"]).then_inc(loaded, 16)
                sp.dma_start(xim[half], io["x_im"]).then_inc(loaded, 16)
            sp.dma_start(bvals[:], io["bvals"]).then_inc(loaded, 16)
            sp.dma_start(avals[:], io["avals"]).then_inc(loaded, 16)
            sp.dma_start(quarter[:], io["quarter"]).then_inc(loaded, 16)
            sp.dma_start(W["ident"][:], io["ident"]).then_inc(loaded, 16)
            sp.dma_start(io["h_dram"].rearrange("(c s) d -> c s d", s=S)[:, CH:S, :], io["txt"]).then_inc(txt_copied, 16)

            def load_piece(k):
                if k >= 2:
                    sp.wait_ge(w_lo, k - 1)
                if k < KC:
                    sp.dma_start(stage[:, k % 2, :], io["Wqkv"][k * 128:(k + 1) * 128, 0:DM]).then_inc(w_loaded[k % 2], 64)
                else:
                    kv = stage[:, k % 2, :].rearrange("p (k m) -> p k m", m=128)
                    src = io["Wqkv"][:, DM:DM + 2 * HD].rearrange("(k p) m -> p k m", p=128)
                    for q in range(4):
                        sp.dma_start(kv[:, :, q * HD:(q + 1) * HD],
                                     src[:, :, (q // 3) * HD:(q // 3 + 1) * HD]).then_inc(w_loaded[k % 2], 16)

            load_piece(0)
            load_piece(1)
            for step in range(MIX_STEPS):
                if step + 2 < PIECES:
                    load_piece(step + 2)
                sp.wait_ge(y_copied, step + 1)
                for c in range(SEQS):
                    sp.dma_start(h_rows[c][:, step * HCH:(step + 1) * HCH, :],
                                 Y[c * AH:(c + 1) * AH]).then_inc(y_stored, 16)
            sp.wait_ge(y_stored, 16 * SEQS * MIX_STEPS)
            sp.wait_ge(txt_copied, 16)

        LOADS = 18

        @block.scalar
        def _(act):
            act.wait_ge(loaded, 16 * LOADS)
            act.wait_ge(re_ready, 1)
            nc.scalar.activation(TH, RE, ACT.Tanh, scale=0.5).then_inc(tanh_ready, 1)
            act.wait_ge(ph_ready, 1)
            nc.scalar.activation(SIN1, F_D, ACT.Sin, scale=-TWO_PI / 2).then_inc(sin_ready, 1)
            nc.scalar.activation(SIN2, F_D, ACT.Sin, scale=-TWO_PI).then_inc(sin_ready, 1)
            act.wait_ge(ph_ready, 3)
            nc.scalar.activation(tab[:, 1], tab[:, 1], ACT.Sin, scale=-TWO_PI, bias=quarter[:, 2:3]).then_inc(sin_ready, 1)
            nc.scalar.activation(tab[:, 2], tab[:, 2], ACT.Sin, scale=-TWO_PI).then_inc(sin_ready, 1)
            nc.scalar.activation(tab[:, 3], tab[:, 3], ACT.Exp).then_inc(sin_ready, 1)

            def split_hi(k):
                act.wait_ge(w_loaded[k % 2], 64 * (k // 2 + 1))
                nc.scalar.activation(piece(W["wq_hi"], k), stage[:, k % 2, :], ACT.Copy).then_inc(w_hi, 1)

            def copy_out(step):
                if step >= 1:
                    act.wait_ge(y_stored, 16 * SEQS * step)
                for q in range(HCH // 4):
                    act.wait_ge(mix_done, step * (HCH // 4) + q + 1)
                    last = nc.scalar.activation(Y[:, 4 * q:4 * q + 4, :], ps[q][:], ACT.Copy)
                last.then_inc(y_copied, 1)

            for step in range(MIX_STEPS):
                if step >= 1:
                    act.wait_ge(q_ready, step)
                for j in range(HCH):
                    h = step * HCH + j
                    last = nc.scalar.activation(mag_b[:, j, :], bvals[:], ACT.Exp, scale=RE[:, h:h + 1])
                last.then_inc(act_chain, 1)
                act.wait_ge(frac_ready, step + 1)
                nc.scalar.activation(frac_b[:], frac_b[:], ACT.Sin, scale=-TWO_PI, bias=quarter[:, 1:2]).then_inc(wave_ready, 1)
                split_hi(step)
                if step >= 1:
                    copy_out(step - 1)
            copy_out(MIX_STEPS - 1)
            split_hi(PIECES - 1)

        @block.gpsimd
        def _(pool):
            pool.wait_ge(tab_ready, 2)
            for step in range(MIX_STEPS):
                hs = slice(step * HCH, (step + 1) * HCH)
                if step >= 1:
                    pool.wait_ge(frac_ready, step)
                nc.gpsimd.tensor_tensor(turn_b[:], TURNS[:, hs].unsqueeze(2).to_broadcast((128, HCH, 128)),
                                        bvals[:].unsqueeze(1).to_broadcast((128, HCH, 128)), ALU.mult).then_inc(turns_ready, 1)
                if step >= 1:
                    pool.wait_ge(x_ready, step)
                for j in range(HCH):
                    h = step * HCH + j
                    last = nc.gpsimd.tensor_tensor(X2[:, j], xim[:, h, :].unsqueeze(2).to_broadcast((128, SEQS, AH)),
                                                   G2[:, h, :].unsqueeze(1).to_broadcast((128, SEQS, AH)), ALU.mult)
                last.then_inc(x2_ready, 1)
                pool.wait_ge(w_hi, step + 1)
                nc.gpsimd.tensor_tensor(piece(W["wq_lo"], step), stage[:, step % 2, :],
                                        piece(W["wq_hi"], step).bitcast(F32), ALU.subtract).then_inc(w_lo, 1)
            pool.wait_ge(w_hi, PIECES)
            k = PIECES - 1
            nc.gpsimd.tensor_tensor(piece(W["wq_lo"], k), stage[:, k % 2, :],
                                    piece(W["wq_hi"], k).bitcast(F32), ALU.subtract).then_inc(w_lo, 1)
            pool.wait_ge(w_lo, PIECES)

        @block.vector
        def _(dve):
            link = Chain(dve, chain).done
            v = nc.vector
            dve.wait_ge(loaded, 16 * LOADS)
            exp_exact(nc, link, DT, LDT, T0, T1)
            exp_exact(nc, link, ARE, IAR, T0, T1)
            link(v.tensor_scalar(ARE, ARE, -1.0, None, ALU.mult))
            v.tensor_tensor(RE, ARE, DT, ALU.mult).then_inc(re_ready, 1)
            link(v.tensor_tensor(TURNS, AIM, DT, ALU.mult))
            link(v.tensor_scalar(TURNS, TURNS, 1.0 / (2.0 * math.pi), None, ALU.mult))
            link(v.tensor_scalar(F_D, TURNS, ROUND, None, ALU.add))
            v.scalar_tensor_tensor(out=F_D, in0=F_D, scalar=ROUND, in1=TURNS, op0=ALU.subtract, op1=ALU.subtract).then_inc(ph_ready, 1)
            tb, ab = TURNS.unsqueeze(2).to_broadcast((128, CH, AH)), avals[:].unsqueeze(1).to_broadcast((128, CH, AH))
            link(v.tensor_tensor(tab[:, 0], tb, ab, ALU.mult))
            link(v.tensor_scalar(tab[:, 1], tab[:, 0], 0.25, ROUND, ALU.add, ALU.add))
            link(v.tensor_scalar(tab[:, 2], tab[:, 0], ROUND, None, ALU.add))
            v.scalar_tensor_tensor(out=tab[:, 1], in0=tab[:, 1], scalar=ROUND, in1=tab[:, 0], op0=ALU.subtract, op1=ALU.subtract).then_inc(ph_ready, 1)
            dve.wait_ge(re_ready, 1)
            link(v.tensor_tensor(tab[:, 3], RE.unsqueeze(2).to_broadcast((128, CH, AH)), ab, ALU.mult))
            v.scalar_tensor_tensor(out=tab[:, 2], in0=tab[:, 2], scalar=ROUND, in1=tab[:, 0], op0=ALU.subtract, op1=ALU.subtract).then_inc(ph_ready, 1)
            dve.wait_ge(tanh_ready, 1)
            link(v.tensor_scalar(T0, TH, -1.0, 1.0, ALU.mult, ALU.add))
            link(v.reciprocal(T0, T0))
            link(v.scalar_tensor_tensor(out=T0, in0=TH, scalar=2.0, in1=T0, op0=ALU.mult, op1=ALU.mult))
            link(v.tensor_scalar(T1, T0, 1.0, None, ALU.add))
            dve.wait_ge(sin_ready, 2)
            link(v.tensor_tensor(T2, SIN1, SIN1, ALU.mult))
            link(v.scalar_tensor_tensor(out=T2, in0=T2, scalar=-2.0, in1=T1, op0=ALU.mult, op1=ALU.mult))
            link(v.tensor_tensor(T0, T0, T2, ALU.add))
            link(v.tensor_tensor(T1, T1, SIN2, ALU.mult))
            link(v.tensor_tensor(T2, ARE, ARE, ALU.mult))
            link(v.tensor_tensor(T3, AIM, AIM, ALU.mult))
            link(v.tensor_tensor(T2, T2, T3, ALU.add))
            link(v.reciprocal(INV, T2))
            link(v.tensor_scalar(INV, INV, 2.0, None, ALU.mult))
            link(v.tensor_tensor(T2, T0, ARE, ALU.mult))
            link(v.tensor_tensor(T3, T1, AIM, ALU.mult))
            link(v.tensor_tensor(T2, T2, T3, ALU.add))
            link(v.tensor_tensor(T3, T1, ARE, ALU.mult))
            link(v.tensor_tensor(T4, T0, AIM, ALU.mult))
            link(v.tensor_tensor(T3, T3, T4, ALU.subtract))
            link(v.tensor_tensor(T2, T2, INV, ALU.mult))
            link(v.tensor_tensor(T3, T3, INV, ALU.mult))
            link(v.tensor_tensor(T0, BRE, T2, ALU.mult))
            link(v.tensor_tensor(T1, BIM, T3, ALU.mult))
            link(v.tensor_tensor(DRE, T0, T1, ALU.subtract))
            link(v.tensor_tensor(T0, BRE, T3, ALU.mult))
            link(v.tensor_tensor(T1, BIM, T2, ALU.mult))
            link(v.tensor_tensor(DIM_, T0, T1, ALU.add))
            dve.wait_ge(sin_ready, 5)
            ta, tb2 = (X2[:, 8 * i:8 * i + 8].rearrange("p h c a -> p (h c a)").rearrange("p (h a) -> p h a", a=AH) for i in range(2))
            dre, dim = (z.unsqueeze(2).to_broadcast((128, CH, AH)) for z in (DRE, DIM_))
            link(v.tensor_tensor(tab[:, 1], tab[:, 1], tab[:, 3], ALU.mult))
            link(v.tensor_tensor(tab[:, 2], tab[:, 2], tab[:, 3], ALU.mult))
            link(v.tensor_tensor(ta, dre, tab[:, 1], ALU.mult))
            link(v.tensor_tensor(tb2, dim, tab[:, 2], ALU.mult))
            link(v.tensor_tensor(tab[:, 0], ta, tb2, ALU.subtract))
            link(v.tensor_tensor(ta, dre, tab[:, 2], ALU.mult))
            link(v.tensor_tensor(tb2, dim, tab[:, 1], ALU.mult))
            link(v.tensor_tensor(tab[:, 3], ta, tb2, ALU.add))
            top, low = slice(0, 64), slice(64, 128)
            v.tensor_copy(tab[top, 4], tab[top, 0]).then_inc(chain, 1)
            v.tensor_scalar(tab[low, 4], tab[low, 3], -1.0, None, ALU.mult).then_inc(chain, 1)
            v.tensor_scalar(tab[top, 5], tab[top, 3], -1.0, None, ALU.mult).then_inc(tab_ready, 1)
            v.tensor_scalar(tab[low, 5], tab[low, 0], -1.0, None, ALU.mult).then_inc(tab_ready, 1)
            dve.wait_ge(tab_ready, 2)
            steps = Chain(dve, sem("mix_step_chain"))
            for step in range(MIX_STEPS):
                par2 = step % 2
                dve.wait_ge(turns_ready, step + 1)
                if step >= 1:
                    dve.wait_ge(q_ready, step)
                steps.done(v.tensor_scalar(frac_b[:], turn_b[:], quarter[:, 0:1], ROUND, ALU.add, ALU.add))
                v.scalar_tensor_tensor(out=frac_b[:], in0=frac_b[:], scalar=ROUND, in1=turn_b[:],
                                       op0=ALU.subtract, op1=ALU.subtract).then_inc(frac_ready, 1)
                if step >= 2:
                    dve.wait_ge(mix_done, (step - 1) * (HCH // 4))
                for j in range(HCH):
                    h = step * HCH + j
                    last = v.tensor_tensor(X[:, par2, j], xre[:, h, :].unsqueeze(2).to_broadcast((128, SEQS, AH)),
                                           G1[:, h, :].unsqueeze(1).to_broadcast((128, SEQS, AH)), ALU.mult)
                steps.done(last)
                dve.wait_ge(x2_ready, step + 1)
                v.tensor_tensor(X[:, par2], X[:, par2], X2[:], ALU.add).then_inc(x_ready, 1)
                dve.wait_ge(wave_ready, step + 1)
                dve.wait_ge(act_chain, step + 1)
                v.tensor_tensor(Qt[:, par2], frac_b[:], mag_b[:], ALU.mult).then_inc(q_ready, 1)

        @block.tensor
        def _(pe):
            for step in range(MIX_STEPS):
                pe.wait_ge(x_ready, step + 1)
                pe.wait_ge(q_ready, step + 1)
                if step >= 1:
                    pe.wait_ge(y_copied, step)
                for j in range(HCH):
                    last = nc.tensor.matmul(ps[j // 4][:, j % 4, :], X[:, step % 2, j].rearrange("p c a -> p (c a)"),
                                            Qt[:, step % 2, j, :], start=True, stop=True)
                    if j % 4 == 3:
                        last.then_inc(mix_done, 1)


def attention_block(nc, ctx, io, W):
    def sb(name, shape, dt=F32):
        return ctx.enter_context(nc.sbuf_tensor(name, shape, dt))

    def pb(name, shape):
        return ctx.enter_context(nc.psum_tensor(name, shape, F32))

    def sem(name):
        return ctx.enter_context(nc.semaphore(name))

    ident = W["ident"]
    wq = [W["wq_hi"][:, 0:KC * DM].rearrange("p (k m) -> p k m", k=KC), W["wq_lo"][:, 0:KC * DM].rearrange("p (k m) -> p k m", k=KC)]
    wkv = [w[:, KC * DM:(KC + 1) * DM].rearrange("p (k m) -> p k m", k=KC) for w in (W["wq_hi"], W["wq_lo"])]
    ht = sb("ht", [128, 4, DM])
    stats, mv = sb("stats", [128, 4, 2, 6]), sb("mv", [128, 4, 2])
    rstd, rtmp, veps = sb("rstd", [128, 4]), sb("rtmp", [128, 4]), sb("veps", [128, 4])
    xT = [sb("xT_hi", [128, KC, PT], F32R), sb("xT_lo", [128, KC, PT], F32R)]
    q_hi, q_lo = sb("q_hi", [128, 2, PT], F32R), sb("q_lo", [128, 2, PT], F32R)
    QR = 3 * HD + 4
    Qs = sb("Qs", [128, 2, GH, PT], F32R)
    Ks = sb("Ks", [128, 2, 2, S + 1], F32R)
    crow = sb("crow", [128, 16 + 4 * (S + 1)])
    vT = sb("vT", [128, PT])
    V0, V1 = sb("V0", [128, 2, HD]), sb("V1", [128, 2, HD])
    mask = sb("mask", [128, 2 * 128])
    P = sb("P", [128, 2, GH, CH + S])
    nmax, den, rden = (sb(n, [128, 2, 2, 2, 4]) for n in ("nmax", "den", "rden"))
    PTR = sb("PTR", [128, 2, GH, S + TXT])
    PT0, PT1 = PTR[:, :, :, 0:S], PTR[:, :, :, S:S + TXT]
    att = sb("att", [128, 2, 2, S])

    sc = [pb(f"sc{i}", [128, 512]) for i in range(2)]
    pt = [pb(f"pt{i}", [128, 512]) for i in range(2)]
    av = pb("av", [128, 512])
    pr = [pb(f"pr{i}", [128, 512]) for i in range(BANKS)]

    const_loaded, const_ready = sem("att_const_loaded"), sem("att_const_ready")
    h_loaded = [sem(f"h_loaded{i}") for i in range(4)]
    chain = sem("att_dve_chain")
    xn_ready = sem("xn_ready")
    proj_done, hi_written, bank_read = sem("proj_done"), sem("hi_written"), sem("bank_read")
    q_stacked = [sem("q_stacked0"), sem("q_stacked1")]
    scores_done, scores_biased, exp_done = sem("scores_done"), sem("scores_biased"), sem("exp_done")
    recip_done, probs_ready = sem("recip_done"), sem("probs_ready")
    transposed, pT_copied = sem("transposed"), sem("pT_copied")
    av_done, att_copied = sem("av_done"), sem("att_copied")
    att_stored = [sem("att_stored0"), sem("att_stored1")]
    wo_loaded = [sem(f"wo_loaded{i}") for i in range(KC + 1)]
    wo_hi, wo_lo = sem("wo_hi"), sem("wo_lo")

    SCALE = HD ** -0.5
    STACKS = 3
    MAIN = ["ln", ("q", 0), ("q", 1), "kv", ("q", 2), ("q", 3), ("q", 4), ("q", 5), ("q", 6), ("q", 7)]
    USE = {0: 8, 1: 9, 2: 11, 3: 12, 4: 14, 5: 15, 6: 16, 7: 17}
    KV_USE, VT_USE = 10, 13
    V_SLOT = 6
    LN_HI_AFTER, LN_LO_AFTER = 1, 2
    SCORE_SLOT = [5, 6, 7, 8, 9, 11, 12, 13]

    def hi_count(use):
        return use + 1 if use < VT_USE else use

    def att_unit(slot, lag):
        for back in range(2):
            if slot + back * SLOTS - lag in SCORE_SLOT:
                return back, SCORE_SLOT.index(slot + back * SLOTS - lag)
        return None

    WO_PIECES = KC + 1
    SPLIT_AT = [1, 2, 3, 4] + [32, 33, 34, 35, 44]
    LO_AFTER = 2

    def wo_piece(last, slot, i, after=0):
        turn = GH * slot + i - after
        return SPLIT_AT.index(turn) if last is None and turn in SPLIT_AT else None

    def part_of(w, k):
        return w[:, k * DM:(k + 1) * DM]

    def visit(body):
        def run(eng):
            body(0, True, False)
            with eng.Fori(1, PAIRS - 1) as p:
                body(p, False, False)
            body(PAIRS - 1, False, True)
            body(PAIRS, False, None)
        return run

    def slots(p, first, last):
        for slot in range(SLOTS):
            def unit(lag, slot=slot):
                found = att_unit(slot, lag)
                if found is None:
                    return None
                back, j = found
                if (back and first) or (not back and last is None):
                    return None
                return (p - back, j)
            yield slot, (MAIN[slot] if last is not None else None), unit(0), unit(1), unit(2)

    with nc.Block() as block:
        @block.sync
        def _(sp):
            sp.dma_start(mask[:], io["mask"]).then_inc(const_loaded, 16)
            sp.dma_start(crow[96:100, :], io["rows"]).then_inc(const_loaded, 16)

            def load_h(p, s):
                c, t0, n = TILES[s]
                r0 = p * PT + (c * S + t0)
                sp.dma_start(ht[0:n, s, :], io["h_dram"][bass.ds(r0, n), :]).then_inc(h_loaded[s], 16)

            def stack_q(p, k):
                g, r = k // 2, k % 2
                wait_apart(sp, bank_read, BANK_USES * p + USE[k] + 1, const_loaded, 32)
                wait_count(sp, scores_done, 64 * p + 16 * g - 16)
                for row, src in ((0, q_hi), (HD, q_hi), (2 * HD, q_lo)):
                    sp.dma_start(Qs[row:row + HD, g % 2, 4 * r:4 * r + 4, :].bitcast(F32),
                                 src[:, r, :].bitcast(F32)).then_inc(q_stacked[r], 16)

            def store_att(p, j):
                g, b = j // 2, j % 2
                sp.wait_ge(att_copied, 8 * p + j + 1)
                dst = io["att_dram"].rearrange("(k p) t -> p k t", p=128)[:, 2 * g:2 * g + 2, bass.ds(p * PT + b * S, S)]
                sp.dma_start(dst, att[:, b, :, :]).then_inc(att_stored[b], 16)

            def load_wo(k):
                src = io["Wo"][k * 128:(k + 1) * 128, :] if k < KC else io["BT"]
                sp.dma_start(ht[:, k % 4, :], src).then_inc(wo_loaded[k], 16)

            def body(p, first, last):
                for slot, main, sj, tj, aj in slots(p, first, last):
                    if last is None and slot == 1:
                        for k in range(4, 8):
                            sp.wait_ge(wo_lo, k - 3)
                            load_wo(k)
                    if last is None and slot == 2:
                        for q in att_stored:
                            sp.wait_ge(q, 16 * UNITS // 2)
                        for t in range(2):
                            sp.dma_start(W["at"][:, t], io["att_dram"].rearrange("(k p) t -> p k t", p=128)[:, :, t * 128:(t + 1) * 128]).then_inc(W["a_loaded"][t], 16)
                    if last is None and slot == 5:
                        sp.wait_ge(wo_lo, 5)
                        load_wo(8)
                    if slot == 1 and last is True:
                        for k in range(4):
                            sp.wait_ge(proj_done, BANK_USES * p + 4 + k + 1)
                            load_wo(k)
                    if main is not None and slot >= 1 and isinstance(MAIN[slot - 1], tuple):
                        stack_q(p, MAIN[slot - 1][1])
                    if slot == 0 and not first:
                        stack_q(p - 1, 7)
                    if slot == 1 and last is False:
                        for s in range(4):
                            sp.wait_ge(proj_done, BANK_USES * p + 4 + s + 1)
                            load_h(p + 1, s)
                    if aj is not None:
                        store_att(*aj)
            for s in range(4):
                load_h(0, s)
            visit(body)(sp)
            for s in att_stored:
                sp.wait_ge(s, 16 * PAIRS * UNITS // 2)
            for s in W["a_loaded"]:
                sp.wait_ge(s, 16)

        @block.tensor
        def _(pe):
            def scores(p, j, i):
                g, b = j // 2, j % 2
                if i == 0:
                    for q in q_stacked:
                        pe.wait_ge(q, 16 * STACKS * (4 * p + g + 1))
                    if j == 0:
                        pe.wait_ge(bank_read, BANK_USES * p + KV_USE + 1)
                n = 64 * p + 8 * j + i
                wait_count(pe, scores_biased, n - 1)
                bank, q = sc[i % 2], Qs[0:QR, g % 2, i, b * S:(b + 1) * S]
                nc.tensor.matmul(bank[:, 0:CH], q[:, 0:CH], Ks[0:QR, g // 2, b, 0:CH], start=True, stop=True)
                nc.tensor.matmul(bank[0:TXT, CH:CH + S + 1], q[:, CH:S], Ks[0:QR, g // 2, b, :],
                                 start=True, stop=True).then_inc(scores_done, 1)

            def turn(p, j, i):
                if i % 4 == 0:
                    pe.wait_ge(probs_ready, 16 * p + 2 * j + i // 4 + 1)
                wait_count(pe, pT_copied, 64 * p + 8 * j + i - 1)
                bank, src = pt[i % 2], P[:, j % 2, i, :]
                nc.tensor.transpose(bank[:, 0:CH], src[:, 0:CH], ident[:])
                nc.tensor.transpose(bank[:, CH:S], src[0:TXT, CH:2 * CH], ident[0:TXT, 0:TXT])
                nc.tensor.transpose(bank[0:TXT, S:S + TXT], src[0:TXT, 2 * CH:CH + S],
                                    ident[0:TXT, 0:TXT]).then_inc(transposed, 1)

            def values(p, j):
                b, o = j % 2, av
                pe.wait_ge(pT_copied, 64 * p + 8 * (j + 1))
                wait_count(pe, att_copied, 8 * p + j)
                if j == 0:
                    pe.wait_ge(bank_read, BANK_USES * p + VT_USE + 1)
                for q in range(4):
                    rows = slice(32 * q, 32 * q + 32)
                    nc.tensor.matmul(o[rows, 0:2 * S], V0[:, b, :], PT0[:, j % 2, q:q + 5:4, :], start=True, stop=False)
                for q in range(4):
                    rows = slice(32 * q, 32 * q + 32)
                    last = nc.tensor.matmul(o[rows, 0:2 * S].rearrange("p (c t) -> p c t", c=2)[:, :, CH:S],
                                            V1[0:TXT, b, :], PT1[0:TXT, j % 2, q:q + 5:4, :], start=False, stop=True)
                last.then_inc(av_done, 1)

            def three(out, w, cols, i):
                for m, (a, x) in enumerate(((0, 0), (0, 1), (1, 0))):
                    last = nc.tensor.matmul(out, w[a][:, i, cols], xT[x][:, i, :], start=(i == 0 and m == 0),
                                            stop=(i == KC - 1 and m == 2))
                return last

            def main_step(p, slot, what, i):
                if what == "ln":
                    wait_count(pe, bank_read, BANK_USES * p + i - BANKS + 1)
                    s, half = i % 4, i // 4
                    if half == 0:
                        pe.wait_ge(xn_ready, 4 * p + s + 1)
                    n = TILES[s][2]
                    for q in range(4):
                        last = nc.tensor.transpose(pr[i % BANKS][:, 128 * q:128 * q + n],
                                                   ht[0:n, s, (4 * half + q) * 128:(4 * half + q + 1) * 128], ident[0:n, 0:n])
                    last.then_inc(proj_done, 1)
                    return
                use = KV_USE if what == "kv" else USE[what[1]]
                if i == 0:
                    if slot == V_SLOT:
                        wait_apart(pe, bank_read, BANK_USES * p + VT_USE - BANKS + 1, const_ready)
                        for c in range(2):
                            nc.tensor.transpose(pr[VT_USE % BANKS][:, 64 * c:64 * c + HD], vT[96:128, c * S:c * S + CH], ident[96:128, 96:128])
                            last = nc.tensor.transpose(pr[VT_USE % BANKS][0:TXT, 64 * c + HD:64 * c + 2 * HD],
                                                       vT[96:128, c * S + CH:(c + 1) * S], ident[96:128, 96:128])
                        last.then_inc(proj_done, 1)
                    pe.wait_ge(bank_read, BANK_USES * p + use - BANKS + 1)
                if i == KC // 2 and what == ("q", 0):
                    pe.wait_ge(bank_read, BANK_USES * p + 8)
                if what == "kv":
                    last = three(pr[use % BANKS][:, 0:PT], wkv, slice(0, 128), i)
                else:
                    last = three(pr[use % BANKS][:, 0:PT], wq, slice(128 * what[1], 128 * what[1] + 128), i)
                if i == KC - 1:
                    last.then_inc(proj_done, 1)

            def body(p, first, last):
                for slot, main, sj, tj, aj in slots(p, first, last):
                    for i in range(GH):
                        if sj is not None:
                            scores(*sj, i)
                        if main is not None:
                            main_step(p, slot, main, i)
                        turning = tj if i >= 4 else aj
                        if turning is not None:
                            turn(*turning, (i + 4) % GH)
                        if i == 5 and aj is not None:
                            values(*aj)
            pe.wait_ge(const_ready, 1)
            visit(body)(pe)

        @block.scalar
        def _(act):
            def exp_head(p, j, i):
                act.wait_ge(scores_biased, 64 * p + 8 * j + i + 1)
                for t, (rows, cols) in enumerate(((slice(0, CH), slice(0, CH)), (slice(0, TXT), slice(CH, CH + S)))):
                    at = (rows, j % 2, i // 4, t, slice(i % 4, i % 4 + 1))
                    last = nc.scalar.activation(P[rows, j % 2, i, cols], P[rows, j % 2, i, cols], ACT.Exp, scale=-1.0,
                                                bias=nmax[at], accum_out=den[at])
                last.then_inc(exp_done, 1)

            def hi_part(p, slot, i):
                what = MAIN[slot]
                if what == "ln":
                    s, half = i % 4, i // 4
                    c, t0, n = TILES[s]
                    act.wait_ge(proj_done, BANK_USES * p + i + 1)
                    src = pr[i % BANKS][:, :].rearrange("p (q t) -> p q t", q=4)[:, :, 0:n]
                    nc.scalar.activation(xT[0][:, 4 * half:4 * half + 4, c * S + t0:c * S + t0 + n], src, ACT.Copy).then_inc(hi_written, 1)
                elif what == "kv":
                    act.wait_ge(proj_done, BANK_USES * p + KV_USE + 1)
                    wait_count(act, scores_done, 64 * p)
                    src = pr[KV_USE % BANKS]
                    for v in range(2):
                        nc.scalar.activation(Ks[0:96, v, :, 0:S], src[0:96, 0:PT].rearrange("p (b t) -> p b t", b=2), ACT.Copy)
                    nc.scalar.activation(vT[96:128, :], src[96:128, 0:PT], ACT.Copy).then_inc(hi_written, 1)
                else:
                    k = what[1]
                    act.wait_ge(proj_done, BANK_USES * p + USE[k] + 1)
                    wait_count(act, q_stacked[k % 2], 16 * STACKS * (4 * p + k // 2))
                    nc.scalar.activation(q_hi[:, k % 2, :], pr[USE[k] % BANKS][:, 0:PT], ACT.Copy, scale=-SCALE).then_inc(hi_written, 1)

            def body(p, first, last):
                for slot, main, sj, tj, aj in slots(p, first, last):
                    for i in range(GH):
                        if i == 0 and slot == 0 and not first:
                            hi_part(p - 1, SLOTS - 1, 0)
                        if i == 0 and slot >= 2 and main is not None:
                            hi_part(p, slot - 1, 0)
                        turn = GH * slot + i - LN_HI_AFTER
                        if 0 <= turn < GH and main is not None:
                            hi_part(p, 0, turn)
                        if sj is not None:
                            exp_head(*sj, i)
                        k = wo_piece(last, slot, i)
                        if k is not None:
                            act.wait_ge(wo_loaded[k], 16)
                            nc.scalar.activation(part_of(W["wq_hi"], k), ht[:, k % 4, :], ACT.Copy).then_inc(wo_hi, 1)
                        if i == 6 and aj is not None:
                            q, j = aj
                            act.wait_ge(av_done, 8 * q + j + 1)
                            wait_count(act, att_stored[j % 2], 16 * (4 * q + j // 2))
                            nc.scalar.activation(att[:, j % 2].rearrange("p c t -> p (c t)"), av[:, 0:2 * S], ACT.Copy).then_inc(att_copied, 1)
            act.wait_ge(const_ready, 1)
            visit(body)(act)

        @block.gpsimd
        def _(pool):
            def body(p, first, last):
                for slot, main, sj, tj, aj in slots(p, first, last):
                    for unit, half in ((tj, 1), (sj, 0)):
                        if unit is None:
                            continue
                        q, j = unit
                        pool.wait_ge(recip_done, 16 * q + 2 * j + half + 1)
                        for t, (n, cols) in enumerate(((CH, slice(0, CH)), (TXT, slice(CH, CH + S)))):
                            w = P[0:n, j % 2, 4 * half:4 * half + 4, cols]
                            r = rden[0:n, j % 2, half, t, :].unsqueeze(2).to_broadcast((n, 4, cols.stop - cols.start))
                            lastp = nc.gpsimd.tensor_tensor(w, w, r, ALU.mult)
                        lastp.then_inc(probs_ready, 1)
            visit(body)(pool)

        RECIP_AT = (5, 2)
        LO_AT, KV_LO_AT = 1, 3
        STATS_AT, RSTD_RATE = 12, 1
        APPLY_AT, APPLY_EVERY = 35, 1
        CHAINS = 8 + 4 + 1 + RSQRT_LINKS

        @block.vector
        def _(dve):
            v = nc.vector

            def bias_head(p, j, i):
                wait_apart(dve, scores_done, 64 * p + 8 * j + i + 1, const_loaded, 32)
                for t, (n, cols, m) in enumerate(((CH, slice(0, CH), slice(CH, 2 * CH)), (TXT, slice(CH, CH + S), slice(0, S)))):
                    lastv = v.tensor_tensor_reduce(P[0:n, j % 2, i, cols], sc[i % 2][0:n, cols], mask[0:n, m], 1.0, 3.0e38,
                                                   ALU.add, ALU.min, nmax[0:n, j % 2, i // 4, t, i % 4:i % 4 + 1])
                lastv.then_inc(scores_biased, 1)

            def recip(p, j, half):
                dve.wait_ge(exp_done, 64 * p + 8 * j + 4 * half + 4)
                v.reciprocal(rden[:, j % 2, half], den[:, j % 2, half]).then_inc(recip_done, 1)

            def copy_turned(p, j, i):
                dve.wait_ge(transposed, 64 * p + 8 * j + i + 1)
                if i == 0:
                    wait_count(dve, av_done, 8 * p + j - 1)
                v.tensor_copy(PTR[:, j % 2, i, :], pt[i % 2][:, 0:S + TXT]).then_inc(pT_copied, 1)

            def lo_part(p, slot, i):
                what = MAIN[slot]
                if what == "ln":
                    s, half = i % 4, i // 4
                    c, t0, n = TILES[s]
                    dve.wait_ge(hi_written, (BANK_USES - 1) * p + i + 1)
                    at = (slice(None), slice(4 * half, 4 * half + 4), slice(c * S + t0, c * S + t0 + n))
                    src = pr[i % BANKS][:, :].rearrange("p (q t) -> p q t", q=4)[:, :, 0:n]
                    v.tensor_tensor(xT[1][at], src, xT[0][at].bitcast(F32), ALU.subtract).then_inc(bank_read, 1)
                elif what == "kv":
                    dve.wait_ge(hi_written, (BANK_USES - 1) * p + hi_count(KV_USE))
                    src = pr[KV_USE % BANKS][HD:2 * HD, 0:PT].rearrange("p (b t) -> p b t", b=2)
                    for var in range(2):
                        at = Ks[HD:2 * HD, var, :, 0:S]
                        lastv = v.tensor_tensor(at, src, at.bitcast(F32), ALU.subtract)
                    lastv.then_inc(bank_read, 1)
                else:
                    k = what[1]
                    dve.wait_ge(hi_written, (BANK_USES - 1) * p + hi_count(USE[k]))
                    v.scalar_tensor_tensor(out=q_lo[:, k % 2, :], in0=pr[USE[k] % BANKS][:, 0:PT], scalar=-SCALE,
                                           in1=q_hi[:, k % 2, :].bitcast(F32), op0=ALU.mult, op1=ALU.subtract).then_inc(bank_read, 1)

            def copy_v(p):
                dve.wait_ge(proj_done, BANK_USES * p + VT_USE + 1)
                wait_count(dve, av_done, 8 * p)
                src = pr[VT_USE % BANKS][:, 0:128].rearrange("p (b t d) -> p b t d", b=2, t=2)
                v.tensor_copy(V0[:], src[:, :, 0, :])
                v.tensor_copy(V1[0:TXT], src[0:TXT, :, 1, :]).then_inc(bank_read, 1)

            def ln_stats(p, step, link):
                s, part = step // 3, step % 3
                n = TILES[s][2]
                if part == 0:
                    dve.wait_ge(h_loaded[s], 16 * (p + 1))
                if part < 2:
                    link.issued(v.bn_stats(stats[0:n, s, part, :], ht[0:n, s, 512 * part:512 * part + 512]))
                else:
                    link.wait(apart=True)
                    link.issued(v.bn_aggr(mv[0:n, s, :], stats[0:n, s].rearrange("p a b -> p (a b)")))

            def ln_rstd(step, link):
                link.wait()
                if step == 0:
                    link.issued(v.tensor_scalar(veps[:], mv[:, :, 1], EPS, None, ALU.add))
                else:
                    link.issued(rsqrt_step(nc, step - 1, rstd[:], veps[:], rtmp[:]))

            def ln_apply(p, s, link):
                n = TILES[s][2]
                if s == 0:
                    link.wait()
                v.tensor_scalar(ht[0:n, s, :], ht[0:n, s, :], mv[0:n, s, 0:1], rstd[0:n, s:s + 1],
                                ALU.subtract, ALU.mult).then_inc(xn_ready, 1)

            def body(p, first, last):
                link = Chain(dve, chain, CHAINS * (p + 1) if last is False else 0, const_ready)
                for slot, main, sj, tj, aj in slots(p, first, last):
                    for i in range(GH):
                        if sj is not None:
                            bias_head(*sj, i)
                        if i == LO_AT and slot == 0 and not first:
                            lo_part(p - 1, SLOTS - 1, 0)
                        if i == (KV_LO_AT if MAIN[slot - 1] == "kv" else LO_AT) and slot >= 2 and main is not None:
                            lo_part(p, slot - 1, 0)
                        if i == 2 and slot == V_SLOT and main is not None:
                            copy_v(p)
                        if 0 <= GH * slot + i - LN_LO_AFTER < GH and main is not None:
                            lo_part(p, 0, GH * slot + i - LN_LO_AFTER)
                        k = wo_piece(last, slot, i, LO_AFTER)
                        if k is not None:
                            dve.wait_ge(wo_hi, k + 1)
                            v.tensor_tensor(part_of(W["wq_lo"], k), ht[:, k % 4, :], part_of(W["wq_hi"], k).bitcast(F32),
                                            ALU.subtract).then_inc(wo_lo, 1)
                        if i == RECIP_AT[1] and tj is not None:
                            recip(*tj, 1)
                        if i == RECIP_AT[0] and sj is not None:
                            recip(*sj, 0)
                        if last is False:
                            turn = GH * slot + i
                            if STATS_AT <= turn < STATS_AT + 12:
                                ln_stats(p + 1, turn - STATS_AT, link)
                            for step in range(RSQRT_LINKS + 1):
                                if turn == STATS_AT + 12 + step // RSTD_RATE:
                                    ln_rstd(step, link)
                            for s in range(4):
                                if turn == APPLY_AT + APPLY_EVERY * s:
                                    ln_apply(p + 1, s, link)
                        turning = tj if i >= 4 else aj
                        if turning is not None:
                            copy_turned(*turning, (i + 4) % GH)

            first = Chain(dve, sem("att_setup_chain"))
            dve.wait_ge(const_loaded, 32)
            v.memset(den[:], 1.0)
            v.memset(mv[:], 1.0)
            for bank in pt:
                v.memset(bank[:, 0:S + TXT], 0.0)
            first.done(v.memset(Ks[:].bitcast(F32), 0.0))
            v.tensor_copy(Ks[96:100], crow[96:100, 16:16 + 4 * (S + 1)].rearrange("p (v b t) -> p v b t", v=2, b=2))
            first.done(v.tensor_copy(Qs[96:100].rearrange("p s h t -> p (s h) t"),
                                     crow[96:100, 0:16].unsqueeze(2).to_broadcast((4, 16, PT))))
            link = Chain(dve, chain, met=const_ready)
            for step in range(12):
                ln_stats(0, step, link)
            for step in range(RSQRT_LINKS + 1):
                ln_rstd(step, link)
            for s in range(4):
                ln_apply(0, s, link)
            v.memset(rtmp[:, 0:1], 0.0).then_inc(const_ready, 1)
            visit(body)(dve)


def mlp_block(nc, ctx, io, W):
    def sb(name, shape, dt=F32):
        return ctx.enter_context(nc.sbuf_tensor(name, shape, dt))

    def pb(name):
        return ctx.enter_context(nc.psum_tensor(name, [128, 512], F32))

    def sem(name):
        return ctx.enter_context(nc.semaphore(name))

    ident = W["ident"]
    ARW = 144
    PIECES = KC + 2
    SIZES = [DM] * KC + [KC * ARW // 2] * 2
    OFFS = [sum(SIZES[:k]) for k in range(PIECES + 1)]
    w_hi, w_lo = sb("w2_hi", [128, OFFS[-1]], F32R), sb("w2_lo", [128, OFFS[-1]], F32R)
    RING = 3
    TILE1_AFTER = 5
    stage = sb("w2_stage", [128, RING, DM])

    def part(hi_lo, off, n, w):
        return [t[:, off:off + n * w].rearrange("p (k m) -> p k m", k=n) for t in hi_lo]

    early = (W["wq_hi"], W["wq_lo"])
    wo, wB = part(early, 0, KC, DM), part(early, KC * DM, 1, DM)
    wb, war = part((w_hi, w_lo), 0, KC, DM), part((w_hi, w_lo), OFFS[KC], KC, ARW)
    base_b, rout_b = sb("base_b", [128, DM]), sb("rout_b", [128, ROUTES])
    emap, emapf, sel_map = sb("emap", [128, ROUTES], I32), sb("emapf", [128, ROUTES]), sb("sel_map", [128, EXPERTS, ROUTES])
    at, a_loaded = W["at"], W["a_loaded"]
    aT = [sb("aT_hi", [128, KC, 128], F32R), sb("aT_lo", [128, KC, 128], F32R)]
    h2 = sb("h2", [128, 2, DM])
    xn = sb("xn", [128, DM])
    xT = [sb("x2T_hi", [128, KC, 128], F32R), sb("x2T_lo", [128, KC, 128], F32R)]
    stats, mv, rstd, rtmp, veps = sb("stats2", [128, 2, 6]), sb("mv2", [128, 2]), sb("rstd2", [128, 1]), sb("rtmp2", [128, 1]), sb("veps2", [128, 1])
    lg, m8, nm = sb("lg", [128, ROUTES]), sb("m8", [128, 8]), sb("nm", [128, 1])
    ex, e8, er, dn, rd = sb("ex", [128, ROUTES]), sb("e8", [128, 8]), sb("er", [128, ROUTES]), sb("dn", [128, 1]), sb("rd", [128, 1])
    wsel, w8 = sb("wsel", [128, EXPERTS, ROUTES]), sb("w8", [128, EXPERTS])
    z = sb("z", [128, ER])
    zT = [sb("zT_hi", [128, 128], F32R), sb("zT_lo", [128, 128], F32R)]

    wo_ps, x_ps, base_ps = [pb("wo0"), pb("wo1")], [pb("x0"), pb("x1")], [pb("b0"), pb("b1")]
    ar_ps, z_ps = pb("ar"), pb("zp")

    const_loaded, w_loaded = sem("mlp_const_loaded"), [sem(f"w2_loaded{i}") for i in range(RING)]
    hi_split, lo_split = sem("w2_hi_done"), sem("w2_lo_done")
    r_loaded = [sem("r_loaded0"), sem("r_loaded1")]
    a_hi, a_lo, wo_done, wo_read = sem("a_hi"), sem("a_lo"), sem("wo_done"), sem("wo_read")
    x_ready, biased = sem("x2_ready"), sem("h2_biased")
    xT_done, xT_hi, xT_lo = sem("x2T_done"), sem("x2T_hi_done"), sem("x2T_lo_done")
    ar_done, logits_ready, exp_ready, z_ready = sem("ar_done"), sem("logits_ready"), sem("router_exp"), sem("z_ready")
    zT_done, zT_hi, zT_lo = sem("zT_done"), sem("zT_hi_done"), sem("zT_lo_done")
    base_done, out_ready, setup, chain = sem("base_done"), sem("out_ready"), sem("mlp_setup"), sem("mlp_chain")
    out_stored = [sem("out_stored0"), sem("out_stored1")]
    LAST = FULL

    def visit(eng, body):
        size = lambda t: 128 if t < FULL else (REST if t == FULL else 0)
        pairs = (FULL - 2) // 2
        for t in range(2):
            body(t, t % 2, t // 2, 128, 128, 128)
        with eng.Fori(1, pairs) as i:
            for par in range(2):
                body(i * 2 + par, par, i, 128, 128, 128)
        for t in range(2 * pairs, FULL + 1):
            body(t, t % 2, t // 2, size(t), size(t + 1), size(t + 2))

    with nc.Block() as block:
        @block.sync
        def _(sp):
            sp.dma_start(base_b[:], io["base_b"].partition_broadcast(128)).then_inc(const_loaded, 16)
            sp.dma_start(rout_b[:], io["router_b"].partition_broadcast(128)).then_inc(const_loaded, 16)
            sp.dma_start(emap[:], io["expert_map"].partition_broadcast(128)).then_inc(const_loaded, 16)

            def load_att(t, par, n):
                wait_count(sp, a_lo, t - 1)
                sp.dma_start(at[:, par, :, 0:n], io["att_dram"].rearrange("(k p) t -> p k t", p=128)[:, :, bass.ds(t * 128, n)]).then_inc(a_loaded[par], 16)

            def load_res(t, par, n):
                sp.dma_start(h2[0:n, par, :], io["h_dram"][bass.ds(t * 128, n), :]).then_inc(r_loaded[par], 16)

            srcs = [io["base_WT"][k * 128:(k + 1) * 128, :] for k in range(KC)]
            srcs += [io["ARW"][:, k * KC // 2:(k + 1) * KC // 2, :] for k in range(2)]
            load_res(0, 0, 128)
            for k in range(PIECES):
                if k >= RING:
                    sp.wait_ge(lo_split, k - RING + 1)
                dst = stage[:, k % RING, 0:SIZES[k]]
                if len(srcs[k].shape) == 3:
                    dst = dst.rearrange("p (k m) -> p k m", m=ARW)
                sp.dma_start(dst, srcs[k]).then_inc(w_loaded[k % RING], 16)
                if k == 3:
                    load_res(1, 1, 128)

            def body(t, par, half_t, n, n1, n2):
                if n2:
                    load_att(t + 2, par, n2)
                sp.wait_ge(out_ready, t + 1)
                sp.dma_start(io["out"][bass.ds(t * 128, n), :], h2[0:n, par, :]).then_inc(out_stored[par], 16)
                if n2:
                    sp.wait_ge(out_stored[par], 16 * half_t + 16)
                    load_res(t + 2, par, n2)
            visit(sp, body)
            sp.wait_ge(out_stored[0], 16 * ((FULL + 2) // 2))
            sp.wait_ge(out_stored[1], 16 * ((FULL + 1) // 2))

        @block.tensor
        def _(pe):
            def three(bank, n, lhs, w, cols, K, start=True, stop=True, between=None):
                for k in range(K):
                    if k == K // 2 and between is not None:
                        between()
                    for m, (a, b) in enumerate(((0, 0), (0, 1), (1, 0))):
                        last = nc.tensor.matmul(bank[0:n, 0:cols.stop - cols.start], lhs[a][:, k, 0:n], w[b][:, k, cols],
                                                start=(start and k == 0 and m == 0), stop=(stop and k == K - 1 and m == 2))
                return last

            def turn_z(t, n):
                pe.wait_ge(z_ready, t + 1)
                nc.tensor.transpose(z_ps[:, 0:n], z[0:n, :], ident[0:n, 0:n]).then_inc(zT_done, 1)

            def attn_out(t, n, between=None):
                pe.wait_ge(a_lo, t + 1)
                wait_count(pe, wo_read, t)
                three(wo_ps[0], n, aT, wo, slice(0, 512), KC)
                if between is not None:
                    between()
                three(wo_ps[1], n, aT, wo, slice(512, 1024), KC).then_inc(wo_done, 1)

            def transpose_x(t, n):
                pe.wait_ge(x_ready, t + 1)
                wait_count(pe, xT_lo, 2 * t)
                for half in range(2):
                    for q in range(4):
                        last = nc.tensor.transpose(x_ps[half][:, 128 * q:128 * q + n], xn[0:n, (4 * half + q) * 128:(4 * half + q + 1) * 128], ident[0:n, 0:n])
                    last.then_inc(xT_done, 1)

            def body(t, par, half_t, n, n1, n2):
                first = isinstance(t, int) and t == 0
                pe.wait_ge(xT_lo, 2 * t + 1)
                if first:
                    pe.wait_ge(lo_split, PIECES)
                wait_count(pe, z_ready, t)
                three(ar_ps, n, xT, war, slice(0, ARW), KC, between=lambda: pe.wait_ge(xT_lo, 2 * t + 2)).then_inc(ar_done, 1)
                if n1 and not first:
                    attn_out(t + 1, n1, between=lambda: turn_z(t, n))
                wait_count(pe, out_ready, t)
                three(base_ps[0], n, xT, wb, slice(0, 512), KC, stop=False)
                if first or not n1:
                    turn_z(t, n)
                three(base_ps[1], n, xT, wb, slice(512, 1024), KC, stop=False)
                if n1:
                    transpose_x(t + 1, n1)
                pe.wait_ge(zT_lo, t + 1)
                zz = [q[:, 0:n].unsqueeze(1) for q in zT]
                for half in range(2):
                    last = three(base_ps[half], n, zz, wB, slice(512 * half, 512 * half + 512), 1, start=False)
                last.then_inc(base_done, 1)
            attn_out(0, 128)
            attn_out(1, 128)
            transpose_x(0, 128)
            visit(pe, body)

        @block.scalar
        def _(act):
            def x_hi(t, n):
                for half in range(2):
                    act.wait_ge(xT_done, 2 * t + half + 1)
                    src = x_ps[half][:, :].rearrange("p (q t) -> p q t", q=4)[:, :, 0:n]
                    nc.scalar.activation(xT[0][:, 4 * half:4 * half + 4, 0:n], src, ACT.Copy).then_inc(xT_hi, 1)

            def a_split(half_t, t, par, n):
                act.wait_ge(a_loaded[par], 16 * half_t + 16)
                wait_count(act, wo_done, t)
                nc.scalar.activation(aT[0][:, :, 0:n], at[:, par, :, 0:n], ACT.Copy).then_inc(a_hi, 1)

            def body(t, par, half_t, n, n1, n2):
                act.wait_ge(logits_ready, t + 1)
                nc.scalar.activation(ex[0:n], lg[0:n], ACT.Exp, bias=nm[0:n, 0:1], accum_out=dn[0:n, 0:1]).then_inc(exp_ready, 1)
                act.wait_ge(zT_done, t + 1)
                nc.scalar.activation(zT[0][:, 0:n], z_ps[:, 0:n], ACT.Copy).then_inc(zT_hi, 1)
                if n2:
                    a_split(half_t + 1, t + 2, par, n2)
                if n1:
                    x_hi(t + 1, n1)

            a_split(0, 0, 0, 128)
            for k in range(PIECES):
                act.wait_ge(w_loaded[k % RING], 16 * (k // RING + 1))
                o = slice(OFFS[k], OFFS[k + 1])
                nc.scalar.activation(w_hi[:, o], stage[:, k % RING, 0:SIZES[k]], ACT.Copy).then_inc(hi_split, 1)
                if k == TILE1_AFTER:
                    a_split(0, 1, 1, 128)
            x_hi(0, 128)
            visit(act, body)

        @block.gpsimd
        def _(pool):
            def add_bias(t, par, n):
                pool.wait_ge(x_ready, t + 1)
                nc.gpsimd.tensor_tensor(h2[0:n, par, :], h2[0:n, par, :], base_b[0:n, :], ALU.add).then_inc(biased, 1)

            def body(t, par, half_t, n, n1, n2):
                if n1:
                    add_bias(t + 1, 1 - par, n1)
            pool.wait_ge(const_loaded, 48)
            add_bias(0, 0, 128)
            visit(pool, body)

        LINKS = (5 + RSQRT_LINKS) + 9

        @block.vector
        def _(dve):
            v = nc.vector

            def residual_ln(t, par, half_t, n, link):
                dve.wait_ge(wo_done, t + 1)
                dve.wait_ge(r_loaded[par], 16 * half_t + 16)
                link.done(v.tensor_tensor(h2[0:n, par, 0:512], wo_ps[0][0:n, :], h2[0:n, par, 0:512], ALU.add))
                v.tensor_tensor(h2[0:n, par, 512:1024], wo_ps[1][0:n, :], h2[0:n, par, 512:1024], ALU.add).then_inc(wo_read, 1)
                dve.wait_ge(wo_read, t + 1)
                link.done(v.bn_stats(stats[0:n, 0, :], h2[0:n, par, 0:512]))
                link.done(v.bn_stats(stats[0:n, 1, :], h2[0:n, par, 512:1024]), apart=True)
                link.done(v.bn_aggr(mv[0:n, :], stats[0:n].rearrange("p a b -> p (a b)")))
                link.done(v.tensor_scalar(veps[0:n], mv[0:n, 1:2], EPS, None, ALU.add))
                rsqrt_newton(nc, link.done, rstd[0:n], veps[0:n], rtmp[0:n])
                wait_count(dve, xT_done, 2 * t)
                v.tensor_scalar(xn[0:n, :], h2[0:n, par, :], mv[0:n, 0:1], rstd[0:n, 0:1], ALU.subtract, ALU.mult).then_inc(x_ready, 1)

            def att_lo(t, par, n):
                dve.wait_ge(a_hi, t + 1)
                v.tensor_tensor(aT[1][:, :, 0:n], at[:, par, :, 0:n], aT[0][:, :, 0:n].bitcast(F32), ALU.subtract).then_inc(a_lo, 1)

            def x_lo(t, n):
                for half in range(2):
                    dve.wait_ge(xT_hi, 2 * t + half + 1)
                    src = x_ps[half][:, :].rearrange("p (q t) -> p q t", q=4)[:, :, 0:n]
                    c = slice(4 * half, 4 * half + 4)
                    v.tensor_tensor(xT[1][:, c, 0:n], src, xT[0][:, c, 0:n].bitcast(F32), ALU.subtract).then_inc(xT_lo, 1)

            def router(t, n, link):
                dve.wait_ge(ar_done, t + 1)
                link.done(v.tensor_tensor(lg[0:n], ar_ps[0:n, ER:ER + ROUTES], rout_b[0:n], ALU.add), apart=True)
                link.done(v.max(m8[0:n], lg[0:n]))
                v.tensor_scalar(nm[0:n], m8[0:n, 0:1], -1.0, None, ALU.mult).then_inc(logits_ready, 1)
                wait_apart(dve, exp_ready, t + 1, setup)
                link.done(v.max(e8[0:n], ex[0:n]), apart=True)
                link.done(v.match_replace(er[0:n], e8[0:n], ex[0:n], 0.0))
                link.done(v.tensor_tensor(er[0:n], ex[0:n], er[0:n], ALU.subtract))
                link.done(v.tensor_tensor(wsel[0:n], er[0:n].unsqueeze(1).to_broadcast((n, EXPERTS, ROUTES)), sel_map[0:n], ALU.mult))
                link.done(v.tensor_reduce(w8[0:n], wsel[0:n], AX.X, ALU.add))
                link.done(v.reciprocal(rd[0:n], dn[0:n]))
                link.done(v.tensor_scalar(rd[0:n], rd[0:n], 2.0, None, ALU.mult))
                wait_count(dve, zT_done, t)
                v.scalar_tensor_tensor(out=z[0:n].rearrange("p (e r) -> p e r", e=EXPERTS),
                                       in0=ar_ps[0:n, 0:ER].rearrange("p (e r) -> p e r", e=EXPERTS), scalar=rd[0:n, 0:1],
                                       in1=w8[0:n].unsqueeze(2).to_broadcast((n, EXPERTS, RANK)), op0=ALU.mult, op1=ALU.mult).then_inc(z_ready, 1)

            def body(t, par, half_t, n, n1, n2):
                link = Chain(dve, chain, LINKS * t + (5 + RSQRT_LINKS), setup)
                router(t, n, link)
                dve.wait_ge(zT_hi, t + 1)
                v.tensor_tensor(zT[1][:, 0:n], z_ps[:, 0:n], zT[0][:, 0:n].bitcast(F32), ALU.subtract).then_inc(zT_lo, 1)
                if n1:
                    residual_ln(t + 1, 1 - par, half_t + par, n1, link)
                if n2:
                    att_lo(t + 2, par, n2)
                if n1:
                    x_lo(t + 1, n1)
                dve.wait_ge(base_done, t + 1)
                dve.wait_ge(biased, t + 1)
                for half in range(2):
                    c = slice(512 * half, 512 * half + 512)
                    last = v.tensor_tensor(h2[0:n, par, c], base_ps[half][0:n, :], h2[0:n, par, c], ALU.add)
                last.then_inc(out_ready, 1)

            first = Chain(dve, setup)
            att_lo(0, 0, 128)
            dve.wait_ge(const_loaded, 48)
            first.done(v.tensor_copy(emapf[:], emap[:]))
            for e in range(EXPERTS):
                last = v.tensor_scalar(sel_map[:, e, :], emapf[:], float(e), None, ALU.is_equal)
            first.done(last)
            for k in range(PIECES):
                dve.wait_ge(hi_split, k + 1)
                o = slice(OFFS[k], OFFS[k + 1])
                v.tensor_tensor(w_lo[:, o], stage[:, k % RING, 0:SIZES[k]], w_hi[:, o].bitcast(F32), ALU.subtract).then_inc(lo_split, 1)
                if k == TILE1_AFTER:
                    att_lo(1, 1, 128)
                    residual_ln(0, 0, 0, 128, Chain(dve, chain))
            x_lo(0, 128)
            visit(dve, body)


def build(nc, io):
    with ExitStack() as whole:
        W = {"ident": whole.enter_context(nc.sbuf_tensor("ident", [128, 128], F32))}
        for n in ("wq_hi", "wq_lo"):
            W[n] = whole.enter_context(nc.sbuf_tensor(n, [128, (KC + 1) * DM], F32R))
        with ExitStack() as ctx:
            mixer_block(nc, ctx, io, W)
        W["at"] = whole.enter_context(nc.sbuf_tensor("at", [128, 2, KC, 128], F32))
        W["a_loaded"] = [whole.enter_context(nc.semaphore(f"a_loaded{i}")) for i in range(2)]
        with ExitStack() as ctx:
            attention_block(nc, ctx, io, W)
        with ExitStack() as ctx:
            mlp_block(nc, ctx, io, W)


def constants():
    f = np.float32
    base = 2.0 ** (-2.0 ** (-(math.log2(HEADS) - 3)))
    slopes = (base ** np.arange(1, HEADS + 1, dtype=np.float64)).astype(f)
    hi = (((slopes.view(np.uint32) + np.uint32(0x800)) & np.uint32(0xFFFFF000))).view(f)
    lo = slopes - hi
    rows = np.zeros((4, 16 + 4 * (S + 1)), f)
    for slot in range(2):
        for late in range(2):
            g = slot + 2 * late
            rows[2 * late, slot * GH:(slot + 1) * GH] = hi[g * GH:(g + 1) * GH]
            rows[2 * late + 1, slot * GH:(slot + 1) * GH] = lo[g * GH:(g + 1) * GH]
    pos = np.zeros((2, 2, S + 1), f)
    pos[:, :, :S] = -np.arange(S, dtype=f)
    zero = np.zeros_like(pos[0])
    for late in range(2):
        both = np.stack([pos[0] if late == 0 else zero, pos[0] if late == 1 else zero])
        rows[2 * late:2 * late + 2, 16:] = both.reshape(-1)
    k, p = np.arange(256)[None, :] - 128, np.arange(128)[:, None]
    quarter = np.zeros((128, 3), f)
    quarter[0:64, 0], quarter[0:64, 1], quarter[:, 2] = 0.25, TWO_PI / 4, TWO_PI / 4
    return {
        "bvals": np.broadcast_to(np.arange(128, dtype=f), (128, 128)).copy(),
        "avals": np.broadcast_to(128 * np.arange(AH, dtype=f), (128, AH)).copy(),
        "quarter": quarter,
        "ident": np.eye(128, dtype=f),
        "mask": np.where(k > p, f(1e30), f(0)).astype(f),
        "rows": rows,
    }


def kernel(**inputs):
    import concourse.bacc as bacc
    from concourse.bass_utils import run_bass_kernel_spmd

    g = {k: np.asarray(v) for k, v in inputs.items()}
    x, wqkv = g["x"], g["L0_attn_Wqkv"]
    arw = np.zeros((DM, 144), np.float32)
    arw[:, 0:ER] = g["L0_ffn_A"].reshape(ER, DM).T
    arw[:, ER:ER + ROUTES] = g["L0_ffn_router_W"].T
    laid = {
        "x_re": x[..., 0].transpose(2, 1, 0),
        "x_im": x[..., 1].transpose(2, 1, 0),
        "txt": g["txt"],
        "log_dt": np.broadcast_to(g["L0_tok_log_dt"], (64, CH)),
        "B_re": g["L0_tok_B"][..., 0].T,
        "B_im": g["L0_tok_B"][..., 1].T,
        "inv_A_real": g["L0_tok_inv_A_real"].T,
        "A_imag": g["L0_tok_A_imag"].T,
        "Wqkv": np.concatenate([wqkv[:, 0:DM].reshape(DM, KC, 4, HD).transpose(0, 1, 3, 2).reshape(DM, DM), wqkv[:, DM:]], 1),
        "Wo": g["L0_attn_Wo"],
        "base_WT": g["L0_ffn_base_W"].T,
        "base_b": g["L0_ffn_base_b"],
        "router_b": g["L0_ffn_router_b"],
        "ARW": arw.reshape(KC, 128, 144).transpose(1, 0, 2),
        "BT": g["L0_ffn_B"].transpose(0, 2, 1).reshape(ER, DM),
        "expert_map": g["L0_ffn_expert_map"],
        **constants(),
    }
    nc = bacc.Bacc("TRN2", target_bir_lowering=False, num_devices=1)
    arrays, io = {}, {}
    for name, a in laid.items():
        a = np.ascontiguousarray(a)
        arrays[f"in_{name}"] = a
        io[name] = nc.dram_tensor(f"in_{name}", a.shape, mybir.dt.from_np(a.dtype), kind="ExternalInput").ap()
    io["h_dram"] = nc.dram_tensor("h_dram", (TOK, DM), F32, kind="Internal").ap()
    io["att_dram"] = nc.dram_tensor("att_dram", (DM, TOK), F32, kind="Internal").ap()
    io["out"] = nc.dram_tensor("out_0", (TOK, DM), F32, kind="ExternalOutput").ap()
    build(nc, io)
    r = run_bass_kernel_spmd(nc, [arrays], core_ids=[0])
    return r.results[0]["out_0"].reshape(SEQS, S, DM)
```

```python
import math
from contextlib import ExitStack

import numpy as np

import concourse.bass as bass
from concourse import mybir

F32, F32R, I32 = mybir.dt.float32, mybir.dt.float32r, mybir.dt.int32
ALU, ACT, AX = mybir.AluOpType, mybir.ActivationFunctionType, mybir.AxisListType

SEQS, CH, STATES = 16, 128, 64
TXT, DM = 77, 1024
S = CH + TXT
TOK = SEQS * S
HEADS, HD = 32, 32
KC = DM // 128
EXPERTS, RANK, ROUTES = 8, 16, 15
ER = EXPERTS * RANK
EPS = 1e-5

AH = DM // 128
ROUND = 1.5 * 2.0 ** 23
TWO_PI = 6.28318
HCH = 16
MIX_STEPS = CH // HCH
QRING = 3

PAIRS = SEQS // 2
PT = 2 * S
SLOTS = 10
BANKS = 3
BANK_USES = 18
GH = 8
UNITS = 8
TILES = [(0, 0, CH), (0, CH, TXT), (1, 0, CH), (1, CH, TXT)]

FULL = TOK // 128
REST = TOK - FULL * 128
RSQRT_GUESS = float(0x5F3759DF)
NEWTON = 3


def wait_count(eng, sem, count):
    if isinstance(count, int) and count <= 0:
        return
    eng.wait_ge(sem, count)


def wait_apart(eng, sem, count, met, met_count=1):
    if isinstance(count, int):
        wait_count(eng, sem, count)
        return
    value = eng.to_reg(count)
    eng.wait_ge(met, met_count)
    eng.wait_ge(sem, value)


class Chain:

    def __init__(self, eng, sem, base=0, met=None):
        self.eng, self.sem, self.base, self.n, self.met = eng, sem, base, 0, met

    def issued(self, ins):
        self.n += 1
        ins.then_inc(self.sem, 1)

    def wait(self, apart=False):
        if apart:
            wait_apart(self.eng, self.sem, self.base + self.n, self.met)
        else:
            self.eng.wait_ge(self.sem, self.base + self.n)

    def done(self, ins, apart=False):
        self.n += 1
        ins.then_inc(self.sem, 1)
        if apart:
            wait_apart(self.eng, self.sem, self.base + self.n, self.met)
        else:
            self.eng.wait_ge(self.sem, self.base + self.n)


RSQRT_LINKS = 1 + 3 * NEWTON


def rsqrt_step(nc, k, y, v, t):
    if k == 0:
        return nc.vector.tensor_scalar(y.bitcast(I32), v.bitcast(I32), -0.5, RSQRT_GUESS, ALU.mult, ALU.add)
    if k % 3 == 1:
        return nc.vector.tensor_tensor(t, y, y, ALU.mult)
    if k % 3 == 2:
        return nc.vector.scalar_tensor_tensor(out=t, in0=t, scalar=-0.5, in1=v, op0=ALU.mult, op1=ALU.mult)
    return nc.vector.scalar_tensor_tensor(out=y, in0=t, scalar=1.5, in1=y, op0=ALU.add, op1=ALU.mult)


def rsqrt_newton(nc, link, y, v, t):
    for k in range(RSQRT_LINKS):
        link(rsqrt_step(nc, k, y, v, t))


def exp_exact(nc, link, y, x, n, r):
    v = nc.vector
    link(v.tensor_scalar(n, x, 1.0 / math.log(2.0), ROUND, ALU.mult, ALU.add))
    link(v.tensor_scalar(n, n, ROUND, None, ALU.subtract))
    link(v.scalar_tensor_tensor(out=r, in0=n, scalar=-0.693359375, in1=x, op0=ALU.mult, op1=ALU.add))
    link(v.scalar_tensor_tensor(out=r, in0=n, scalar=0.693359375 - math.log(2.0), in1=r, op0=ALU.mult, op1=ALU.add))
    link(v.tensor_scalar(y, r, 1.0 / 5040, None, ALU.mult))
    for k in (6, 5, 4, 3, 2, 1):
        link(v.scalar_tensor_tensor(out=y, in0=y, scalar=1.0 / math.factorial(k), in1=r, op0=ALU.add, op1=ALU.mult))
    link(v.tensor_scalar(n.bitcast(I32), n, 2.0 ** 23, 127 * 2.0 ** 23, ALU.mult, ALU.add))
    link(v.scalar_tensor_tensor(out=y, in0=y, scalar=1.0, in1=n, op0=ALU.add, op1=ALU.mult))


def mixer_block(nc, ctx, io, W):
    def sb(name, shape, dt=F32):
        return ctx.enter_context(nc.sbuf_tensor(name, shape, dt))

    def sem(name):
        return ctx.enter_context(nc.semaphore(name))

    xre, xim = sb("xre", [128, CH, SEQS]), sb("xim", [128, CH, SEQS])
    par = sb("par", [128, 5, CH])
    bvals, avals, phase = sb("bvals", [128, 128]), sb("avals", [128, AH]), sb("phase", [128, 6])
    small = sb("small", [128, 16, CH])
    tab = sb("tab", [128, 4, CH, AH])
    turn_b, mag_b = sb("turn_b", [128, HCH, 128]), sb("mag_b", [128, HCH, 128])
    Q = sb("Q", [128, QRING, HCH, 128])
    X, X2 = sb("X", [128, 2, HCH, AH, SEQS]), sb("X2", [128, 2, HCH, AH, SEQS])
    Y = sb("Y", [128, HCH, 128])
    stage = sb("w_stage", [128, 2, DM])
    BANKS_STEP = HCH // 4
    ps = [ctx.enter_context(nc.psum_tensor(f"mix_ps{i}", [128, 4, 128], F32)) for i in range(2 * BANKS_STEP)]

    par_loaded, loaded, txt_copied = sem("par_loaded"), sem("mix_loaded"), sem("txt_copied")
    w_loaded = [sem("w_loaded0"), sem("w_loaded1")]
    w_hi, w_lo = sem("w_hi"), sem("w_lo")
    chain, mag_ready = sem("mix_dve_chain"), sem("mag_ready")
    re_ready, tanh_ready, base_turns = sem("re_ready"), sem("tanh_ready"), sem("base_turns")
    ph_ready, sin_ready, tab_ready = sem("ph_ready"), sem("sin_ready"), sem("tab_ready")
    turns_ready, frac_ready, wave_ready = sem("turns_ready"), sem("frac_ready"), sem("wave_ready")
    q_ready, x2_ready, x_ready = sem("q_ready"), sem("x2_ready"), sem("x_ready")
    mix_done, y_copied = sem("mix_done"), sem("y_copied")
    y_stored = sem("y_stored")

    LDT_IAR, BRE, BIM, AIM = par[:, 0:2], par[:, 2], par[:, 3], par[:, 4]
    DT, ARE, RE, TURNS, TH, F_D, SIN1, SIN2, T0, T1, T2, T3, DRE, DIM_, INV, T4 = (small[:, i] for i in range(16))
    DT_ARE, PAIR0, PAIR1 = small[:, 0:2], small[:, 8:10], small[:, 10:12]
    G1, G2 = tab[:, 0], tab[:, 3]
    PIECES = KC + 1
    h_rows = io["h_dram"].rearrange("(c s) (a b) -> a c s b", s=S, b=128)

    def piece(dst, k):
        return dst[:, k * DM:(k + 1) * DM]

    STORED_STEP = 16 * AH
    LOADS = 8

    with nc.Block() as block:
        @block.sync
        def _(sp):
            halves = (slice(0, 64), slice(64, 128))
            sp.dma_start(par[:], io["par"]).then_inc(par_loaded, 16)
            for dst, name in ((bvals, "bvals"), (avals, "avals"), (phase, "phase")):
                sp.dma_start(dst[:], io[name]).then_inc(loaded, 16)
            for dst, name in ((xre, "x_re"), (xim, "x_im")):
                for half in halves:
                    sp.dma_start(dst[half], io[name]).then_inc(loaded, 16)
            sp.dma_start(W["ident"][:], io["ident"]).then_inc(loaded, 16)

            def load_piece(k):
                if k >= 2:
                    sp.wait_ge(w_lo, k - 1)
                if k < KC:
                    sp.dma_start(stage[:, k % 2, :], io["Wqkv"][k * 128:(k + 1) * 128, 0:DM]).then_inc(w_loaded[k % 2], 64)
                else:
                    kv = stage[:, k % 2, :].rearrange("p (k m) -> p k m", m=128)
                    src = io["Wqkv"][:, DM:DM + 2 * HD].rearrange("(k p) m -> p k m", p=128)
                    for q in range(4):
                        sp.dma_start(kv[:, :, q * HD:(q + 1) * HD],
                                     src[:, :, (q // 3) * HD:(q // 3 + 1) * HD]).then_inc(w_loaded[k % 2], 16)

            load_piece(0)
            load_piece(1)
            sp.dma_start(io["h_dram"].rearrange("(c s) d -> c s d", s=S)[:, CH:S, :], io["txt"]).then_inc(txt_copied, 16)
            for step in range(MIX_STEPS):
                if step + 2 < PIECES:
                    load_piece(step + 2)
                sp.wait_ge(y_copied, step + 1)
                for a in range(AH):
                    sp.dma_start(h_rows[a][:, step * HCH:(step + 1) * HCH, :], Y[a * SEQS:(a + 1) * SEQS]).then_inc(y_stored, 16)
            sp.wait_ge(y_stored, STORED_STEP * MIX_STEPS)
            sp.wait_ge(txt_copied, 16)

        @block.scalar
        def _(act):
            act.wait_ge(re_ready, 1)
            nc.scalar.activation(TH, RE, ACT.Tanh, scale=0.5).then_inc(tanh_ready, 1)
            act.wait_ge(ph_ready, 1)
            nc.scalar.activation(SIN1, F_D, ACT.Sin, scale=-TWO_PI / 2).then_inc(sin_ready, 1)
            nc.scalar.activation(SIN2, F_D, ACT.Sin, scale=-TWO_PI).then_inc(sin_ready, 1)
            act.wait_ge(loaded, 16 * LOADS)
            for i in (1, 2):
                act.wait_ge(ph_ready, 1 + i)
                nc.scalar.activation(tab[:, i], tab[:, i], ACT.Sin, scale=-TWO_PI, bias=phase[:, 2 * i + 1:2 * i + 2]).then_inc(sin_ready, 1)

            def wave(step):
                q = Q[:, step % QRING]
                act.wait_ge(frac_ready, step + 1)
                nc.scalar.activation(q, q, ACT.Sin, scale=-TWO_PI, bias=phase[:, 1:2]).then_inc(wave_ready, 1)

            def magnitudes(step):
                if step == 0:
                    act.wait_ge(ph_ready, 4)
                    nc.scalar.activation(tab[:, 3], tab[:, 3], ACT.Exp).then_inc(sin_ready, 1)
                else:
                    act.wait_ge(q_ready, step)
                for j in range(HCH):
                    h = step * HCH + j
                    last = nc.scalar.activation(mag_b[:, j, :], bvals[:], ACT.Exp, scale=RE[:, h:h + 1])
                last.then_inc(mag_ready, 1)

            def copy_out(step):
                if step == 0:
                    act.wait_ge(tab_ready, 2)
                else:
                    act.wait_ge(y_stored, STORED_STEP * step)
                for q in range(BANKS_STEP):
                    act.wait_ge(mix_done, step * BANKS_STEP + q + 1)
                    last = nc.scalar.activation(Y[:, 4 * q:4 * q + 4, :], ps[step % 2 * BANKS_STEP + q][:], ACT.Copy)
                last.then_inc(y_copied, 1)

            for step in range(MIX_STEPS):
                for part in ((wave, magnitudes), (magnitudes, wave))[step % 2]:
                    part(step)
                if step >= 1:
                    copy_out(step - 1)
            copy_out(MIX_STEPS - 1)

        @block.gpsimd
        def _(pool):
            def turns(step):
                hs = slice(step * HCH, (step + 1) * HCH)
                if step >= 1:
                    pool.wait_ge(frac_ready, step)
                nc.gpsimd.tensor_tensor(turn_b[:], TURNS[:, hs].unsqueeze(2).to_broadcast((128, HCH, 128)),
                                        bvals[:].unsqueeze(1).to_broadcast((128, HCH, 128)), ALU.mult).then_inc(turns_ready, 1)

            def lo_piece(k):
                pool.wait_ge(w_hi, k + 1)
                nc.gpsimd.tensor_tensor(piece(W["wq_lo"], k), stage[:, k % 2, :], piece(W["wq_hi"], k).bitcast(F32), ALU.subtract).then_inc(w_lo, 1)

            pool.wait_ge(loaded, 16 * LOADS)
            pool.wait_ge(base_turns, 1)
            turns(0)
            for step in range(MIX_STEPS):
                hs = slice(step * HCH, (step + 1) * HCH)
                if step + 1 < MIX_STEPS:
                    turns(step + 1)
                pool.wait_ge(tab_ready, 1 if step < MIX_STEPS // 2 else 2)
                if step >= 2:
                    pool.wait_ge(mix_done, (step - 1) * BANKS_STEP)
                nc.gpsimd.tensor_tensor(X2[:, step % 2], xim[:, hs].unsqueeze(2).to_broadcast((128, HCH, AH, SEQS)),
                                        G2[:, hs].unsqueeze(3).to_broadcast((128, HCH, AH, SEQS)), ALU.mult).then_inc(x2_ready, 1)
                if step >= 1:
                    lo_piece(step - 1)
            lo_piece(PIECES - 2)
            lo_piece(PIECES - 1)
            pool.wait_ge(w_lo, PIECES)

        @block.vector
        def _(dve):
            one = Chain(dve, chain)
            link, free = one.done, one.issued
            v = nc.vector
            dve.wait_ge(par_loaded, 16)
            exp_exact(nc, link, DT_ARE, LDT_IAR, PAIR0, PAIR1)
            link(v.tensor_scalar(ARE, ARE, -1.0, None, ALU.mult))
            v.tensor_tensor(RE, ARE, DT, ALU.mult).then_inc(re_ready, 1)
            link(v.tensor_tensor(TURNS, AIM, DT, ALU.mult))
            v.tensor_scalar(TURNS, TURNS, 1.0 / (2.0 * math.pi), None, ALU.mult).then_inc(base_turns, 1)
            dve.wait_ge(base_turns, 1)
            link(v.tensor_scalar(F_D, TURNS, ROUND, None, ALU.add))
            v.scalar_tensor_tensor(out=F_D, in0=F_D, scalar=ROUND, in1=TURNS, op0=ALU.subtract, op1=ALU.subtract).then_inc(ph_ready, 1)
            dve.wait_ge(loaded, 16 * LOADS)
            tb, ab = TURNS.unsqueeze(2).to_broadcast((128, CH, AH)), avals[:].unsqueeze(1).to_broadcast((128, CH, AH))
            link(v.tensor_tensor(tab[:, 0], tb, ab, ALU.mult))
            for i in (1, 2):
                link(v.tensor_scalar(tab[:, i], tab[:, 0], phase[:, 2 * i:2 * i + 1], ROUND, ALU.add, ALU.add))
                v.scalar_tensor_tensor(out=tab[:, i], in0=tab[:, i], scalar=ROUND, in1=tab[:, 0], op0=ALU.subtract, op1=ALU.subtract).then_inc(ph_ready, 1)
            dve.wait_ge(re_ready, 1)
            v.tensor_tensor(tab[:, 3], RE.unsqueeze(2).to_broadcast((128, CH, AH)), ab, ALU.mult).then_inc(ph_ready, 1)

            def fraction(step, link):
                dve.wait_ge(turns_ready, step + 1)
                if step >= QRING:
                    dve.wait_ge(mix_done, (step - QRING + 1) * BANKS_STEP)
                q = Q[:, step % QRING]
                link(v.tensor_scalar(q, turn_b[:], phase[:, 0:1], ROUND, ALU.add, ALU.add))
                v.scalar_tensor_tensor(out=q, in0=q, scalar=ROUND, in1=turn_b[:], op0=ALU.subtract, op1=ALU.subtract).then_inc(frac_ready, 1)

            fraction(0, link)
            free(v.tensor_tensor(T2, ARE, ARE, ALU.mult))
            link(v.tensor_tensor(T3, AIM, AIM, ALU.mult))
            link(v.tensor_tensor(T2, T2, T3, ALU.add))
            link(v.reciprocal(INV, T2))
            link(v.tensor_scalar(INV, INV, 2.0, None, ALU.mult))
            dve.wait_ge(tanh_ready, 1)
            link(v.tensor_scalar(T0, TH, -1.0, 1.0, ALU.mult, ALU.add))
            link(v.reciprocal(T0, T0))
            dve.wait_ge(sin_ready, 2)
            free(v.tensor_tensor(T2, SIN1, SIN1, ALU.mult))
            link(v.scalar_tensor_tensor(out=T0, in0=TH, scalar=2.0, in1=T0, op0=ALU.mult, op1=ALU.mult))
            link(v.tensor_scalar(T1, T0, 1.0, None, ALU.add))
            link(v.scalar_tensor_tensor(out=T2, in0=T2, scalar=-2.0, in1=T1, op0=ALU.mult, op1=ALU.mult))
            free(v.tensor_tensor(T0, T0, T2, ALU.add))
            link(v.tensor_tensor(T1, T1, SIN2, ALU.mult))
            free(v.tensor_tensor(T2, T0, ARE, ALU.mult))
            free(v.tensor_tensor(T3, T1, AIM, ALU.mult))
            free(v.tensor_tensor(TH, T1, ARE, ALU.mult))
            link(v.tensor_tensor(T4, T0, AIM, ALU.mult))
            free(v.tensor_tensor(T2, T2, T3, ALU.add))
            link(v.tensor_tensor(TH, TH, T4, ALU.subtract))
            free(v.tensor_tensor(T2, T2, INV, ALU.mult))
            link(v.tensor_tensor(T3, TH, INV, ALU.mult))
            free(v.tensor_tensor(T0, BRE, T2, ALU.mult))
            free(v.tensor_tensor(T1, BIM, T3, ALU.mult))
            free(v.tensor_tensor(TH, BRE, T3, ALU.mult))
            link(v.tensor_tensor(T4, BIM, T2, ALU.mult))
            free(v.tensor_tensor(DRE, T0, T1, ALU.subtract))
            link(v.tensor_tensor(DIM_, TH, T4, ALU.add))

            def tables(part, link, free):
                hs = slice(part * CH // 2, (part + 1) * CH // 2)
                t1, t2, t3 = tab[:, 1, hs], tab[:, 2, hs], tab[:, 3, hs]
                ta, tc, td, te = (Y[:].rearrange("p h b -> p (h b)")[:, i * 512:(i + 1) * 512].rearrange("p (h a) -> p h a", a=AH) for i in range(4))
                dre, dim = (z[:, hs].unsqueeze(2).to_broadcast((128, CH // 2, AH)) for z in (DRE, DIM_))
                free(v.tensor_tensor(t1, t1, t3, ALU.mult))
                link(v.tensor_tensor(t2, t2, t3, ALU.mult))
                free(v.tensor_tensor(ta, dre, t1, ALU.mult))
                free(v.tensor_tensor(tc, dim, t2, ALU.mult))
                free(v.tensor_tensor(td, dre, t2, ALU.mult))
                link(v.tensor_tensor(te, dim, t1, ALU.mult))
                free(v.tensor_tensor(G1[:, hs], ta, tc, ALU.subtract))
                v.scalar_tensor_tensor(out=G2[:, hs], in0=td, scalar=-1.0, in1=te, op0=ALU.mult, op1=ALU.subtract).then_inc(tab_ready, 1)

            def hi_piece(k):
                dve.wait_ge(w_loaded[k % 2], 64 * (k // 2 + 1))
                v.tensor_copy(piece(W["wq_hi"], k), stage[:, k % 2, :]).then_inc(w_hi, 1)

            dve.wait_ge(sin_ready, 5)
            tables(0, link, free)
            for step in range(MIX_STEPS):
                hs = slice(step * HCH, (step + 1) * HCH)
                if step + 1 < MIX_STEPS:
                    fraction(step + 1, link)
                if step >= 2:
                    dve.wait_ge(mix_done, (step - 1) * BANKS_STEP)
                dve.wait_ge(tab_ready, 1 if step < MIX_STEPS // 2 else 2)
                if step == 0:
                    one.wait()
                v.tensor_tensor(X[:, step % 2], xre[:, hs].unsqueeze(2).to_broadcast((128, HCH, AH, SEQS)),
                                G1[:, hs].unsqueeze(3).to_broadcast((128, HCH, AH, SEQS)), ALU.mult).then_inc(x_ready, 1)
                dve.wait_ge(wave_ready, step + 1)
                dve.wait_ge(mag_ready, step + 1)
                v.tensor_tensor(Q[:, step % QRING], Q[:, step % QRING], mag_b[:], ALU.mult).then_inc(q_ready, 1)
                if step == 0:
                    tables(1, link, free)
                    one.wait()
                hi_piece(step)
            hi_piece(PIECES - 1)

        @block.tensor
        def _(pe):
            for step in range(MIX_STEPS):
                pe.wait_ge(x_ready, step + 1)
                pe.wait_ge(x2_ready, step + 1)
                pe.wait_ge(q_ready, step + 1)
                if step >= 2:
                    pe.wait_ge(y_copied, step - 1)
                for j in range(HCH):
                    out = ps[step % 2 * BANKS_STEP + j // 4][:, j % 4, :]
                    for x, first in ((X, True), (X2, False)):
                        last = nc.tensor.matmul(out, x[:, step % 2, j].rearrange("p a c -> p (a c)"),
                                                Q[:, step % QRING, j, :], start=first, stop=not first)
                    if j % 4 == 3:
                        last.then_inc(mix_done, 1)


def attention_block(nc, ctx, io, W):
    def sb(name, shape, dt=F32):
        return ctx.enter_context(nc.sbuf_tensor(name, shape, dt))

    def pb(name, shape):
        return ctx.enter_context(nc.psum_tensor(name, shape, F32))

    def sem(name):
        return ctx.enter_context(nc.semaphore(name))

    ident = W["ident"]
    wq = [W["wq_hi"][:, 0:KC * DM].rearrange("p (k m) -> p k m", k=KC), W["wq_lo"][:, 0:KC * DM].rearrange("p (k m) -> p k m", k=KC)]
    wkv = [w[:, KC * DM:(KC + 1) * DM].rearrange("p (k m) -> p k m", k=KC) for w in (W["wq_hi"], W["wq_lo"])]
    ht = sb("ht", [128, 4, DM])
    stats, mv = sb("stats", [128, 4, 2, 6]), sb("mv", [128, 4, 2])
    rstd, rtmp, veps = sb("rstd", [128, 4]), sb("rtmp", [128, 4]), sb("veps", [128, 4])
    xT = [sb("xT_hi", [128, KC, PT], F32R), sb("xT_lo", [128, KC, PT], F32R)]
    q_hi, q_lo = sb("q_hi", [128, 2, PT], F32R), sb("q_lo", [128, 2, PT], F32R)
    QR = 3 * HD + 4
    Qs = sb("Qs", [128, 2, GH, PT], F32R)
    Ks = sb("Ks", [128, 2, 2, S + 1], F32R)
    crow = sb("crow", [128, 16 + 4 * (S + 1)])
    vT = sb("vT", [128, PT])
    V0, V1 = sb("V0", [128, 2, HD]), sb("V1", [128, 2, HD])
    mask = sb("mask", [128, 2 * 128])
    P = sb("P", [128, 2, GH, CH + S])
    nmax, den, rden = (sb(n, [128, 2, 2, 2, 4]) for n in ("nmax", "den", "rden"))
    PTR = sb("PTR", [128, 2, GH, S + TXT])
    PT0, PT1 = PTR[:, :, :, 0:S], PTR[:, :, :, S:S + TXT]
    att = sb("att", [128, 2, 2, S])

    sc = [pb(f"sc{i}", [128, 512]) for i in range(2)]
    pt = [pb(f"pt{i}", [128, 512]) for i in range(2)]
    av = pb("av", [128, 512])
    pr = [pb(f"pr{i}", [128, 512]) for i in range(BANKS)]

    const_loaded, const_ready = sem("att_const_loaded"), sem("att_const_ready")
    h_loaded = [sem(f"h_loaded{i}") for i in range(4)]
    chain = sem("att_dve_chain")
    xn_ready = sem("xn_ready")
    proj_done, hi_written, bank_read = sem("proj_done"), sem("hi_written"), sem("bank_read")
    q_stacked = [sem("q_stacked0"), sem("q_stacked1")]
    scores_done, scores_biased, exp_done = sem("scores_done"), sem("scores_biased"), sem("exp_done")
    recip_done, probs_ready = sem("recip_done"), sem("probs_ready")
    transposed, pT_copied = sem("transposed"), sem("pT_copied")
    av_done, att_copied = sem("av_done"), sem("att_copied")
    att_stored = [sem("att_stored0"), sem("att_stored1")]
    wo_loaded = [sem(f"wo_loaded{i}") for i in range(KC + 1)]
    rows_ready = sem("rows_ready")
    wo_hi, wo_lo = sem("wo_hi"), sem("wo_lo")

    SCALE = HD ** -0.5
    STACKS = 3
    MAIN = ["ln", ("q", 0), ("q", 1), "kv", ("q", 2), ("q", 3), ("q", 4), ("q", 5), ("q", 6), ("q", 7)]
    USE = {0: 8, 1: 9, 2: 11, 3: 12, 4: 14, 5: 15, 6: 16, 7: 17}
    KV_USE, VT_USE = 10, 13
    V_SLOT = 6
    LN_HI_AFTER, LN_LO_AFTER = 1, 2
    SCORE_SLOT = [5, 6, 7, 8, 9, 11, 12, 13]

    def hi_count(use):
        return use + 1 if use < VT_USE else use

    def att_unit(slot, lag):
        for back in range(2):
            if slot + back * SLOTS - lag in SCORE_SLOT:
                return back, SCORE_SLOT.index(slot + back * SLOTS - lag)
        return None

    WO_PIECES = KC + 1
    SPLIT_AT = [1, 2, 3, 4] + [32, 33, 34, 35, 44]
    LO_AFTER = 2

    def wo_piece(last, slot, i, after=0):
        turn = GH * slot + i - after
        return SPLIT_AT.index(turn) if last is None and turn in SPLIT_AT else None

    def part_of(w, k):
        return w[:, k * DM:(k + 1) * DM]

    def visit(body):
        def run(eng):
            body(0, True, False)
            with eng.Fori(1, PAIRS - 1) as p:
                body(p, False, False)
            body(PAIRS - 1, False, True)
            body(PAIRS, False, None)
        return run

    def slots(p, first, last):
        for slot in range(SLOTS):
            def unit(lag, slot=slot):
                found = att_unit(slot, lag)
                if found is None:
                    return None
                back, j = found
                if (back and first) or (not back and last is None):
                    return None
                return (p - back, j)
            yield slot, (MAIN[slot] if last is not None else None), unit(0), unit(1), unit(2)

    with nc.Block() as block:
        @block.sync
        def _(sp):

            def load_h(p, s):
                c, t0, n = TILES[s]
                r0 = p * PT + (c * S + t0)
                sp.dma_start(ht[0:n, s, :], io["h_dram"][bass.ds(r0, n), :]).then_inc(h_loaded[s], 16)

            def stack_q(p, k):
                g, r = k // 2, k % 2
                wait_apart(sp, bank_read, BANK_USES * p + USE[k] + 1, const_loaded, 32)
                wait_count(sp, scores_done, 64 * p + 16 * g - 16)
                for row, src in ((0, q_hi), (HD, q_hi), (2 * HD, q_lo)):
                    sp.dma_start(Qs[row:row + HD, g % 2, 4 * r:4 * r + 4, :].bitcast(F32),
                                 src[:, r, :].bitcast(F32)).then_inc(q_stacked[r], 16)

            def store_att(p, j):
                g, b = j // 2, j % 2
                sp.wait_ge(att_copied, 8 * p + j + 1)
                dst = io["att_dram"].rearrange("(k p) t -> p k t", p=128)[:, 2 * g:2 * g + 2, bass.ds(p * PT + b * S, S)]
                sp.dma_start(dst, att[:, b, :, :]).then_inc(att_stored[b], 16)

            def load_wo(k):
                src = io["Wo"][k * 128:(k + 1) * 128, :] if k < KC else io["BT"]
                sp.dma_start(ht[:, k % 4, :], src).then_inc(wo_loaded[k], 16)

            def body(p, first, last):
                for slot, main, sj, tj, aj in slots(p, first, last):
                    if last is None and slot == 1:
                        for k in range(4, 8):
                            sp.wait_ge(wo_lo, k - 3)
                            load_wo(k)
                    if last is None and slot == 2:
                        for q in att_stored:
                            sp.wait_ge(q, 16 * UNITS // 2)
                        for t in range(2):
                            sp.dma_start(W["at"][:, t], io["att_dram"].rearrange("(k p) t -> p k t", p=128)[:, :, t * 128:(t + 1) * 128]).then_inc(W["a_loaded"][t], 16)
                    if last is None and slot == 5:
                        sp.wait_ge(wo_lo, 5)
                        load_wo(8)
                    if slot == 1 and last is True:
                        for k in range(4):
                            sp.wait_ge(proj_done, BANK_USES * p + 4 + k + 1)
                            load_wo(k)
                    if main is not None and slot >= 1 and isinstance(MAIN[slot - 1], tuple):
                        stack_q(p, MAIN[slot - 1][1])
                    if slot == 0 and not first:
                        stack_q(p - 1, 7)
                    if slot == 1 and last is False:
                        for s in range(4):
                            sp.wait_ge(proj_done, BANK_USES * p + 4 + s + 1)
                            load_h(p + 1, s)
                    if aj is not None:
                        store_att(*aj)
            for s in range(4):
                load_h(0, s)
            sp.dma_start(mask[:], io["mask"]).then_inc(const_loaded, 16)
            sp.dma_start(crow[96:100, :], io["rows"]).then_inc(const_loaded, 16)
            visit(body)(sp)
            for s in att_stored:
                sp.wait_ge(s, 16 * PAIRS * UNITS // 2)
            for s in W["a_loaded"]:
                sp.wait_ge(s, 16)

        @block.tensor
        def _(pe):
            def scores(p, j, i):
                g, b = j // 2, j % 2
                if i == 0:
                    for q in q_stacked:
                        pe.wait_ge(q, 16 * STACKS * (4 * p + g + 1))
                    if j == 0:
                        pe.wait_ge(bank_read, BANK_USES * p + KV_USE + 1)
                    if isinstance(p, int) and p + j == 0:
                        pe.wait_ge(rows_ready, 3)
                n = 64 * p + 8 * j + i
                wait_count(pe, scores_biased, n - 1)
                bank, q = sc[i % 2], Qs[0:QR, g % 2, i, b * S:(b + 1) * S]
                nc.tensor.matmul(bank[:, 0:CH], q[:, 0:CH], Ks[0:QR, g // 2, b, 0:CH], start=True, stop=True)
                nc.tensor.matmul(bank[0:TXT, CH:CH + S + 1], q[:, CH:S], Ks[0:QR, g // 2, b, :],
                                 start=True, stop=True).then_inc(scores_done, 1)

            def turn(p, j, i):
                if i % 4 == 0:
                    pe.wait_ge(probs_ready, 16 * p + 2 * j + i // 4 + 1)
                wait_count(pe, pT_copied, 64 * p + 8 * j + i - 1)
                bank, src = pt[i % 2], P[:, j % 2, i, :]
                nc.tensor.transpose(bank[:, 0:CH], src[:, 0:CH], ident[:])
                nc.tensor.transpose(bank[:, CH:S], src[0:TXT, CH:2 * CH], ident[0:TXT, 0:TXT])
                nc.tensor.transpose(bank[0:TXT, S:S + TXT], src[0:TXT, 2 * CH:CH + S],
                                    ident[0:TXT, 0:TXT]).then_inc(transposed, 1)

            def values(p, j):
                b, o = j % 2, av
                pe.wait_ge(pT_copied, 64 * p + 8 * (j + 1))
                wait_count(pe, att_copied, 8 * p + j)
                if j == 0:
                    pe.wait_ge(bank_read, BANK_USES * p + VT_USE + 1)
                for q in range(4):
                    rows = slice(32 * q, 32 * q + 32)
                    nc.tensor.matmul(o[rows, 0:2 * S], V0[:, b, :], PT0[:, j % 2, q:q + 5:4, :], start=True, stop=False)
                for q in range(4):
                    rows = slice(32 * q, 32 * q + 32)
                    last = nc.tensor.matmul(o[rows, 0:2 * S].rearrange("p (c t) -> p c t", c=2)[:, :, CH:S],
                                            V1[0:TXT, b, :], PT1[0:TXT, j % 2, q:q + 5:4, :], start=False, stop=True)
                last.then_inc(av_done, 1)

            def three(out, w, cols, i):
                for m, (a, x) in enumerate(((0, 0), (0, 1), (1, 0))):
                    last = nc.tensor.matmul(out, w[a][:, i, cols], xT[x][:, i, :], start=(i == 0 and m == 0),
                                            stop=(i == KC - 1 and m == 2))
                return last

            def main_step(p, slot, what, i):
                if what == "ln":
                    wait_count(pe, bank_read, BANK_USES * p + i - BANKS + 1)
                    s, half = i % 4, i // 4
                    if half == 0:
                        pe.wait_ge(xn_ready, 4 * p + s + 1)
                    n = TILES[s][2]
                    for q in range(4):
                        last = nc.tensor.transpose(pr[i % BANKS][:, 128 * q:128 * q + n],
                                                   ht[0:n, s, (4 * half + q) * 128:(4 * half + q + 1) * 128], ident[0:n, 0:n])
                    last.then_inc(proj_done, 1)
                    return
                use = KV_USE if what == "kv" else USE[what[1]]
                if i == 0:
                    if slot == V_SLOT:
                        wait_apart(pe, bank_read, BANK_USES * p + VT_USE - BANKS + 1, const_ready)
                        for c in range(2):
                            nc.tensor.transpose(pr[VT_USE % BANKS][:, 64 * c:64 * c + HD], vT[96:128, c * S:c * S + CH], ident[96:128, 96:128])
                            last = nc.tensor.transpose(pr[VT_USE % BANKS][0:TXT, 64 * c + HD:64 * c + 2 * HD],
                                                       vT[96:128, c * S + CH:(c + 1) * S], ident[96:128, 96:128])
                        last.then_inc(proj_done, 1)
                    pe.wait_ge(bank_read, BANK_USES * p + use - BANKS + 1)
                if i == KC // 2 and what == ("q", 0):
                    pe.wait_ge(bank_read, BANK_USES * p + 8)
                if what == "kv":
                    last = three(pr[use % BANKS][:, 0:PT], wkv, slice(0, 128), i)
                else:
                    last = three(pr[use % BANKS][:, 0:PT], wq, slice(128 * what[1], 128 * what[1] + 128), i)
                if i == KC - 1:
                    last.then_inc(proj_done, 1)

            def body(p, first, last):
                for slot, main, sj, tj, aj in slots(p, first, last):
                    for i in range(GH):
                        if sj is not None:
                            scores(*sj, i)
                        turning = tj if i >= 4 else aj
                        if turning is not None:
                            turn(*turning, (i + 4) % GH)
                        if main is not None:
                            main_step(p, slot, main, i)
                        if i == 6 and aj is not None:
                            values(*aj)
            pe.wait_ge(const_ready, 1)
            visit(body)(pe)

        @block.scalar
        def _(act):
            def exp_head(p, j, i):
                act.wait_ge(scores_biased, 64 * p + 8 * j + i + 1)
                for t, (rows, cols) in enumerate(((slice(0, CH), slice(0, CH)), (slice(0, TXT), slice(CH, CH + S)))):
                    at = (rows, j % 2, i // 4, t, slice(i % 4, i % 4 + 1))
                    last = nc.scalar.activation(P[rows, j % 2, i, cols], P[rows, j % 2, i, cols], ACT.Exp, scale=-1.0,
                                                bias=nmax[at], accum_out=den[at])
                last.then_inc(exp_done, 1)

            def hi_part(p, slot, i):
                what = MAIN[slot]
                if what == "ln":
                    s, half = i % 4, i // 4
                    c, t0, n = TILES[s]
                    act.wait_ge(proj_done, BANK_USES * p + i + 1)
                    src = pr[i % BANKS][:, :].rearrange("p (q t) -> p q t", q=4)[:, :, 0:n]
                    nc.scalar.activation(xT[0][:, 4 * half:4 * half + 4, c * S + t0:c * S + t0 + n], src, ACT.Copy).then_inc(hi_written, 1)
                elif what == "kv":
                    act.wait_ge(proj_done, BANK_USES * p + KV_USE + 1)
                    wait_count(act, scores_done, 64 * p)
                    if isinstance(p, int) and p == 0:
                        act.wait_ge(rows_ready, 2)
                    src = pr[KV_USE % BANKS]
                    for v in range(2):
                        nc.scalar.activation(Ks[0:96, v, :, 0:S], src[0:96, 0:PT].rearrange("p (b t) -> p b t", b=2), ACT.Copy)
                    nc.scalar.activation(vT[96:128, :], src[96:128, 0:PT], ACT.Copy).then_inc(hi_written, 1)
                else:
                    k = what[1]
                    act.wait_ge(proj_done, BANK_USES * p + USE[k] + 1)
                    wait_count(act, q_stacked[k % 2], 16 * STACKS * (4 * p + k // 2))
                    nc.scalar.activation(q_hi[:, k % 2, :], pr[USE[k] % BANKS][:, 0:PT], ACT.Copy, scale=-SCALE).then_inc(hi_written, 1)

            def body(p, first, last):
                for slot, main, sj, tj, aj in slots(p, first, last):
                    for i in range(GH):
                        if i == 0 and slot == 0 and not first:
                            hi_part(p - 1, SLOTS - 1, 0)
                        if i == 0 and slot >= 2 and main is not None:
                            hi_part(p, slot - 1, 0)
                        turn = GH * slot + i - LN_HI_AFTER
                        if 0 <= turn < GH and main is not None:
                            hi_part(p, 0, turn)
                        if sj is not None:
                            exp_head(*sj, i)
                        k = wo_piece(last, slot, i)
                        if k is not None:
                            act.wait_ge(wo_loaded[k], 16)
                            nc.scalar.activation(part_of(W["wq_hi"], k), ht[:, k % 4, :], ACT.Copy).then_inc(wo_hi, 1)
                        if i == 6 and aj is not None:
                            q, j = aj
                            act.wait_ge(av_done, 8 * q + j + 1)
                            wait_count(act, att_stored[j % 2], 16 * (4 * q + j // 2))
                            nc.scalar.activation(att[:, j % 2].rearrange("p c t -> p (c t)"), av[:, 0:2 * S], ACT.Copy).then_inc(att_copied, 1)
            act.wait_ge(const_ready, 1)
            visit(body)(act)

        @block.gpsimd
        def _(pool):
            def body(p, first, last):
                for slot, main, sj, tj, aj in slots(p, first, last):
                    for unit, half in ((tj, 1), (sj, 0)):
                        if unit is None:
                            continue
                        q, j = unit
                        pool.wait_ge(recip_done, 16 * q + 2 * j + half + 1)
                        for t, (n, cols) in enumerate(((CH, slice(0, CH)), (TXT, slice(CH, CH + S)))):
                            w = P[0:n, j % 2, 4 * half:4 * half + 4, cols]
                            r = rden[0:n, j % 2, half, t, :].unsqueeze(2).to_broadcast((n, 4, cols.stop - cols.start))
                            lastp = nc.gpsimd.tensor_tensor(w, w, r, ALU.mult)
                        lastp.then_inc(probs_ready, 1)
            nc.gpsimd.memset(Ks[:].bitcast(F32), 0.0).then_inc(rows_ready, 1)
            pool.wait_ge(rows_ready, 1)
            pool.wait_ge(const_loaded, 32)
            nc.gpsimd.tensor_copy(Ks[96:100], crow[96:100, 16:16 + 4 * (S + 1)].rearrange("p (v b t) -> p v b t", v=2, b=2)).then_inc(rows_ready, 1)
            nc.gpsimd.tensor_copy(Qs[96:100].rearrange("p s h t -> p (s h) t"),
                                  crow[96:100, 0:16].unsqueeze(2).to_broadcast((4, 16, PT))).then_inc(rows_ready, 1)
            visit(body)(pool)

        RECIP_AT = (5, 2)
        LO_AT, KV_LO_AT = 1, 3
        STATS_AT, RSTD_RATE = 12, 1
        APPLY_AT, APPLY_EVERY = 36, 1
        CHAINS = 8 + 4 + 1 + RSQRT_LINKS

        @block.vector
        def _(dve):
            v = nc.vector

            def bias_head(p, j, i):
                wait_apart(dve, scores_done, 64 * p + 8 * j + i + 1, const_loaded, 32)
                for t, (n, cols, m) in enumerate(((CH, slice(0, CH), slice(CH, 2 * CH)), (TXT, slice(CH, CH + S), slice(0, S)))):
                    lastv = v.tensor_tensor_reduce(P[0:n, j % 2, i, cols], sc[i % 2][0:n, cols], mask[0:n, m], 1.0, 3.0e38,
                                                   ALU.add, ALU.min, nmax[0:n, j % 2, i // 4, t, i % 4:i % 4 + 1])
                lastv.then_inc(scores_biased, 1)

            def recip(p, j, half):
                dve.wait_ge(exp_done, 64 * p + 8 * j + 4 * half + 4)
                v.reciprocal(rden[:, j % 2, half], den[:, j % 2, half]).then_inc(recip_done, 1)

            def copy_turned(p, j, i):
                dve.wait_ge(transposed, 64 * p + 8 * j + i + 1)
                if i == 0:
                    wait_count(dve, av_done, 8 * p + j - 1)
                v.tensor_copy(PTR[:, j % 2, i, :], pt[i % 2][:, 0:S + TXT]).then_inc(pT_copied, 1)

            def lo_part(p, slot, i):
                what = MAIN[slot]
                if what == "ln":
                    s, half = i % 4, i // 4
                    c, t0, n = TILES[s]
                    dve.wait_ge(hi_written, (BANK_USES - 1) * p + i + 1)
                    at = (slice(None), slice(4 * half, 4 * half + 4), slice(c * S + t0, c * S + t0 + n))
                    src = pr[i % BANKS][:, :].rearrange("p (q t) -> p q t", q=4)[:, :, 0:n]
                    v.tensor_tensor(xT[1][at], src, xT[0][at].bitcast(F32), ALU.subtract).then_inc(bank_read, 1)
                elif what == "kv":
                    dve.wait_ge(hi_written, (BANK_USES - 1) * p + hi_count(KV_USE))
                    src = pr[KV_USE % BANKS][HD:2 * HD, 0:PT].rearrange("p (b t) -> p b t", b=2)
                    for var in range(2):
                        at = Ks[HD:2 * HD, var, :, 0:S]
                        lastv = v.tensor_tensor(at, src, at.bitcast(F32), ALU.subtract)
                    lastv.then_inc(bank_read, 1)
                else:
                    k = what[1]
                    dve.wait_ge(hi_written, (BANK_USES - 1) * p + hi_count(USE[k]))
                    v.scalar_tensor_tensor(out=q_lo[:, k % 2, :], in0=pr[USE[k] % BANKS][:, 0:PT], scalar=-SCALE,
                                           in1=q_hi[:, k % 2, :].bitcast(F32), op0=ALU.mult, op1=ALU.subtract).then_inc(bank_read, 1)

            def copy_v(p):
                dve.wait_ge(proj_done, BANK_USES * p + VT_USE + 1)
                wait_count(dve, av_done, 8 * p)
                src = pr[VT_USE % BANKS][:, 0:128].rearrange("p (b t d) -> p b t d", b=2, t=2)
                v.tensor_copy(V0[:], src[:, :, 0, :])
                v.tensor_copy(V1[0:TXT], src[0:TXT, :, 1, :]).then_inc(bank_read, 1)

            def ln_stats(p, step, link):
                s, part = step // 3, step % 3
                n = TILES[s][2]
                if part == 0:
                    dve.wait_ge(h_loaded[s], 16 * (p + 1))
                if part < 2:
                    link.issued(v.bn_stats(stats[0:n, s, part, :], ht[0:n, s, 512 * part:512 * part + 512]))
                else:
                    link.wait(apart=True)
                    link.issued(v.bn_aggr(mv[0:n, s, :], stats[0:n, s].rearrange("p a b -> p (a b)")))

            def ln_rstd(step, link):
                link.wait()
                if step == 0:
                    link.issued(v.tensor_scalar(veps[:], mv[:, :, 1], EPS, None, ALU.add))
                else:
                    link.issued(rsqrt_step(nc, step - 1, rstd[:], veps[:], rtmp[:]))

            def ln_apply(p, s, link):
                n = TILES[s][2]
                if s == 0:
                    link.wait()
                v.tensor_scalar(ht[0:n, s, :], ht[0:n, s, :], mv[0:n, s, 0:1], rstd[0:n, s:s + 1],
                                ALU.subtract, ALU.mult).then_inc(xn_ready, 1)

            def body(p, first, last):
                link = Chain(dve, chain, CHAINS * (p + 1) if last is False else 0, const_ready)
                for slot, main, sj, tj, aj in slots(p, first, last):
                    for i in range(GH):
                        if sj is not None:
                            bias_head(*sj, i)
                        if i == LO_AT and slot == 0 and not first:
                            lo_part(p - 1, SLOTS - 1, 0)
                        if i == (KV_LO_AT if MAIN[slot - 1] == "kv" else LO_AT) and slot >= 2 and main is not None:
                            lo_part(p, slot - 1, 0)
                        if i == 2 and slot == V_SLOT and main is not None:
                            copy_v(p)
                        if 0 <= GH * slot + i - LN_LO_AFTER < GH and main is not None:
                            lo_part(p, 0, GH * slot + i - LN_LO_AFTER)
                        k = wo_piece(last, slot, i, LO_AFTER)
                        if k is not None:
                            dve.wait_ge(wo_hi, k + 1)
                            v.tensor_tensor(part_of(W["wq_lo"], k), ht[:, k % 4, :], part_of(W["wq_hi"], k).bitcast(F32),
                                            ALU.subtract).then_inc(wo_lo, 1)
                        if i == RECIP_AT[1] and tj is not None:
                            recip(*tj, 1)
                        if i == RECIP_AT[0] and sj is not None:
                            recip(*sj, 0)
                        if last is False:
                            turn = GH * slot + i
                            if STATS_AT <= turn < STATS_AT + 12:
                                ln_stats(p + 1, turn - STATS_AT, link)
                            for step in range(RSQRT_LINKS + 1):
                                if turn == STATS_AT + 12 + step // RSTD_RATE:
                                    ln_rstd(step, link)
                            for s in range(4):
                                if turn == APPLY_AT + APPLY_EVERY * s:
                                    ln_apply(p + 1, s, link)
                        turning = tj if i >= 4 else aj
                        if turning is not None:
                            copy_turned(*turning, (i + 4) % GH)

            v.memset(den[:], 1.0)
            v.memset(mv[:], 1.0)
            for bank in pt:
                v.memset(bank[:, 0:S + TXT], 0.0)
            dve.wait_ge(const_loaded, 32)
            link = Chain(dve, chain, met=const_ready)
            v.memset(PTR[:, 0, 0, 0:1], 0.0).then_inc(const_ready, 1)
            for step in range(12):
                ln_stats(0, step, link)
            for step in range(RSQRT_LINKS + 1):
                ln_rstd(step, link)
            for s in range(4):
                ln_apply(0, s, link)
            visit(body)(dve)


def mlp_block(nc, ctx, io, W):
    def sb(name, shape, dt=F32):
        return ctx.enter_context(nc.sbuf_tensor(name, shape, dt))

    def pb(name):
        return ctx.enter_context(nc.psum_tensor(name, [128, 512], F32))

    def sem(name):
        return ctx.enter_context(nc.semaphore(name))

    ident = W["ident"]
    ARW = 144
    PIECES = KC + 2
    SIZES = [DM] * KC + [KC * ARW // 2] * 2
    OFFS = [sum(SIZES[:k]) for k in range(PIECES + 1)]
    w_hi, w_lo = sb("w2_hi", [128, OFFS[-1]], F32R), sb("w2_lo", [128, OFFS[-1]], F32R)
    RING = 3
    RESIDUAL_AFTER = 4
    stage = sb("w2_stage", [128, RING, DM])

    def part(hi_lo, off, n, w):
        return [t[:, off:off + n * w].rearrange("p (k m) -> p k m", k=n) for t in hi_lo]

    early = (W["wq_hi"], W["wq_lo"])
    wo, wB = part(early, 0, KC, DM), part(early, KC * DM, 1, DM)
    wb, war = part((w_hi, w_lo), 0, KC, DM), part((w_hi, w_lo), OFFS[KC], KC, ARW)
    base_b, rout_b = sb("base_b", [128, DM]), sb("rout_b", [128, ROUTES])
    emap, emapf, sel_map = sb("emap", [128, ROUTES], I32), sb("emapf", [128, ROUTES]), sb("sel_map", [128, EXPERTS, ROUTES])
    at, a_loaded = W["at"], W["a_loaded"]
    aT = [sb("aT_hi", [128, 2, KC, 128], F32R), sb("aT_lo", [128, 2, KC, 128], F32R)]
    h2 = sb("h2", [128, 2, DM])
    xn = sb("xn", [128, DM])
    xT = [sb("x2T_hi", [128, KC, 128], F32R), sb("x2T_lo", [128, KC, 128], F32R)]
    stats, mv, rstd, rtmp, veps = sb("stats2", [128, 2, 6]), sb("mv2", [128, 2]), sb("rstd2", [128, 1]), sb("rtmp2", [128, 1]), sb("veps2", [128, 1])
    lg, m8, nm = sb("lg", [128, ROUTES]), sb("m8", [128, 8]), sb("nm", [128, 1])
    ex, e8, er, dn, rd = sb("ex", [128, ROUTES]), sb("e8", [128, 8]), sb("er", [128, ROUTES]), sb("dn", [128, 1]), sb("rd", [128, 1])
    w8 = sb("w8", [128, EXPERTS])
    z, wsel = xn[:, 0:ER], xn[:, ER:ER + EXPERTS * ROUTES].rearrange("p (e r) -> p e r", e=EXPERTS)
    zT = [sb("zT_hi", [128, 128], F32R), sb("zT_lo", [128, 128], F32R)]

    wo_ps, x_ps, base_ps = [pb("wo0"), pb("wo1")], [pb("x0"), pb("x1")], [pb("b0"), pb("b1")]
    ar_ps, z_ps = pb("ar"), pb("zp")

    const_loaded, w_loaded = sem("mlp_const_loaded"), [sem(f"w2_loaded{i}") for i in range(RING)]
    hi_split, lo_split = sem("w2_hi_done"), sem("w2_lo_done")
    r_loaded = [sem("r_loaded0"), sem("r_loaded1")]
    a_hi, a_lo, wo_done, wo_read = sem("a_hi"), sem("a_lo"), sem("wo_done"), sem("wo_read")
    x_ready, biased = sem("x2_ready"), sem("h2_biased")
    xT_done, xT_hi, xT_lo = sem("x2T_done"), sem("x2T_hi_done"), sem("x2T_lo_done")
    ar_done, logits_ready, exp_ready, z_ready = sem("ar_done"), sem("logits_ready"), sem("router_exp"), sem("z_ready")
    zT_done, zT_hi, zT_lo = sem("zT_done"), sem("zT_hi_done"), sem("zT_lo_done")
    base_done, out_ready, setup, chain = sem("base_done"), sem("out_ready"), sem("mlp_setup"), sem("mlp_chain")
    out_stored = [sem("out_stored0"), sem("out_stored1")]
    LAST = FULL

    def visit(eng, body):
        size = lambda t: 128 if t < FULL else (REST if t == FULL else 0)
        pairs = (FULL - 2) // 2
        for t in range(2):
            body(t, t % 2, t // 2, 128, 128, 128)
        with eng.Fori(1, pairs) as i:
            for par in range(2):
                body(i * 2 + par, par, i, 128, 128, 128)
        for t in range(2 * pairs, FULL + 1):
            body(t, t % 2, t // 2, size(t), size(t + 1), size(t + 2))

    with nc.Block() as block:
        @block.sync
        def _(sp):
            sp.dma_start(base_b[:], io["base_b"].partition_broadcast(128)).then_inc(const_loaded, 16)
            sp.dma_start(rout_b[:], io["router_b"].partition_broadcast(128)).then_inc(const_loaded, 16)
            sp.dma_start(emap[:], io["expert_map"].partition_broadcast(128)).then_inc(const_loaded, 16)

            def load_att(t, par, n):
                wait_count(sp, a_lo, t - 1)
                sp.dma_start(at[:, par, :, 0:n], io["att_dram"].rearrange("(k p) t -> p k t", p=128)[:, :, bass.ds(t * 128, n)]).then_inc(a_loaded[par], 16)

            def load_res(t, par, n):
                sp.dma_start(h2[0:n, par, :], io["h_dram"][bass.ds(t * 128, n), :]).then_inc(r_loaded[par], 16)

            srcs = [io["base_WT"][k * 128:(k + 1) * 128, :] for k in range(KC)]
            srcs += [io["ARW"][:, k * KC // 2:(k + 1) * KC // 2, :] for k in range(2)]
            load_res(0, 0, 128)
            for k in range(PIECES):
                if k >= RING:
                    sp.wait_ge(lo_split, k - RING + 1)
                dst = stage[:, k % RING, 0:SIZES[k]]
                if len(srcs[k].shape) == 3:
                    dst = dst.rearrange("p (k m) -> p k m", m=ARW)
                sp.dma_start(dst, srcs[k]).then_inc(w_loaded[k % RING], 16)
                if k == 3:
                    load_res(1, 1, 128)

            def body(t, par, half_t, n, n1, n2):
                if n2:
                    load_att(t + 2, par, n2)
                sp.wait_ge(out_ready, t + 1)
                sp.dma_start(io["out"][bass.ds(t * 128, n), :], h2[0:n, par, :]).then_inc(out_stored[par], 16)
                if n2:
                    sp.wait_ge(out_stored[par], 16 * half_t + 16)
                    load_res(t + 2, par, n2)
            visit(sp, body)
            sp.wait_ge(out_stored[0], 16 * ((FULL + 2) // 2))
            sp.wait_ge(out_stored[1], 16 * ((FULL + 1) // 2))

        @block.tensor
        def _(pe):
            def three(bank, n, lhs, w, cols, K, start=True, stop=True, between=None):
                for k in range(K):
                    if k == K // 2 and between is not None:
                        between()
                    for m, (a, b) in enumerate(((0, 0), (0, 1), (1, 0))):
                        last = nc.tensor.matmul(bank[0:n, 0:cols.stop - cols.start], lhs[a][:, k, 0:n], w[b][:, k, cols],
                                                start=(start and k == 0 and m == 0), stop=(stop and k == K - 1 and m == 2))
                return last

            def turn_z(t, n):
                pe.wait_ge(z_ready, t + 1)
                nc.tensor.transpose(z_ps[:, 0:n], z[0:n, :], ident[0:n, 0:n]).then_inc(zT_done, 1)

            def attn_out(t, par, n, between=None):
                a = [w[:, par] for w in aT]
                pe.wait_ge(a_lo, t + 1)
                wait_count(pe, wo_read, t)
                three(wo_ps[0], n, a, wo, slice(0, 512), KC)
                if between is not None:
                    between()
                three(wo_ps[1], n, a, wo, slice(512, 1024), KC).then_inc(wo_done, 1)

            def transpose_x(t, n):
                pe.wait_ge(x_ready, t + 1)
                wait_count(pe, xT_lo, 2 * t)
                for half in range(2):
                    for q in range(4):
                        last = nc.tensor.transpose(x_ps[half][:, 128 * q:128 * q + n], xn[0:n, (4 * half + q) * 128:(4 * half + q + 1) * 128], ident[0:n, 0:n])
                    last.then_inc(xT_done, 1)

            def body(t, par, half_t, n, n1, n2):
                first = isinstance(t, int) and t == 0
                pe.wait_ge(xT_lo, 2 * t + 1)
                if first:
                    pe.wait_ge(lo_split, PIECES)
                wait_count(pe, z_ready, t)
                three(ar_ps, n, xT, war, slice(0, ARW), KC, between=lambda: pe.wait_ge(xT_lo, 2 * t + 2)).then_inc(ar_done, 1)
                if n1 and not first:
                    attn_out(t + 1, 1 - par, n1, between=lambda: turn_z(t, n))
                wait_count(pe, out_ready, t)
                three(base_ps[0], n, xT, wb, slice(0, 512), KC, stop=False)
                if first or not n1:
                    turn_z(t, n)
                three(base_ps[1], n, xT, wb, slice(512, 1024), KC, stop=False)
                if n1:
                    transpose_x(t + 1, n1)
                pe.wait_ge(zT_lo, t + 1)
                zz = [q[:, 0:n].unsqueeze(1) for q in zT]
                for half in range(2):
                    last = three(base_ps[half], n, zz, wB, slice(512 * half, 512 * half + 512), 1, start=False)
                last.then_inc(base_done, 1)
            attn_out(0, 0, 128)
            attn_out(1, 1, 128)
            transpose_x(0, 128)
            visit(pe, body)

        @block.scalar
        def _(act):
            def x_hi(t, n):
                for half in range(2):
                    act.wait_ge(xT_done, 2 * t + half + 1)
                    src = x_ps[half][:, :].rearrange("p (q t) -> p q t", q=4)[:, :, 0:n]
                    nc.scalar.activation(xT[0][:, 4 * half:4 * half + 4, 0:n], src, ACT.Copy).then_inc(xT_hi, 1)

            def a_split(half_t, t, par, n):
                act.wait_ge(a_loaded[par], 16 * half_t + 16)
                wait_count(act, wo_done, t - 1)
                nc.scalar.activation(aT[0][:, par, :, 0:n], at[:, par, :, 0:n], ACT.Copy).then_inc(a_hi, 1)

            def body(t, par, half_t, n, n1, n2):
                act.wait_ge(logits_ready, t + 1)
                nc.scalar.activation(ex[0:n], lg[0:n], ACT.Exp, bias=nm[0:n, 0:1], accum_out=dn[0:n, 0:1]).then_inc(exp_ready, 1)
                act.wait_ge(zT_done, t + 1)
                nc.scalar.activation(zT[0][:, 0:n], z_ps[:, 0:n], ACT.Copy).then_inc(zT_hi, 1)
                if n2:
                    a_split(half_t + 1, t + 2, par, n2)
                if n1:
                    x_hi(t + 1, n1)

            a_split(0, 0, 0, 128)
            a_split(0, 1, 1, 128)
            for k in range(PIECES):
                act.wait_ge(w_loaded[k % RING], 16 * (k // RING + 1))
                o = slice(OFFS[k], OFFS[k + 1])
                nc.scalar.activation(w_hi[:, o], stage[:, k % RING, 0:SIZES[k]], ACT.Copy).then_inc(hi_split, 1)
            x_hi(0, 128)
            visit(act, body)

        @block.gpsimd
        def _(pool):
            def add_bias(t, par, n):
                pool.wait_ge(x_ready, t + 1)
                nc.gpsimd.tensor_tensor(h2[0:n, par, :], h2[0:n, par, :], base_b[0:n, :], ALU.add).then_inc(biased, 1)

            def body(t, par, half_t, n, n1, n2):
                if n1:
                    add_bias(t + 1, 1 - par, n1)
            pool.wait_ge(const_loaded, 48)
            add_bias(0, 0, 128)
            visit(pool, body)

        LINKS = (5 + RSQRT_LINKS) + 9

        @block.vector
        def _(dve):
            v = nc.vector

            def residual_ln(t, par, half_t, n, link):
                dve.wait_ge(wo_done, t + 1)
                dve.wait_ge(r_loaded[par], 16 * half_t + 16)
                link.done(v.tensor_tensor(h2[0:n, par, 0:512], wo_ps[0][0:n, :], h2[0:n, par, 0:512], ALU.add))
                v.tensor_tensor(h2[0:n, par, 512:1024], wo_ps[1][0:n, :], h2[0:n, par, 512:1024], ALU.add).then_inc(wo_read, 1)
                dve.wait_ge(wo_read, t + 1)
                link.done(v.bn_stats(stats[0:n, 0, :], h2[0:n, par, 0:512]))
                link.done(v.bn_stats(stats[0:n, 1, :], h2[0:n, par, 512:1024]), apart=True)
                link.done(v.bn_aggr(mv[0:n, :], stats[0:n].rearrange("p a b -> p (a b)")))
                link.done(v.tensor_scalar(veps[0:n], mv[0:n, 1:2], EPS, None, ALU.add))
                rsqrt_newton(nc, link.done, rstd[0:n], veps[0:n], rtmp[0:n])
                wait_count(dve, xT_done, 2 * t)
                v.tensor_scalar(xn[0:n, :], h2[0:n, par, :], mv[0:n, 0:1], rstd[0:n, 0:1], ALU.subtract, ALU.mult).then_inc(x_ready, 1)

            def att_lo(t, par, n):
                dve.wait_ge(a_hi, t + 1)
                v.tensor_tensor(aT[1][:, par, :, 0:n], at[:, par, :, 0:n], aT[0][:, par, :, 0:n].bitcast(F32), ALU.subtract).then_inc(a_lo, 1)

            def x_lo(t, n):
                for half in range(2):
                    dve.wait_ge(xT_hi, 2 * t + half + 1)
                    src = x_ps[half][:, :].rearrange("p (q t) -> p q t", q=4)[:, :, 0:n]
                    c = slice(4 * half, 4 * half + 4)
                    v.tensor_tensor(xT[1][:, c, 0:n], src, xT[0][:, c, 0:n].bitcast(F32), ALU.subtract).then_inc(xT_lo, 1)

            def router(t, n, link):
                dve.wait_ge(ar_done, t + 1)
                link.done(v.tensor_tensor(lg[0:n], ar_ps[0:n, ER:ER + ROUTES], rout_b[0:n], ALU.add), apart=True)
                link.done(v.max(m8[0:n], lg[0:n]))
                v.tensor_scalar(nm[0:n], m8[0:n, 0:1], -1.0, None, ALU.mult).then_inc(logits_ready, 1)
                wait_apart(dve, exp_ready, t + 1, setup)
                link.done(v.max(e8[0:n], ex[0:n]), apart=True)
                link.done(v.match_replace(er[0:n], e8[0:n], ex[0:n], 0.0))
                link.done(v.tensor_tensor(er[0:n], ex[0:n], er[0:n], ALU.subtract))
                link.done(v.tensor_tensor(wsel[0:n], er[0:n].unsqueeze(1).to_broadcast((n, EXPERTS, ROUTES)), sel_map[0:n], ALU.mult))
                link.done(v.tensor_reduce(w8[0:n], wsel[0:n], AX.X, ALU.add))
                link.done(v.reciprocal(rd[0:n], dn[0:n]))
                link.done(v.tensor_scalar(rd[0:n], rd[0:n], 2.0, None, ALU.mult))
                wait_count(dve, zT_done, t)
                v.scalar_tensor_tensor(out=z[0:n].rearrange("p (e r) -> p e r", e=EXPERTS),
                                       in0=ar_ps[0:n, 0:ER].rearrange("p (e r) -> p e r", e=EXPERTS), scalar=rd[0:n, 0:1],
                                       in1=w8[0:n].unsqueeze(2).to_broadcast((n, EXPERTS, RANK)), op0=ALU.mult, op1=ALU.mult).then_inc(z_ready, 1)

            def body(t, par, half_t, n, n1, n2):
                link = Chain(dve, chain, LINKS * t + (5 + RSQRT_LINKS), setup)
                router(t, n, link)
                dve.wait_ge(zT_hi, t + 1)
                v.tensor_tensor(zT[1][:, 0:n], z_ps[:, 0:n], zT[0][:, 0:n].bitcast(F32), ALU.subtract).then_inc(zT_lo, 1)
                if n1:
                    residual_ln(t + 1, 1 - par, half_t + par, n1, link)
                if n2:
                    att_lo(t + 2, par, n2)
                if n1:
                    x_lo(t + 1, n1)
                dve.wait_ge(base_done, t + 1)
                dve.wait_ge(biased, t + 1)
                for half in range(2):
                    c = slice(512 * half, 512 * half + 512)
                    last = v.tensor_tensor(h2[0:n, par, c], base_ps[half][0:n, :], h2[0:n, par, c], ALU.add)
                last.then_inc(out_ready, 1)

            first = Chain(dve, setup)
            att_lo(0, 0, 128)
            att_lo(1, 1, 128)
            dve.wait_ge(const_loaded, 48)
            first.done(v.tensor_copy(emapf[:], emap[:]))
            for e in range(EXPERTS):
                last = v.tensor_scalar(sel_map[:, e, :], emapf[:], float(e), None, ALU.is_equal)
            first.done(last)
            for k in range(PIECES):
                dve.wait_ge(hi_split, k + 1)
                o = slice(OFFS[k], OFFS[k + 1])
                v.tensor_tensor(w_lo[:, o], stage[:, k % RING, 0:SIZES[k]], w_hi[:, o].bitcast(F32), ALU.subtract).then_inc(lo_split, 1)
                if k == RESIDUAL_AFTER:
                    residual_ln(0, 0, 0, 128, Chain(dve, chain))
            x_lo(0, 128)
            visit(dve, body)


def build(nc, io):
    with ExitStack() as whole:
        W = {"ident": whole.enter_context(nc.sbuf_tensor("ident", [128, 128], F32))}
        for n in ("wq_hi", "wq_lo"):
            W[n] = whole.enter_context(nc.sbuf_tensor(n, [128, (KC + 1) * DM], F32R))
        with ExitStack() as ctx:
            mixer_block(nc, ctx, io, W)
        W["at"] = whole.enter_context(nc.sbuf_tensor("at", [128, 2, KC, 128], F32))
        W["a_loaded"] = [whole.enter_context(nc.semaphore(f"a_loaded{i}")) for i in range(2)]
        with ExitStack() as ctx:
            attention_block(nc, ctx, io, W)
        with ExitStack() as ctx:
            mlp_block(nc, ctx, io, W)


def constants():
    f = np.float32
    base = 2.0 ** (-2.0 ** (-(math.log2(HEADS) - 3)))
    slopes = (base ** np.arange(1, HEADS + 1, dtype=np.float64)).astype(f)
    hi = (((slopes.view(np.uint32) + np.uint32(0x800)) & np.uint32(0xFFFFF000))).view(f)
    lo = slopes - hi
    rows = np.zeros((4, 16 + 4 * (S + 1)), f)
    for slot in range(2):
        for late in range(2):
            g = slot + 2 * late
            rows[2 * late, slot * GH:(slot + 1) * GH] = hi[g * GH:(g + 1) * GH]
            rows[2 * late + 1, slot * GH:(slot + 1) * GH] = lo[g * GH:(g + 1) * GH]
    pos = np.zeros((2, 2, S + 1), f)
    pos[:, :, :S] = -np.arange(S, dtype=f)
    zero = np.zeros_like(pos[0])
    for late in range(2):
        both = np.stack([pos[0] if late == 0 else zero, pos[0] if late == 1 else zero])
        rows[2 * late:2 * late + 2, 16:] = both.reshape(-1)
    k, p = np.arange(256)[None, :] - 128, np.arange(128)[:, None]
    phase = np.zeros((128, 6), f)
    for i, (top, low) in enumerate(((0.25, 0), (0.25, 0.5), (0, 0.25))):
        phase[0:64, 2 * i], phase[64:128, 2 * i] = top, low
        phase[:, 2 * i + 1] = phase[:, 2 * i] * TWO_PI
    return {
        "bvals": np.broadcast_to(np.arange(128, dtype=f), (128, 128)).copy(),
        "avals": np.broadcast_to(128 * np.arange(AH, dtype=f), (128, AH)).copy(),
        "phase": phase,
        "ident": np.eye(128, dtype=f),
        "mask": np.where(k > p, f(1e30), f(0)).astype(f),
        "rows": rows,
    }


def kernel(**inputs):
    import concourse.bacc as bacc
    from concourse.bass_utils import run_bass_kernel_spmd

    g = {k: np.asarray(v) for k, v in inputs.items()}
    x, wqkv = g["x"], g["L0_attn_Wqkv"]
    arw = np.zeros((DM, 144), np.float32)
    arw[:, 0:ER] = g["L0_ffn_A"].reshape(ER, DM).T
    arw[:, ER:ER + ROUTES] = g["L0_ffn_router_W"].T
    laid = {
        "x_re": x[..., 0].transpose(2, 1, 0),
        "x_im": x[..., 1].transpose(2, 1, 0),
        "txt": g["txt"],
        "par": np.concatenate([np.stack([np.broadcast_to(g["L0_tok_log_dt"], (64, CH)), g["L0_tok_inv_A_real"].T,
                                         g["L0_tok_B"][..., 0].T, g["L0_tok_B"][..., 1].T, g["L0_tok_A_imag"].T], 1)] * 2, 0),
        "Wqkv": np.concatenate([wqkv[:, 0:DM].reshape(DM, KC, 4, HD).transpose(0, 1, 3, 2).reshape(DM, DM), wqkv[:, DM:]], 1),
        "Wo": g["L0_attn_Wo"],
        "base_WT": g["L0_ffn_base_W"].T,
        "base_b": g["L0_ffn_base_b"],
        "router_b": g["L0_ffn_router_b"],
        "ARW": arw.reshape(KC, 128, 144).transpose(1, 0, 2),
        "BT": g["L0_ffn_B"].transpose(0, 2, 1).reshape(ER, DM),
        "expert_map": g["L0_ffn_expert_map"],
        **constants(),
    }
    nc = bacc.Bacc("TRN2", target_bir_lowering=False, num_devices=1)
    arrays, io = {}, {}
    for name, a in laid.items():
        a = np.ascontiguousarray(a)
        arrays[f"in_{name}"] = a
        io[name] = nc.dram_tensor(f"in_{name}", a.shape, mybir.dt.from_np(a.dtype), kind="ExternalInput").ap()
    io["h_dram"] = nc.dram_tensor("h_dram", (TOK, DM), F32, kind="Internal").ap()
    io["att_dram"] = nc.dram_tensor("att_dram", (DM, TOK), F32, kind="Internal").ap()
    io["out"] = nc.dram_tensor("out_0", (TOK, DM), F32, kind="ExternalOutput").ap()
    build(nc, io)
    r = run_bass_kernel_spmd(nc, [arrays], core_ids=[0])
    return r.results[0]["out_0"].reshape(SEQS, S, DM)
```
